# Optimizing a Trainium2 kernel written in Bass

```python
import numpy as np
import jax
import jax.numpy as jnp

def _softmax(x, axis=-1):
    return jax.nn.softmax(x, axis=axis)

def _gelu(x):
    return jax.nn.gelu(x, approximate=True)

def _silu(x):
    return jax.nn.silu(x)

def _sigmoid(x):
    return jax.nn.sigmoid(x)

def _layernorm(x, axis=-1, eps=1e-05):
    m = jnp.mean(x, axis=axis, keepdims=True)
    v = jnp.var(x, axis=axis, keepdims=True)
    return (x - m) / jnp.sqrt(v + eps)

def _scatter_add(tgt, idx, src, axis=0):
    return tgt.at[idx].add(src)

def _segment_sum(src, seg, n):
    return jax.ops.segment_sum(src, seg, n)
kernel_name = 'mk_seq_preln_d4_jaxref_r8_89563b'

def setup_inputs(seed: int=0):
    np.random.seed(seed)
    _w = jnp.asarray

    def _L0_attn_setup():
        import math
        import jax, jax.numpy as jnp
        import numpy as np
        NUM_HEADS = 16
        NUM_BUCKETS = 32

        def _relative_position_bucket(relative_position):
            num_buckets = NUM_BUCKETS
            n = jnp.maximum(-relative_position, 0)
            max_exact = num_buckets // 2
            is_small = n < max_exact
            n_safe = jnp.maximum(n, 1).astype(jnp.float32)
            val_if_large = max_exact + (jnp.log(n_safe / max_exact) / math.log(num_buckets / max_exact) * (num_buckets - max_exact)).astype(jnp.int32)
            val_if_large = jnp.minimum(val_if_large, num_buckets - 1)
            return jnp.where(is_small, n, val_if_large)
        key = jax.random.key(seed)
        ks = jax.random.split(key, 8)
        B, S, D = (2, 256, 128)
        s = 1.0 / math.sqrt(D)
        return {'hidden_states': jax.random.normal(ks[0], (B, S, D), jnp.float32), 'Wq': jax.random.normal(ks[1], (D, D), jnp.float32) * s, 'bq': jnp.zeros((D,), jnp.float32), 'Wk': jax.random.normal(ks[2], (D, D), jnp.float32) * s, 'bk': jnp.zeros((D,), jnp.float32), 'Wv': jax.random.normal(ks[3], (D, D), jnp.float32) * s, 'bv': jnp.zeros((D,), jnp.float32), 'rel_bias': jax.random.normal(ks[4], (NUM_BUCKETS, NUM_HEADS), jnp.float32) * 0.02}
    _L0_attn_in = _L0_attn_setup()

    def _L0_ffn_setup():
        import jax, jax.numpy as jnp
        import numpy as np
        EPS = 1e-08

        def _ternary_linear(x, w):
            alpha = jnp.mean(jnp.abs(w))
            w_t = jnp.sign(w) * (jnp.abs(w) > 0.5 * alpha).astype(w.dtype)
            w_q = w + jax.lax.stop_gradient(w_t - w)
            d = x.shape[-1]
            rms = jnp.sqrt(jnp.sum(x * x, axis=-1, keepdims=True)) / jnp.sqrt(jnp.asarray(d, x.dtype))
            x_norm = x / (rms + EPS)
            return jnp.einsum('bsd,fd->bsf', x_norm, w_q)
        key = jax.random.key(seed)
        k1, k2, k3 = jax.random.split(key, 3)
        d_model, d_ff = (128, 512)
        B, S = (4, 512)
        x = jax.random.normal(k1, (B, S, d_model), dtype=jnp.float32)
        w_up = jax.random.normal(k2, (d_ff, d_model), dtype=jnp.float32) * 0.02
        w_down = jax.random.normal(k3, (d_model, d_ff), dtype=jnp.float32) * 0.02
        return {'x': x, 'w_up': w_up, 'w_down': w_down}
    _L0_ffn_in = _L0_ffn_setup()

    def _L1_attn_setup():
        import math
        import jax, jax.numpy as jnp
        import numpy as np
        B, T, C = (4, 256, 128)
        H = 16
        D = C // H
        key = jax.random.key(seed)
        ks = jax.random.split(key, 5)
        scale = 0.02
        return {'x': jax.random.normal(ks[0], (B, T, C), dtype=jnp.float32), 'w_attn': jax.random.normal(ks[1], (C, 3 * C), dtype=jnp.float32) * scale, 'b_attn': jax.random.normal(ks[2], (3 * C,), dtype=jnp.float32) * scale, 'w_proj': jax.random.normal(ks[3], (C, C), dtype=jnp.float32) * scale, 'b_proj': jax.random.normal(ks[4], (C,), dtype=jnp.float32) * scale}
    _L1_attn_in = _L1_attn_setup()

    def _L1_ffn_setup():
        import jax, jax.numpy as jnp
        import numpy as np
        from math import ceil
        CAPACITY_FACTOR = 2.0
        MIN_CAPACITY = 4
        key = jax.random.key(seed)
        ks = jax.random.split(key, 4)
        B, S, D, Di, E = (4, 256, 128, 512, 8)
        x = jax.random.normal(ks[0], (B, S, D), dtype=jnp.float32)
        Wr = jax.random.normal(ks[1], (D, E), dtype=jnp.float32) * D ** (-0.5)
        W1 = jax.random.normal(ks[2], (E, D, Di), dtype=jnp.float32) * D ** (-0.5)
        b1 = jnp.zeros((E, Di), dtype=jnp.float32)
        W2 = jax.random.normal(ks[3], (E, Di, D), dtype=jnp.float32) * Di ** (-0.5)
        b2 = jnp.zeros((E, D), dtype=jnp.float32)
        return {'x': x, 'Wr': Wr, 'W1': W1, 'b1': b1, 'W2': W2, 'b2': b2}
    _L1_ffn_in = _L1_ffn_setup()

    def _L2_attn_setup():
        import jax, jax.numpy as jnp
        import numpy as np
        DT_MIN, DT_MAX = (0.001, 0.1)
        DT_RANK, D_STATE, D_CONV = (64, 16, 4)
        key = jax.random.key(seed)
        ks = jax.random.split(key, 8)
        B, T, Dm = (4, 512, 128)
        Dn = 2 * Dm
        s = lambda k, shape, scale=0.02: jax.random.normal(k, shape, jnp.float32) * scale
        return {'x': jax.random.normal(ks[0], (B, T, Dm), jnp.float32), 'W_in': s(ks[1], (2 * Dn, Dm)), 'conv_w': s(ks[2], (Dn, 1, D_CONV), 0.1), 'conv_b': jnp.zeros((Dn,), jnp.float32), 'W_x': s(ks[3], (DT_RANK + 2 * D_STATE, Dn)), 'W_dt': s(ks[4], (Dn, DT_RANK)), 'b_dt': jnp.zeros((Dn,), jnp.float32), 'log_A': jax.random.uniform(ks[5], (Dn, D_STATE), jnp.float32), 'D_param': jnp.ones((Dn,), jnp.float32), 'W_out': s(ks[6], (Dm, Dn)), 'ln_w': jnp.ones((Dm,), jnp.float32), 'ln_b': jnp.zeros((Dm,), jnp.float32)}
    _L2_attn_in = _L2_attn_setup()

    def _L2_ffn_setup():
        import jax, jax.numpy as jnp
        import numpy as np
        H = 128
        E = 32
        I = 64
        TOP_K = 6
        IS = 128
        NORM_MIN = 1e-12
        B, S = (2, 128)
        key = jax.random.key(seed)
        ks = jax.random.split(key, 8)
        sc = 0.02
        return {'hidden_states': jax.random.normal(ks[0], (B, S, H), jnp.float32), 'router_weight': jax.random.normal(ks[1], (E, H), jnp.float32) * sc, 'e_score_bias': jnp.zeros((E,), jnp.float32), 'gate_up_proj': jax.random.normal(ks[2], (E, 2 * I, H), jnp.float32) * sc, 'down_proj': jax.random.normal(ks[3], (E, H, I), jnp.float32) * sc, 'shared_gate_w': jax.random.normal(ks[4], (IS, H), jnp.float32) * sc, 'shared_up_w': jax.random.normal(ks[5], (IS, H), jnp.float32) * sc, 'shared_down_w': jax.random.normal(ks[6], (H, IS), jnp.float32) * sc}
    _L2_ffn_in = _L2_ffn_setup()

    def _L3_attn_setup():
        import jax, jax.numpy as jnp
        import numpy as np
        LN_EPS = 1e-05

        def _min_gru(x, Wz, bz, Wh, bh):
            z = jax.nn.sigmoid(jnp.einsum('btd,de->bte', x, Wz) + bz)
            h_tilde = jnp.einsum('btd,de->bte', x, Wh) + bh
            a = 1.0 - z
            b = z * h_tilde

            def combine(c1, c2):
                a1, b1 = c1
                a2, b2 = c2
                return (a1 * a2, a2 * b1 + b2)
            _, h = jax.lax.associative_scan(combine, (a, b), axis=1)
            return h
        key = jax.random.key(seed)
        ks = jax.random.split(key, 4)
        B, T, D = (8, 256, 128)
        x = jax.random.normal(ks[0], (B, T, D), dtype=jnp.float32)
        Wz = jax.random.normal(ks[1], (D, D), dtype=jnp.float32) * (1.0 / np.sqrt(D))
        bz = jnp.zeros((D,), dtype=jnp.float32)
        Wh = jax.random.normal(ks[2], (D, D), dtype=jnp.float32) * (1.0 / np.sqrt(D))
        bh = jnp.zeros((D,), dtype=jnp.float32)
        swish_beta = jnp.float32(1.0)
        ln_gamma = jnp.ones((D,), dtype=jnp.float32)
        ln_beta = jnp.zeros((D,), dtype=jnp.float32)
        return {'x': x, 'Wz': Wz, 'bz': bz, 'Wh': Wh, 'bh': bh, 'swish_beta': swish_beta, 'ln_gamma': ln_gamma, 'ln_beta': ln_beta}
    _L3_attn_in = _L3_attn_setup()

    def _L3_ffn_setup():
        import jax, jax.numpy as jnp
        import numpy as np
        D_MODEL, D_FF, RANK = (128, 512, 32)
        B, S = (4, 512)
        key = jax.random.key(seed)
        ks = jax.random.split(key, 7)
        return {'x': jax.random.normal(ks[0], (B, S, D_MODEL), dtype=jnp.float32), 'U1': jax.random.normal(ks[1], (D_MODEL, RANK), dtype=jnp.float32) * 0.02, 'V1': jax.random.normal(ks[2], (RANK, D_FF), dtype=jnp.float32) * 0.02, 'b1': jnp.zeros((D_FF,), dtype=jnp.float32), 'U2': jax.random.normal(ks[3], (D_FF, RANK), dtype=jnp.float32) * 0.02, 'V2': jax.random.normal(ks[4], (RANK, D_MODEL), dtype=jnp.float32) * 0.02, 'b2': jnp.zeros((D_MODEL,), dtype=jnp.float32)}
    _L3_ffn_in = _L3_ffn_setup()
    _d = {'L0_attn_hidden_states': _L0_attn_in['hidden_states'], 'L0_attn_Wq': _L0_attn_in['Wq'], 'L0_attn_bq': _L0_attn_in['bq'], 'L0_attn_Wk': _L0_attn_in['Wk'], 'L0_attn_bk': _L0_attn_in['bk'], 'L0_attn_Wv': _L0_attn_in['Wv'], 'L0_attn_bv': _L0_attn_in['bv'], 'L0_attn_rel_bias': _L0_attn_in['rel_bias'], 'L0_ffn_w_up': _L0_ffn_in['w_up'], 'L0_ffn_w_down': _L0_ffn_in['w_down'], 'L1_attn_w_attn': _L1_attn_in['w_attn'], 'L1_attn_b_attn': _L1_attn_in['b_attn'], 'L1_attn_w_proj': _L1_attn_in['w_proj'], 'L1_attn_b_proj': _L1_attn_in['b_proj'], 'L1_ffn_Wr': _L1_ffn_in['Wr'], 'L1_ffn_W1': _L1_ffn_in['W1'], 'L1_ffn_b1': _L1_ffn_in['b1'], 'L1_ffn_W2': _L1_ffn_in['W2'], 'L1_ffn_b2': _L1_ffn_in['b2'], 'L2_attn_W_in': _L2_attn_in['W_in'], 'L2_attn_conv_w': _L2_attn_in['conv_w'], 'L2_attn_conv_b': _L2_attn_in['conv_b'], 'L2_attn_W_x': _L2_attn_in['W_x'], 'L2_attn_W_dt': _L2_attn_in['W_dt'], 'L2_attn_b_dt': _L2_attn_in['b_dt'], 'L2_attn_log_A': _L2_attn_in['log_A'], 'L2_attn_D_param': _L2_attn_in['D_param'], 'L2_attn_W_out': _L2_attn_in['W_out'], 'L2_attn_ln_w': _L2_attn_in['ln_w'], 'L2_attn_ln_b': _L2_attn_in['ln_b'], 'L2_ffn_router_weight': _L2_ffn_in['router_weight'], 'L2_ffn_e_score_bias': _L2_ffn_in['e_score_bias'], 'L2_ffn_gate_up_proj': _L2_ffn_in['gate_up_proj'], 'L2_ffn_down_proj': _L2_ffn_in['down_proj'], 'L2_ffn_shared_gate_w': _L2_ffn_in['shared_gate_w'], 'L2_ffn_shared_up_w': _L2_ffn_in['shared_up_w'], 'L2_ffn_shared_down_w': _L2_ffn_in['shared_down_w'], 'L3_attn_Wz': _L3_attn_in['Wz'], 'L3_attn_bz': _L3_attn_in['bz'], 'L3_attn_Wh': _L3_attn_in['Wh'], 'L3_attn_bh': _L3_attn_in['bh'], 'L3_attn_swish_beta': _L3_attn_in['swish_beta'], 'L3_attn_ln_gamma': _L3_attn_in['ln_gamma'], 'L3_attn_ln_beta': _L3_attn_in['ln_beta'], 'L3_ffn_U1': _L3_ffn_in['U1'], 'L3_ffn_V1': _L3_ffn_in['V1'], 'L3_ffn_b1': _L3_ffn_in['b1'], 'L3_ffn_U2': _L3_ffn_in['U2'], 'L3_ffn_V2': _L3_ffn_in['V2'], 'L3_ffn_b2': _L3_ffn_in['b2']}
    _x0 = _d['L0_attn_hidden_states']
    _d['L0_attn_hidden_states'] = jax.random.normal(jax.random.fold_in(jax.random.key(seed), 1), (32, 256, 128), dtype=_x0.dtype)
    del _x0
    return _d

def reference(L0_attn_hidden_states, L0_attn_Wq, L0_attn_bq, L0_attn_Wk, L0_attn_bk, L0_attn_Wv, L0_attn_bv, L0_attn_rel_bias, L0_ffn_w_up, L0_ffn_w_down, L1_attn_w_attn, L1_attn_b_attn, L1_attn_w_proj, L1_attn_b_proj, L1_ffn_Wr, L1_ffn_W1, L1_ffn_b1, L1_ffn_W2, L1_ffn_b2, L2_attn_W_in, L2_attn_conv_w, L2_attn_conv_b, L2_attn_W_x, L2_attn_W_dt, L2_attn_b_dt, L2_attn_log_A, L2_attn_D_param, L2_attn_W_out, L2_attn_ln_w, L2_attn_ln_b, L2_ffn_router_weight, L2_ffn_e_score_bias, L2_ffn_gate_up_proj, L2_ffn_down_proj, L2_ffn_shared_gate_w, L2_ffn_shared_up_w, L2_ffn_shared_down_w, L3_attn_Wz, L3_attn_bz, L3_attn_Wh, L3_attn_bh, L3_attn_swish_beta, L3_attn_ln_gamma, L3_attn_ln_beta, L3_ffn_U1, L3_ffn_V1, L3_ffn_b1, L3_ffn_U2, L3_ffn_V2, L3_ffn_b2):

    def _L0_attn_ref(hidden_states, Wq, bq, Wk, bk, Wv, bv, rel_bias):
        import math
        import jax, jax.numpy as jnp
        import numpy as np
        NUM_HEADS = 16
        NUM_BUCKETS = 32

        def _relative_position_bucket(relative_position):
            num_buckets = NUM_BUCKETS
            n = jnp.maximum(-relative_position, 0)
            max_exact = num_buckets // 2
            is_small = n < max_exact
            n_safe = jnp.maximum(n, 1).astype(jnp.float32)
            val_if_large = max_exact + (jnp.log(n_safe / max_exact) / math.log(num_buckets / max_exact) * (num_buckets - max_exact)).astype(jnp.int32)
            val_if_large = jnp.minimum(val_if_large, num_buckets - 1)
            return jnp.where(is_small, n, val_if_large)
        B, S, D = hidden_states.shape
        H = NUM_HEADS
        dh = D // H
        q = (hidden_states @ Wq + bq).reshape(B, S, H, dh)
        k = (hidden_states @ Wk + bk).reshape(B, S, H, dh)
        v = (hidden_states @ Wv + bv).reshape(B, S, H, dh)
        scores = jnp.einsum('bqhd,bkhd->bhqk', q, k) / math.sqrt(dh)
        ctx_pos = jnp.arange(S)[:, None]
        mem_pos = jnp.arange(S)[None, :]
        buckets = _relative_position_bucket(mem_pos - ctx_pos)
        bias = rel_bias[buckets]
        bias = jnp.transpose(bias, (2, 0, 1))
        scores = scores + bias[None]
        attn = jax.nn.softmax(scores, axis=-1)
        context = jnp.einsum('bhqk,bkhd->bqhd', attn, v).reshape(B, S, D)
        return context

    def _L0_ffn_ref(x, w_up, w_down):
        import jax, jax.numpy as jnp
        import numpy as np
        EPS = 1e-08

        def _ternary_linear(x, w):
            alpha = jnp.mean(jnp.abs(w))
            w_t = jnp.sign(w) * (jnp.abs(w) > 0.5 * alpha).astype(w.dtype)
            w_q = w + jax.lax.stop_gradient(w_t - w)
            d = x.shape[-1]
            rms = jnp.sqrt(jnp.sum(x * x, axis=-1, keepdims=True)) / jnp.sqrt(jnp.asarray(d, x.dtype))
            x_norm = x / (rms + EPS)
            return jnp.einsum('bsd,fd->bsf', x_norm, w_q)
        h = jax.nn.gelu(_ternary_linear(x, w_up), approximate=False)
        return _ternary_linear(h, w_down)

    def _L1_attn_ref(x, w_attn, b_attn, w_proj, b_proj):
        import math
        import jax, jax.numpy as jnp
        import numpy as np
        B, T, C = (4, 256, 128)
        H = 16
        D = C // H
        b, t, c = x.shape
        qkv = x @ w_attn + b_attn
        q, k, v = jnp.split(qkv, 3, axis=-1)
        q = q.reshape(b, t, H, D)
        k = k.reshape(b, t, H, D)
        v = v.reshape(b, t, H, D)
        att = jnp.einsum('bthd,bshd->bhts', q, k) * (1.0 / math.sqrt(D))
        causal = jnp.tril(jnp.ones((t, t), dtype=bool))
        att = jnp.where(causal, att, -jnp.inf)
        att = jax.nn.softmax(att, axis=-1)
        y = jnp.einsum('bhts,bshd->bthd', att, v).reshape(b, t, c)
        return y @ w_proj + b_proj

    def _L1_ffn_ref(x, Wr, W1, b1, W2, b2):
        import jax, jax.numpy as jnp
        import numpy as np
        from math import ceil
        CAPACITY_FACTOR = 2.0
        MIN_CAPACITY = 4
        B, S, D = x.shape
        E = Wr.shape[1]
        N = B * S
        k = max(MIN_CAPACITY, ceil(N * CAPACITY_FACTOR / E))
        xt = x.reshape(N, D)
        scores = jax.nn.softmax(xt @ Wr, axis=-1)
        G, idx = jax.lax.top_k(scores.T, k)
        X_in = xt[idx]
        h = jax.nn.gelu(jnp.einsum('ekd,edh->ekh', X_in, W1) + b1[:, None, :], approximate=False)
        X_e = jnp.einsum('ekh,ehd->ekd', h, W2) + b2[:, None, :]
        contrib = (G[..., None] * X_e).reshape(E * k, D)
        out = jnp.zeros((N, D), dtype=x.dtype).at[idx.reshape(-1)].add(contrib)
        return out.reshape(B, S, D)

    def _L2_attn_ref(x, W_in, conv_w, conv_b, W_x, W_dt, b_dt, log_A, D_param, W_out, ln_w, ln_b):
        import jax, jax.numpy as jnp
        import numpy as np
        DT_MIN, DT_MAX = (0.001, 0.1)
        DT_RANK, D_STATE, D_CONV = (64, 16, 4)
        B, T, Dm = x.shape
        Dn = W_dt.shape[0]
        residual = x
        mu = x.mean(-1, keepdims=True)
        var = x.var(-1, keepdims=True)
        xn = (x - mu) / jnp.sqrt(var + 1e-05) * ln_w + ln_b
        xz = xn @ W_in.T
        x_inner, z = jnp.split(xz, 2, axis=-1)
        xc = jnp.transpose(x_inner, (0, 2, 1))
        xc = jax.lax.conv_general_dilated(xc, conv_w, window_strides=(1,), padding=[(D_CONV - 1, 0)], dimension_numbers=('NCH', 'OIH', 'NCH'), feature_group_count=Dn)
        xc = xc + conv_b[None, :, None]
        u = jax.nn.silu(jnp.transpose(xc, (0, 2, 1)))
        xbc = u @ W_x.T
        dt_low, B_ssm, C_ssm = jnp.split(xbc, [DT_RANK, DT_RANK + D_STATE], axis=-1)
        dt = jax.nn.softplus(dt_low @ W_dt.T + b_dt) + DT_MIN
        dt = jnp.clip(dt, DT_MIN, DT_MAX)
        A = -jnp.exp(log_A)

        def step(h, inp):
            dt_t, u_t, B_t, C_t = inp
            dA = jnp.exp(dt_t[:, :, None] * A)
            h = dA * h + (dt_t * u_t)[:, :, None] * B_t[:, None, :]
            y = jnp.einsum('bdn,bn->bd', h, C_t)
            return (h, y)
        h0 = jnp.zeros((B, Dn, D_STATE), x.dtype)
        _, ys = jax.lax.scan(step, h0, (jnp.moveaxis(dt, 1, 0), jnp.moveaxis(u, 1, 0), jnp.moveaxis(B_ssm, 1, 0), jnp.moveaxis(C_ssm, 1, 0)))
        y = jnp.moveaxis(ys, 0, 1)
        y = y + u * D_param
        y = y * jax.nn.silu(z)
        return y @ W_out.T + residual

    def _L2_ffn_ref(hidden_states, router_weight, e_score_bias, gate_up_proj, down_proj, shared_gate_w, shared_up_w, shared_down_w):
        import jax, jax.numpy as jnp
        import numpy as np
        H = 128
        E = 32
        I = 64
        TOP_K = 6
        IS = 128
        NORM_MIN = 1e-12
        B, S = (2, 128)
        b, s, h = hidden_states.shape
        x = hidden_states.reshape(-1, h)
        T = x.shape[0]
        shared_out = jax.nn.silu(x @ shared_gate_w.T) * (x @ shared_up_w.T) @ shared_down_w.T
        xf = x.astype(jnp.float32)
        router_logits = xf @ router_weight.T
        routing_weights = jax.nn.softmax(router_logits, axis=-1)
        corrected = routing_weights + e_score_bias
        _, top_idx = jax.lax.top_k(corrected, TOP_K)
        top_w = jnp.take_along_axis(routing_weights, top_idx, axis=-1)
        top_w = top_w / jnp.clip(top_w.sum(axis=-1, keepdims=True), NORM_MIN)
        top_w = top_w.astype(x.dtype)
        combine = jnp.zeros((T, E), x.dtype).at[jnp.arange(T)[:, None], top_idx].add(top_w)
        gu = jnp.einsum('th,eih->tei', x, gate_up_proj)
        gate, up = jnp.split(gu, 2, axis=-1)
        hmid = jax.nn.silu(gate) * up
        y = jnp.einsum('tei,ehi->teh', hmid, down_proj)
        out = jnp.einsum('teh,te->th', y, combine) + shared_out
        return out.reshape(b, s, h)

    def _L3_attn_ref(x, Wz, bz, Wh, bh, swish_beta, ln_gamma, ln_beta):
        import jax, jax.numpy as jnp
        import numpy as np
        LN_EPS = 1e-05

        def _min_gru(x, Wz, bz, Wh, bh):
            z = jax.nn.sigmoid(jnp.einsum('btd,de->bte', x, Wz) + bz)
            h_tilde = jnp.einsum('btd,de->bte', x, Wh) + bh
            a = 1.0 - z
            b = z * h_tilde

            def combine(c1, c2):
                a1, b1 = c1
                a2, b2 = c2
                return (a1 * a2, a2 * b1 + b2)
            _, h = jax.lax.associative_scan(combine, (a, b), axis=1)
            return h
        h = _min_gru(x, Wz, bz, Wh, bh)
        s = swish_beta * h
        y = s * jax.nn.sigmoid(s)
        mu = jnp.mean(y, axis=-1, keepdims=True)
        var = jnp.mean(jnp.square(y - mu), axis=-1, keepdims=True)
        out = (y - mu) * jax.lax.rsqrt(var + LN_EPS) * ln_gamma + ln_beta
        return out

    def _L3_ffn_ref(x, U1, V1, b1, U2, V2, b2):
        import jax, jax.numpy as jnp
        import numpy as np
        D_MODEL, D_FF, RANK = (128, 512, 32)
        B, S = (4, 512)
        P = jnp.einsum('bsd,dr->bsr', x, U1)
        H = jax.nn.gelu(jnp.einsum('bsr,rf->bsf', P, V1) + b1)
        Q = jnp.einsum('bsf,fr->bsr', H, U2)
        return jnp.einsum('bsr,rd->bsd', Q, V2) + b2
    x = L0_attn_hidden_states
    x = x + _L0_attn_ref(_layernorm(x, axis=-1), L0_attn_Wq, L0_attn_bq, L0_attn_Wk, L0_attn_bk, L0_attn_Wv, L0_attn_bv, L0_attn_rel_bias)
    x = x + _L0_ffn_ref(_layernorm(x, axis=-1), L0_ffn_w_up, L0_ffn_w_down)
    x = x + _L1_attn_ref(_layernorm(x, axis=-1), L1_attn_w_attn, L1_attn_b_attn, L1_attn_w_proj, L1_attn_b_proj)
    x = x + _L1_ffn_ref(_layernorm(x, axis=-1), L1_ffn_Wr, L1_ffn_W1, L1_ffn_b1, L1_ffn_W2, L1_ffn_b2)
    x = x + _L2_attn_ref(_layernorm(x, axis=-1), L2_attn_W_in, L2_attn_conv_w, L2_attn_conv_b, L2_attn_W_x, L2_attn_W_dt, L2_attn_b_dt, L2_attn_log_A, L2_attn_D_param, L2_attn_W_out, L2_attn_ln_w, L2_attn_ln_b)
    x = x + _L2_ffn_ref(_layernorm(x, axis=-1), L2_ffn_router_weight, L2_ffn_e_score_bias, L2_ffn_gate_up_proj, L2_ffn_down_proj, L2_ffn_shared_gate_w, L2_ffn_shared_up_w, L2_ffn_shared_down_w)
    x = x + _L3_attn_ref(_layernorm(x, axis=-1), L3_attn_Wz, L3_attn_bz, L3_attn_Wh, L3_attn_bh, L3_attn_swish_beta, L3_attn_ln_gamma, L3_attn_ln_beta)
    x = x + _L3_ffn_ref(_layernorm(x, axis=-1), L3_ffn_U1, L3_ffn_V1, L3_ffn_b1, L3_ffn_U2, L3_ffn_V2, L3_ffn_b2)
    return x

_drawn_inputs = setup_inputs


def setup_inputs(seed=0):
    import zlib

    import numpy as np

    out = dict(_drawn_inputs(seed))
    spreads = {'L0_attn_bq': (0.0, 0.638),
     'L0_attn_bk': (0.0, 2.0),
     'L0_attn_bv': (0.0, 0.1),
     'L1_ffn_b1': (0.0, 0.8),
     'L1_ffn_b2': (0.0, 0.8),
     'L2_attn_conv_b': (0.0, 0.8),
     'L2_attn_b_dt': (0.0, 0.8),
     'L2_attn_D_param': (1.0, 0.6),
     'L2_attn_ln_w': (1.0, 0.6),
     'L2_attn_ln_b': (0.0, 0.8),
     'L2_ffn_e_score_bias': (0.0, 2.0),
     'L3_attn_bz': (0.0, 2.0),
     'L3_attn_bh': (0.0, 2.0),
     'L3_attn_ln_gamma': (1.0, 0.6),
     'L3_attn_ln_beta': (0.0, 2.0),
     'L3_ffn_b1': (0.0, 2.0),
     'L3_ffn_b2': (0.0, 2.0)}
    factors = {'L0_attn_rel_bias': 8.0,
     'L1_attn_w_attn': 8.0,
     'L1_attn_b_attn': 8.0,
     'L1_attn_w_proj': 8.0,
     'L1_attn_b_proj': 8.0,
     'L1_ffn_Wr': 3.69,
     'L1_ffn_W1': 4.029,
     'L1_ffn_W2': 3.753,
     'L2_attn_W_in': 8.0,
     'L2_attn_conv_w': 8.0,
     'L2_attn_W_x': 8.0,
     'L2_attn_log_A': 8.0,
     'L2_attn_W_out': 8.0,
     'L2_ffn_router_weight': 64.0,
     'L2_ffn_gate_up_proj': 64.0,
     'L2_ffn_down_proj': 64.0,
     'L2_ffn_shared_gate_w': 64.0,
     'L2_ffn_shared_up_w': 64.0,
     'L2_ffn_shared_down_w': 64.0,
     'L3_attn_Wz': 26.744,
     'L3_ffn_U1': 64.0,
     'L3_ffn_V1': 64.0,
     'L3_ffn_U2': 64.0,
     'L3_ffn_V2': 64.0,
     'L3_attn_Wh': 8.0}
    for name, (base, spread) in spreads.items():
        noise = np.random.default_rng([zlib.crc32(name.encode()), seed]).standard_normal(out[name].shape)
        drawn = base * np.exp(spread * noise) if base else spread * noise
        out[name] = jnp.asarray(drawn.astype(out[name].dtype))
    for name, factor in factors.items():
        out[name] = (out[name] * factor).astype(out[name].dtype)
    return out
```

```python
import math
from contextlib import ExitStack

import numpy as np
import concourse.bass as bass
from concourse import mybir

F32 = mybir.dt.float32
BF16 = mybir.dt.bfloat16
HOST_BF16 = mybir.dt.np(BF16)
ALU = mybir.AluOpType
ACT = mybir.ActivationFunctionType
AX = mybir.AxisListType

P = 128
B, S, D = 32, 256, 128
TILES = B * S // P
TB = S // P
H, DH = 16, 8
EPS = 1e-5


def wait(eng, sem, value):
    if not isinstance(value, int) or value > 0:
        eng.wait_ge(sem, value)


def waits(eng, *pairs):
    pairs = [(sem, v if isinstance(v, int) else eng.snap(v)) for sem, v in pairs]
    for sem, v in pairs:
        wait(eng, sem, v)


class Scope:

    def __init__(self, nc, ctx, name):
        self.nc, self.ctx, self.name, self.sems = nc, ctx, name, []
        ctx.callback(self.close)

    def sb(self, name, shape, dt=F32):
        return self.ctx.enter_context(self.nc.sbuf_tensor(f"{self.name}_{name}", shape, dt))

    def ps(self, name, shape, dt=F32):
        return self.ctx.enter_context(self.nc.psum_tensor(f"{self.name}_{name}", shape, dt))

    def sem(self, name):
        self.sems.append(self.nc.alloc_semaphore(name=f"{self.name}_{name}"))
        return self.sems[-1]

    def close(self):
        if self.sems:
            self.nc.clear_and_free_semaphores(self.sems)
            self.nc.all_engine_barrier()


def norm_factors(nc, res, name, then=None):
    st, mean, rstd, rstd2 = res["stats"], res["mean"], res["rstd"], res["rstd2"]
    with ExitStack() as ctx:
        sc = Scope(nc, ctx, name)
        tmp, dif, var, nvar = (sc.sb(n, [P, TILES]) for n in ("tmp", "dif", "var", "nvar"))
        step, var_ready, root_ready = sc.sem("step"), sc.sem("var_ready"), sc.sem("root_ready")
        block = ctx.enter_context(nc.Block())
        me, ce, mo, co = st[:, :, 1], st[:, :, 2], st[:, :, 4], st[:, :, 5]

        @block.vector
        def _(v):
            nc.vector.tensor_tensor(tmp[:], me, mo, ALU.add).then_inc(step, 1)
            nc.vector.tensor_tensor(dif[:], me, mo, ALU.subtract).then_inc(step, 1)
            nc.vector.tensor_tensor(var[:], ce, co, ALU.add).then_inc(step, 1)
            v.wait_ge(step, 3)
            nc.vector.tensor_scalar(mean[:], tmp[:], 0.5, None, ALU.mult).then_inc(step, 1)
            nc.vector.scalar_tensor_tensor(out=dif[:], in0=dif[:], scalar=0.25, in1=dif[:],
                                           op0=ALU.mult, op1=ALU.mult).then_inc(step, 1)
            v.wait_ge(step, 5)
            nc.vector.scalar_tensor_tensor(out=var[:], in0=var[:], scalar=1.0 / D, in1=dif[:],
                                           op0=ALU.mult, op1=ALU.add).then_inc(step, 1)
            v.wait_ge(step, 6)
            nc.vector.tensor_scalar(nvar[:], var[:], EPS, None, ALU.add).then_inc(var_ready, 1)
            v.wait_ge(root_ready, 1)
            nc.vector.reciprocal(rstd[:], tmp[:]).then_inc(step, 1)
            if then:
                v.wait_ge(step, 7)
                nc.vector.tensor_tensor(dif[:], rstd[:], rstd[:], ALU.mult).then_inc(step, 1)
                v.wait_ge(step, 8)
                nc.vector.tensor_tensor(dif[:], dif[:], var[:], ALU.mult).then_inc(step, 1)
                v.wait_ge(step, 9)
                nc.vector.tensor_scalar(var[:], dif[:], EPS if then == "norm" else 0.0, None, ALU.add)\
                    .then_inc(var_ready, 1)
                v.wait_ge(root_ready, 2)
                nc.vector.tensor_scalar(dif[:], tmp[:], 0.0 if then == "norm" else 1e-8, None, ALU.add)\
                    .then_inc(step, 1)
                v.wait_ge(step, 10)
                nc.vector.reciprocal(var[:], dif[:]).then_inc(step, 1)
                v.wait_ge(step, 11)
                nc.vector.tensor_tensor(rstd2[:], var[:], rstd[:], ALU.mult)

        @block.scalar
        def _(a):
            a.wait_ge(var_ready, 1)
            nc.scalar.activation(tmp[:], nvar[:], ACT.Sqrt).then_inc(root_ready, 1)
            if then:
                a.wait_ge(var_ready, 2)
                nc.scalar.activation(tmp[:], var[:], ACT.Sqrt).then_inc(root_ready, 1)


def pipeline(eng, step, n, lead, unroll=2, back=0, peel=1):
    def static(g):
        step(g, g % unroll, lambda off: 0 <= g + off < n)

    start = peel + back + (n - lead - back - peel) % unroll
    rounds = (n - lead - start) // unroll
    for g in range(-lead, start):
        static(g)
    with eng.Fori(0, rounds) as i:
        for k in range(unroll):
            step(i * unroll + (start + k), (start + k) % unroll, lambda off: True)
    for g in range(n - lead, n + back):
        static(g)


G = 4
GT = G * P
GROUPS = TILES // G


def attention(nc, res, name, w, causal):
    x, mean, rstd, stats = res["x"], res["mean"], res["rstd"], res["stats"]
    scale = 1.0 / math.sqrt(DH)
    ROWS, MROW, KM = 3 * 3 * DH, 96, 96
    NPART, BUF, NP = 3, 4, 4
    BAND = 160
    K0Q, K1Q = S, (P if causal else S)
    with ExitStack() as ctx:
        sc = Scope(nc, ctx, name)
        wqkv = sc.sb("wqkv", [P, 3, P])
        bqk = sc.sb("bqk", [P, 2])
        bqs = sc.sb("bqs", [P, 1])
        bv = sc.sb("bv", [P, P])
        xn = [sc.sb(f"xn{i}", [P, TB, D]) for i in range(2)]
        xnT = sc.sb("xnT", [P, S])
        qk32 = sc.sb("qk32", [P, 2 * S])
        rest = sc.sb("rest", [P, 2 * S])
        parts = sc.sb("parts", [P, NPART, 2 * S], BF16)
        Qp = [sc.sb(f"Qp{i}", [P, H, S], BF16) for i in range(BUF)]
        Kp = [sc.sb(f"Kp{i}", [P, H, S], BF16) for i in range(BUF)]
        V = [sc.sb(f"V{i}", [P, TB, H, 32]) for i in range(BUF)]
        Mx = [sc.sb(f"Mx{i}", [P, TB, H]) for i in range(2)]
        mrest = sc.sb("mrest", [P, TB, H])
        mparts = [sc.sb(f"mparts{i}", [P, TB, P // H, H], BF16) for i in range(2)]
        mrow = [sc.sb(f"mrow{i}", [NPART * H, S], BF16) for i in range(2)]
        Pr = [sc.sb(f"Pr{i}", [P, 2 * S]) for i in range(NP)]
        osb = [sc.sb(f"osb{i}", [P, S]) for i in range(2)]
        rc = [sc.sb(f"rc{i}", [P, TB, 4]) for i in range(2)]
        prod = [sc.sb(f"prod{i}", [P, TB, 4, DH]) for i in range(2)]
        Sx = [sc.ps(f"Sx{i}", [P, 2 * S]) for i in range(2)]
        Se = [sc.ps(f"Se{i}", [P, 2 * S]) for i in range(2)]
        O = [sc.ps(f"O{i}", [P, 2 * S]) for i in range(2)]
        OT = sc.ps("OT", [P, 2 * S])[:, 0:S]
        TURN = sc.ps("TURN", [P, 2 * S])
        mps = TURN[:, 0:P].bitcast(BF16)
        if causal:
            y = [sc.sb(f"y{i}", [P, TB, D]) for i in range(2)]
            yT = sc.sb("yT", [P, S])
            wproj = sc.sb("wproj", [P, P])
            bproj = sc.sb("bproj", [1, P])
            maskq = sc.sb("maskq", [P, P], BF16)
            maskk = sc.sb("maskk", [P, P], BF16)
        else:
            bmax = sc.sb("bmax", [P, H, 3 * P], BF16)
            bexp = sc.sb("bexp", [P, NPART, H, BAND], BF16)
            flip = sc.sb("flip", [P, P], BF16)

        SEMS = ("w v_zero cleared ones consts xn_ready xn_used xt_ready qk_mm qk_ev first_part v_mm v_ready seq split_done written packed "
                "mx_mm red_done mseq mp_ready mt_mm mrow_ready mpacked se_mm exp_done pv_done "
                "o_ev ot_mm cseq fin rseq yt_mm yt_ev pr_mm pr_done").split()
        s = {n: sc.sem(n) for n in SEMS}
        LATE = 2

        def slot(b, j):
            return (b + 2, j - LATE) if j >= LATE else (b + 1, j + 8 - LATE)

        PART = DH * H * S
        packing = nc.dram_tensor(name + "_packing", [NPART, 2, DH, H, S], BF16, kind="Internal").ap()
        loads = [(wqkv[:], w["wqkv"]), (bqk[:], w["bqk"]), (bv[:], w["bv"])]
        if causal:
            loads += [(maskq[:], w["maskq"]), (maskk[:], w["maskk"]), (wproj[:], w["wproj"]), (bproj[:], w["bproj"])]
        ident, identb = res["ident"], res["identb"]
        if not causal:
            loads += [(flip[:], w["flip"])]
            crows = bias_setup(nc, sc, w, bmax, bexp, BAND, [Sx[0], Sx[1], Se[0]])

        with nc.Block() as block:

            @block.sync
            def _(sp):
                for dst, src in loads:
                    sp.dma_start(dst, src).then_inc(s["w"], 16)
                sp.wait_ge(s["cleared"], 1)
                for k in range(BUF):
                    sp.dma_start(Kp[k][MROW:MROW + 9], w["krows"]).then_inc(s["consts"], 16)
                    if not causal:
                        sp.dma_start(Qp[k][MROW + 3:MROW + 9], crows).then_inc(s["consts"], 16)

                def step(b, k, a, x_, m, c, p):
                    if m:
                        kb = (k + 1) % BUF
                        wait(sp, s["mrow_ready"], b + 2)
                        sp.dma_start(Qp[kb][MROW:MROW + 3, :, :], mrow[kb % 2][:, :]).then_inc(s["mpacked"], 16)
                    if a:
                        kb = (k + 3) % BUF
                        wait(sp, s["split_done"], b + 4)
                        sp.dma_start(packing.rearrange("i c e h q -> (e h) (i c) q"),
                                     parts[:].rearrange("p i (c q) -> p (i c) q", c=2)).then_inc(s["written"], 16)
                        wait(sp, s["written"], 16 * (b + 4))
                        row = [[H * S, DH], [1, H * S]]
                        for j in range(3):
                            r = slice(j * 3 * DH, (j + 1) * 3 * DH)
                            sp.dma_start(Qp[kb][r], bass.AP(packing.tensor, 0, [[2 * PART, 3], *row]))\
                                .then_inc(s["packed"], 16)
                            sp.dma_start(Kp[kb][r], bass.AP(packing.tensor, (2 * j + 1) * PART, [[0, 3], *row]))\
                                .then_inc(s["packed"], 16)

                run_steps(sp, step)

            @block.gpsimd
            def _(g):
                for k in range(BUF):
                    nc.gpsimd.memset(V[k][:], 0.0).then_inc(s["v_zero"], 1)
                g.wait_ge(s["v_zero"], BUF)
                for k in range(BUF):
                    last = nc.gpsimd.memset(V[k][:, :, :, DH:DH + 1], 1.0)
                last.then_inc(s["ones"], 1)

                def step(b, k, a, x_, m, c, p):
                    if not a:
                        return
                    bb = b + 3
                    wait(g, s["written"], 16 * bb)
                    wait(g, s["first_part"], bb + 1)
                    for out, name in ((rest[:], "seq"), (parts[:, 1, :], "seq")):
                        nc.gpsimd.tensor_tensor(out, qk32[:], parts[:, 0, :], ALU.subtract).then_inc(s[name], 1)
                    wait(g, s["seq"], 2 * bb + 2)
                    wait(g, s["packed"], 6 * 16 * bb)
                    wait(g, s["pv_done"], 16 * b)
                    nc.gpsimd.tensor_tensor(parts[:, 2, :], rest[:], parts[:, 1, :], ALU.subtract)\
                        .then_inc(s["split_done"], 1)

                run_steps(g, step)

            @block.scalar
            def _(act):
                act.wait_ge(s["ones"], 1)
                act.wait_ge(s["w"], len(loads) * 16)
                nc.scalar.activation(bqs[:], bqk[:, 0:1], ACT.Copy, scale=scale).then_inc(s["rseq"], 1)
                act.wait_ge(s["rseq"], 1)

                def project(bb):
                    wait(act, s["xn_used"], bb + 1)
                    wait(act, s["v_mm"], bb)
                    nc.scalar.activation(xnT[:], TURN[:, 0:S], ACT.Copy).then_inc(s["xt_ready"], 1)

                def split(bb):
                    wait(act, s["qk_mm"], bb + 1)
                    wait(act, s["split_done"], bb)
                    wait(act, s["written"], 16 * bb)
                    nc.scalar.activation(qk32[:, 0:S], TURN[:, 0:S], ACT.Identity, bias=bqs[:], scale=scale)\
                        .then_inc(s["qk_ev"], 1)
                    nc.scalar.activation(qk32[:, S:2 * S], TURN[:, S:2 * S], ACT.Identity, bias=bqk[:, 1:2])\
                        .then_inc(s["qk_ev"], 1)
                    wait(act, s["qk_ev"], 2 * bb + 2)
                    nc.scalar.activation(parts[:, 0], qk32[:], ACT.Copy).then_inc(s["first_part"], 1)

                def evac(b, c):
                    wait(act, s["pv_done"], 16 * b + 4 * c + 4)
                    wait(act, s["ot_mm"], 4 * b + c - 1)
                    nc.scalar.activation(osb[c % 2][:], O[c % 2][:, 0:S], ACT.Copy).then_inc(s["o_ev"], 1)

                def step(b, k, a, x_, m, c, p):
                    for j in range(8):
                        if m and j == 3:
                            wait(act, s["mt_mm"], b + 2)
                            wait(act, s["mpacked"], 16 * b)
                            nc.scalar.activation(mrow[(k + 1) % 2][:], mps[0:NPART * H, :], ACT.Copy).then_inc(s["mrow_ready"], 1)
                        if causal and p and j == 4:
                            wait(act, s["yt_mm"], b)
                            nc.scalar.activation(yT[:], TURN[:, 0:S], ACT.Copy).then_inc(s["yt_ev"], 1)
                        if c:
                            for h in (2 * j, 2 * j + 1):
                                wait(act, s["se_mm"], 16 * b + h + 1)
                                wait(act, s["pv_done"], 16 * b + h + 1 - NP)
                                nc.scalar.activation(Pr[h % NP][:, 0:K0Q + K1Q], Se[h % 2][:, 0:K0Q + K1Q],
                                                     ACT.Exp).then_inc(s["exp_done"], 1)
                            if j % 2 == 0 and j:
                                evac(b, j // 2 - 1)
                        if p and j == 0:
                            evac(b - 1, 3)
                        if a and j == 0:
                            project(b + 3)
                        if a and j == 1:
                            split(b + 3)

                run_steps(act, step)

            @block.vector
            def _(v):
                for k in range(BUF):
                    nc.vector.memset(Qp[k][64:128].rearrange("p h q -> p (h q)").bitcast(F32), 0.0)
                    last = nc.vector.memset(Kp[k][64:128].rearrange("p h q -> p (h q)").bitcast(F32), 0.0)
                for i in range(2):
                    last = nc.vector.memset(mparts[i][:], 0.0)
                last.then_inc(s["cleared"], 1)
                nc.vector.memset(Mx[0][:, 0, 0:1], 0.0).then_inc(s["pr_done"], 1)
                v.wait_ge(s["cleared"], 1)
                v.wait_ge(s["w"], len(loads) * 16)
                v.wait_ge(s["ones"], 1)

                def finish(b, k, c):
                    wait(v, s["ot_mm"], 4 * b + c + 1)
                    q = c % 2
                    o4 = OT.rearrange("p (t h e) -> p t h e", t=TB, h=4)
                    n = 3 * (4 * b + c)
                    nc.vector.reciprocal(rc[q][:], o4[:, :, :, DH]).then_inc(s["cseq"], 1)
                    wait(v, s["cseq"], n + 1)
                    for t in range(TB):
                        dst = y[k % 2][:, t, 32 * c:32 * c + 32].rearrange("p (h e) -> p h e", h=4) if causal \
                            else prod[q][:, t]
                        nc.vector.tensor_tensor(dst, o4[:, t, :, 0:DH],
                                                rc[q][:, t].unsqueeze(2).to_broadcast([P, 4, DH]),
                                                ALU.mult).then_inc(s["cseq"], 1)
                    if not causal:
                        wait(v, s["cseq"], n + 3)
                        xs = x[:, bass.ds(TB * b, TB), 32 * c:32 * c + 32]
                        nc.vector.tensor_tensor(xs, xs, prod[q][:].rearrange("p t h e -> p t (h e)"),
                                                ALU.add).then_inc(s["fin"], 1)

                def split_maxima(bb, kb):
                    wait(v, s["red_done"], 16 * bb + 16)
                    wait(v, s["mt_mm"], bb - 1)
                    mp = mparts[kb]
                    nc.vector.tensor_scalar(mp[:, :, 0], Mx[kb][:], -1.0, None, ALU.mult).then_inc(s["mseq"], 1)
                    wait(v, s["mseq"], 3 * bb + 1)
                    nc.vector.scalar_tensor_tensor(out=mrest[:], in0=Mx[kb][:], scalar=-1.0, in1=mp[:, :, 0],
                                                   op0=ALU.mult, op1=ALU.subtract).then_inc(s["mseq"], 1)
                    wait(v, s["mseq"], 3 * bb + 2)
                    nc.vector.tensor_copy(mp[:, :, 1], mrest[:]).then_inc(s["mseq"], 1)
                    wait(v, s["mseq"], 3 * bb + 3)
                    nc.vector.tensor_tensor(mp[:, :, 2], mrest[:], mp[:, :, 1], ALU.subtract)\
                        .then_inc(s["mp_ready"], 1)

                def step(b, k, a, x_, m, c, p):
                    if a:
                        bb = b + 3
                        wait(v, s["xn_used"], bb - 1)
                        for t in range(TB):
                            nc.vector.tensor_scalar(xn[(k + 3) % 2][:, t], x[:, TB * bb + t],
                                                    mean[:, bass.ds(TB * bb + t, 1)],
                                                    rstd[:, bass.ds(TB * bb + t, 1)],
                                                    ALU.subtract, ALU.mult).then_inc(s["xn_ready"], 1)
                    for j in range(8):
                        bb, jj = slot(b, j)
                        if (x_ if j >= LATE else m):
                            for t in range(TB):
                                wait(v, s["mx_mm"], 16 * bb + (2 * jj + t + 1))
                                wd = P * (t + 1) if causal else S
                                nc.vector.tensor_reduce(
                                    Mx[(k + 2 - (j < LATE)) % 2][:, t, 2 * jj:2 * jj + 2],
                                    Sx[t][:, 0:2 * wd].rearrange("p (h q) -> p h q", h=2), AX.X, ALU.max
                                ).then_inc(s["red_done"], 1)
                        if m and j == LATE - 1:
                            split_maxima(b + 1, (k + 1) % 2)
                        if a and j == 5:
                            bb = b + 3
                            wait(v, s["v_mm"], bb + 1)
                            wait(v, s["pv_done"], 16 * (bb - 3))
                            for t in range(TB):
                                nc.vector.tensor_tensor(
                                    V[(k + 3) % BUF][:, t, :, 0:DH],
                                    TURN[:, t * P:t * P + P].rearrange("p (h e) -> p h e", h=H),
                                    bv[:].rearrange("p (h e) -> p h e", h=H), ALU.add).then_inc(s["v_ready"], 1)
                        if c and j % 2 == 1 and j > 1:
                            finish(b, k, (j - 3) // 2)
                        if p and j == 1:
                            finish(b - 1, k + 3, 3)
                            if not causal:
                                wait(v, s["fin"], 4 * b)
                                for t in range(TB):
                                    nc.vector.bn_stats(stats[:, TB * (b - 1) + t, :], x[:, TB * (b - 1) + t, :])
                        if causal and p and j == 6:
                            wait(v, s["pr_mm"], b)
                            xs = x[:, bass.ds(TB * (b - 1), TB), :]
                            nc.vector.tensor_tensor(xs, xs, TURN[:, 0:S].rearrange("p (t d) -> p t d", t=TB), ALU.add)\
                                .then_inc(s["pr_done"], 1)
                            wait(v, s["pr_done"], b + 1)
                            for t in range(TB):
                                nc.vector.bn_stats(stats[:, TB * (b - 1) + t, :], x[:, TB * (b - 1) + t, :])

                run_steps(v, step)

            @block.tensor
            def _(pe):
                pe.wait_ge(s["w"], len(loads) * 16)
                pe.wait_ge(s["consts"], (BUF if causal else 2 * BUF) * 16)

                def maxima(b, kb, j):
                    for t in range(TB):
                        n = 16 * b + 2 * j + t
                        wait(pe, s["red_done"], n - 1)
                        wd = P * (t + 1) if causal else S
                        if not causal:
                            nc.tensor.matmul(Sx[t][:].rearrange("p (u q) -> p u q", u=2), flip[:],
                                             bmax[:, 2 * j:2 * j + 2, P * (1 - t):P * (1 - t) + S],
                                             start=True, stop=False)
                        for u in range(2):
                            h = 2 * j + u
                            last = nc.tensor.matmul(Sx[t][:, u * wd:u * wd + wd], Qp[kb][0:KM, h, t * P:t * P + P],
                                                    Kp[kb][0:KM, h, 0:wd], start=causal, stop=(not causal and u == 1))
                            if causal:
                                last = nc.tensor.matmul(Sx[t][:, u * wd + wd - P:u * wd + wd], identb[:], maskq[:],
                                                        start=False, stop=True)
                        last.then_inc(s["mx_mm"], 1)

                def scores(b, k, h):
                    wait(pe, s["exp_done"], 16 * b + h - 1)
                    Q, K, out = Qp[k], Kp[k], Se[h % 2]
                    nc.tensor.matmul(out[:, 0:S], K[:, h, 0:P], Q[:, h, :], start=True, stop=False)
                    if causal:
                        nc.tensor.matmul(out[:, 0:P], identb[:], maskk[:], start=False, stop=True)
                    else:
                        for i in range(NPART):
                            nc.tensor.matmul(out[:, 0:BAND], flip[:], bexp[:, i, h, :], start=False,
                                             stop=(i == NPART - 1))
                    nc.tensor.matmul(out[:, K0Q:K0Q + K1Q], K[:, h, P:2 * P], Q[:, h, S - K1Q:S],
                                     start=True, stop=False)
                    if causal:
                        last = nc.tensor.matmul(out[:, K0Q:K0Q + P], identb[:], maskk[:], start=False, stop=True)
                    else:
                        for i in range(NPART):
                            last = nc.tensor.matmul(out[:, S + P:2 * S], flip[:], bexp[:, i, h, 0:P], start=False,
                                                    stop=(i == NPART - 1))
                    last.then_inc(s["se_mm"], 1)

                def values(b, k, h):
                    c, r = h // 4, 32 * (h % 4)
                    if h % 4 == 0:
                        wait(pe, s["o_ev"], 4 * b + c - 1)
                    wait(pe, s["exp_done"], 16 * b + h + 1)
                    nc.tensor.matmul(O[c % 2][r:r + 32, 0:S], V[k][:, 0, h, :], Pr[h % NP][:, 0:S],
                                     start=True, stop=False)
                    nc.tensor.matmul(O[c % 2][r:r + 32, S - K1Q:S], V[k][:, 1, h, :],
                                     Pr[h % NP][:, K0Q:K0Q + K1Q], start=False, stop=True)\
                        .then_inc(s["pv_done"], 1)

                def turn(b, c):
                    wait(pe, s["o_ev"], 4 * b + c + 1)
                    wait(pe, s["cseq"], 3 * (4 * b + c))
                    for t in range(TB):
                        last = nc.tensor.transpose(OT[:, t * P:t * P + P], osb[c % 2][:, t * P:t * P + P], ident[:])
                    last.then_inc(s["ot_mm"], 1)

                uses = {"T": (3, "xt_ready", 1), "K": (3, "qk_ev", 2), "M": (1, "mrow_ready", 1),
                        "Y": (-1, "yt_ev", 1), "V": (3, "v_ready", 2), "R": (-1, "pr_done", 1)}
                order = [u for u in uses if causal or u not in "YR"]

                def claim(use, b):
                    at = order.index(use)
                    for n, u in enumerate(order):
                        off, sem, times = uses[u]
                        done = b + off + (1 if n < at else 0)
                        ahead = 1 if u == "R" else 0
                        if isinstance(b, int):
                            wait(pe, s[sem], times * max(0, min(done, B)) + ahead)
                        elif n == (at - 1) % len(order) or (use == "T" and u == "V"):
                            wait(pe, s[sem], times * done + ahead)

                def step(b, k, a, x_, m, c, p):
                    bb = b + 3
                    if c:
                        wait(pe, s["mpacked"], 16 * (b + 1))
                        wait(pe, s["v_ready"], 2 * (b + 1))
                    for j in range(8):
                        if m and j == 3:
                            wait(pe, s["mp_ready"], b + 2)
                            claim("M", b)
                            for t in range(TB):
                                last = nc.tensor.transpose(
                                    mps[:, t * P:t * P + P],
                                    mparts[(k + 1) % 2][:, t].rearrange("p i h -> p (i h)"), identb[:])
                            last.then_inc(s["mt_mm"], 1)
                        if causal and p and j == 4:
                            wait(pe, s["cseq"], 3 * 4 * b)
                            claim("Y", b)
                            for t in range(TB):
                                last = nc.tensor.transpose(TURN[:, t * P:t * P + P], y[(k + 1) % 2][:, t], ident[:])
                            last.then_inc(s["yt_mm"], 1)
                        if a and j == 5:
                            claim("V", b)
                            for t in range(TB):
                                last = nc.tensor.matmul(TURN[:, t * P:t * P + P], xnT[:, t * P:t * P + P],
                                                        wqkv[:, 2, :], start=True, stop=True)
                            last.then_inc(s["v_mm"], 1)
                        if causal and p and j == 6:
                            wait(pe, s["yt_ev"], b)
                            claim("R", b)
                            for t in range(TB):
                                nc.tensor.matmul(TURN[:, t * P:t * P + P], yT[:, t * P:t * P + P], wproj[:],
                                                 start=True, stop=False)
                                last = nc.tensor.matmul(TURN[:, t * P:t * P + P], res["ones"][0:1, :], bproj[:],
                                                        start=False, stop=True)
                            last.then_inc(s["pr_mm"], 1)
                        if x_ and j == LATE:
                            wait(pe, s["packed"], 6 * 16 * (b + 3))
                        if (x_ if j >= LATE else m):
                            maxima(slot(b, j)[0], (k + 2 - (j < LATE)) % BUF, slot(b, j)[1])
                        for h in (2 * j, 2 * j + 1):
                            if c:
                                scores(b, k, h)
                                if h >= 2:
                                    values(b, k, h - 2)
                            if p and j == 0:
                                values(b - 1, (k + 3) % BUF, h + H - 2)
                        if a and j == 0:
                            wait(pe, s["xn_ready"], 2 * bb + 2)
                            claim("T", b)
                            for t in range(TB):
                                last = nc.tensor.transpose(TURN[:, t * P:t * P + P], xn[(k + 3) % 2][:, t], ident[:])
                            last.then_inc(s["xn_used"], 1)
                        if a and j == 1:
                            wait(pe, s["xt_ready"], bb + 1)
                            claim("K", b)
                            for i in range(2):
                                last = nc.tensor.matmul(TURN[:, i * S:i * S + S], wqkv[:, i, :], xnT[:],
                                                        start=True, stop=True)
                            last.then_inc(s["qk_mm"], 1)
                        if c and j % 2 == 1 and j > 1:
                            turn(b, (j - 3) // 2)
                        if p and j == 1:
                            turn(b - 1, 3)

                run_steps(pe, step)


def run_steps(eng, step):
    def static(b):
        step(b, b % 4, b + 3 < B, 0 <= b + 2 < B, 0 <= b + 1 < B, 0 <= b < B, b >= 1)

    for b in range(-3, 1):
        static(b)
    with eng.Fori(0, B // 4 - 1) as i:
        for k in range(4):
            step(i * 4 + (k + 1), (k + 1) % 4, True, True, True, True, True)
    for b in range(B - 3, B + 1):
        static(b)


def bias_setup(nc, sc, w, bmax, bexp, BAND, banks):
    NPART, N = 3, 512
    rel = sc.sb("rel", [32, H])
    hot = sc.sb("hot", [32, 3, N])
    line = sc.sb("line", [H, 3 * N])
    lrest = sc.sb("lrest", [H, 3 * N])
    lparts = sc.sb("lparts", [H, NPART, 3 * N], BF16)
    with ExitStack() as ctx:
        tmp = Scope(nc, ctx, sc.name + "_bias")
        scratch = nc.dram_tensor(sc.name + "_lines", [NPART, H, 3 * N], BF16, kind="Internal").ap()
        crows = nc.dram_tensor(sc.name + "_crows", [2, NPART, H, S], BF16, kind="Internal").ap()
        loaded, made, got, seq, stored, placed = (tmp.sem(n) for n in "loaded made got seq stored placed".split())
        LP = [bank[0:H, :] for bank in banks]
        block = ctx.enter_context(nc.Block())

        @block.sync
        def _(sp):
            sp.dma_start(rel[:], w["rel"]).then_inc(loaded, 16)
            sp.dma_start(hot[:], w["hot"]).then_inc(loaded, 16)
            sp.wait_ge(seq, 5)
            sp.dma_start(scratch.rearrange("i h n -> h i n"), lparts[:]).then_inc(stored, 16)
            for i in range(NPART):
                sp.dma_start(crows[:, i].rearrange("c h q -> h c q"),
                             lparts[:, i, 2 * N:3 * N].rearrange("h (c q) -> h c q", c=2)).then_inc(placed, 16)
            sp.wait_ge(stored, 16)
            for i in range(NPART):
                sp.dma_start(bexp[:, i], bass.AP(scratch.tensor, i * H * 3 * N + S - P,
                                                 [[1, P], [3 * N, H], [1, BAND]])).then_inc(placed, 16)
            sp.dma_start(bmax[:], bass.AP(scratch.tensor, N,
                                          [[1, P], [3 * N, H], [1, 3 * P]])).then_inc(placed, 16)
            sp.wait_ge(placed, 7 * 16)

        @block.tensor
        def _(pe):
            pe.wait_ge(loaded, 32)
            for i in range(3):
                nc.tensor.matmul(LP[i], rel[:], hot[:, i, :], start=True, stop=True).then_inc(made, 1)

        @block.vector
        def _(v):
            v.wait_ge(made, 3)
            for i in range(3):
                nc.vector.tensor_copy(line[:, i * N:i * N + N], LP[i]).then_inc(got, 1)
            v.wait_ge(got, 3)
            nc.vector.tensor_copy(lparts[:, 0], line[:]).then_inc(seq, 1)
            v.wait_ge(seq, 1)
            nc.vector.tensor_tensor(lrest[:], line[:], lparts[:, 0], ALU.subtract).then_inc(seq, 1)
            v.wait_ge(seq, 2)
            nc.vector.tensor_copy(lparts[:, 1], lrest[:]).then_inc(seq, 1)
            v.wait_ge(seq, 3)
            nc.vector.tensor_tensor(line[:], lrest[:], lparts[:, 1], ALU.subtract).then_inc(seq, 1)
            v.wait_ge(seq, 4)
            nc.vector.tensor_copy(lparts[:, 2], line[:]).then_inc(seq, 1)
    return crows.rearrange("c i h q -> (c i) h q")


def bucket(n):
    n = max(n, 0)
    return n if n < 16 else min(16 + int(math.log(n / 16) / math.log(2) * 16), 31)


def attention_constants():
    bf = HOST_BF16
    n = 512
    hot = np.zeros((32, 3, n), np.float32)
    for c in range(2 * S - 1):
        hot[bucket(c - (S - 1)), 0, c] = 1.0
        hot[bucket((S - 1) - c), 1, c] = 1.0
    hot[31, 2, 160:S] = 1.0
    hot[0, 2, S:S + P] = 1.0
    krows = np.zeros((9, H, S), bf)
    krows[0:3] = 1.0
    krows[3:6, :, 0:P] = 1.0
    krows[6:9, :, P:] = 1.0
    keep = np.tril(np.ones((P, P), bool))
    maskq = np.where(keep, 0.0, -1e30).astype(bf)
    return {"hot": hot, "krows": krows, "maskq": maskq, "maskk": np.ascontiguousarray(maskq.T),
            "ident": np.eye(P, dtype=np.float32), "identb": np.eye(P, dtype=bf),
            "flip": np.ascontiguousarray(np.eye(P, dtype=bf)[::-1])}



def normed(nc, v, res, out, g, rstd, inc):
    for t in range(G):
        nc.vector.tensor_scalar(out[:, t], res["x"][:, G * g + t], res["mean"][:, bass.ds(G * g + t, 1)],
                                rstd[:, bass.ds(G * g + t, 1)], ALU.subtract, ALU.mult).then_inc(inc, 1)


def row_stats(nc, res, g):
    for t in range(G):
        nc.vector.bn_stats(res["stats"][:, G * g + t, :], res["x"][:, G * g + t, :])


def ternary_ffn(nc, res, name, w):
    x, ident = res["x"], res["ident"]
    C = 4
    norm_factors(nc, res, name + "n", then="rms")
    with ExitStack() as ctx:
        sc = Scope(nc, ctx, name)
        wu, wd = sc.sb("wu", [P, C, P]), sc.sb("wd", [P, C, P])
        quantize(nc, res, name, w, wu, wd)
        half = sc.sb("half", [P, G])
        xn = [sc.sb(f"xn{i}", [P, G, D]) for i in range(2)]
        xnT = [sc.sb(f"xnT{i}", [P, GT]) for i in range(2)]
        hT = [sc.sb(f"hT{i}", [P, C, GT]) for i in range(2)]
        sq = [sc.sb(f"sq{i}", [P, C, GT]) for i in range(2)]
        ms, rms, inv = sc.sb("ms", [P, G]), sc.sb("rms", [P, G]), sc.sb("inv", [P, G])
        T = sc.ps("T", [P, GT])
        U = [sc.ps(f"U{i}", [P, GT]) for i in range(3)]
        OUT = [sc.ps(f"OUT{i}", [P, G, D]) for i in range(2)]
        SS = sc.ps("SS", [P, 512])
        xn_ready, xn_used, xt_ready, up_mm, gelu, sq_done, ss_mm, ms_ready, rms_ready, inv_ready, down_mm, added, half_ready = (
            sc.sem(n) for n in "xn_ready xn_used xt_ready up_mm gelu sq_done ss_mm ms_ready rms_ready inv_ready down_mm added half_ready".split())
        block = ctx.enter_context(nc.Block())

        @block.vector
        def _(v):
            nc.vector.memset(half[:], 0.5).then_inc(half_ready, 1)

            def step(g, k, on):
                if on(2):
                    wait(v, xn_used, g + 1)
                    normed(nc, v, res, xn[k], g + 2, res["rstd2"], xn_ready)
                if on(0):
                    wait(v, ss_mm, g + 1)
                    nc.vector.tensor_scalar(ms[:], SS[:, 0:G], 1.0 / (C * P), None, ALU.mult).then_inc(ms_ready, 1)
                    wait(v, rms_ready, g + 1)
                    nc.vector.tensor_scalar(ms[:], rms[:], 1e-8, None, ALU.add).then_inc(inv_ready, 1)
                    wait(v, inv_ready, 2 * g + 1)
                    nc.vector.reciprocal(inv[:], ms[:]).then_inc(inv_ready, 1)
                    wait(v, inv_ready, 2 * g + 2)
                    wait(v, down_mm, g + 1)
                    for t in range(G):
                        xs = x[:, G * g + t]
                        nc.vector.scalar_tensor_tensor(out=xs, in0=OUT[k][:, t], scalar=inv[:, t:t + 1], in1=xs,
                                                       op0=ALU.mult, op1=ALU.add).then_inc(added, 1)
                    wait(v, added, G * (g + 1))
                    row_stats(nc, res, g)

            pipeline(v, step, GROUPS, 2)

        @block.gpsimd
        def _(q):
            q.wait_ge(half_ready, 1)

            def step(g, k, on):
                if on(1):
                    wait(q, ss_mm, g)
                    for c in range(C):
                        h = hT[(k + 1) % 2][:, c]
                        wait(q, gelu, C * (g + 1) + c + 1)
                        nc.gpsimd.tensor_tensor(sq[(k + 1) % 2][:, c], h, h, ALU.mult).then_inc(sq_done, 1)
                if on(0):
                    wait(q, ms_ready, g + 1)
                    nc.gpsimd.tensor_tensor(rms[:], ms[:], half[:], ALU.pow).then_inc(rms_ready, 1)

            pipeline(q, step, GROUPS, 2)

        @block.scalar
        def _(act):
            def step(g, k, on):
                if on(2):
                    wait(act, xn_used, g + 3)
                    wait(act, up_mm, C * (g + 1))
                    nc.scalar.activation(xnT[k][:], T[:], ACT.Copy).then_inc(xt_ready, 1)
                if on(1):
                    wait(act, sq_done, C * g)
                    wait(act, down_mm, g)
                    for c in range(C):
                        n = C * (g + 1) + c
                        wait(act, up_mm, n + 1)
                        nc.scalar.activation(hT[(k + 1) % 2][:, c], U[(C * (k + 1) + c) % 2][:],
                                             ACT.Gelu).then_inc(gelu, 1)

            pipeline(act, step, GROUPS, 2)

        @block.tensor
        def _(pe):
            def step(g, k, on):
                if on(2):
                    wait(pe, xn_ready, G * (g + 3))
                    wait(pe, xt_ready, g + 2)
                    for t in range(G):
                        last = nc.tensor.transpose(T[:, t * P:t * P + P], xn[k][:, t], ident[:])
                    last.then_inc(xn_used, 1)
                if on(1):
                    wait(pe, xt_ready, g + 2)
                    for c in range(C):
                        n = C * (g + 1) + c
                        wait(pe, gelu, n - 1)
                        nc.tensor.matmul(U[(C * (k + 1) + c) % 2][:], wu[:, c], xnT[(k + 1) % 2][:],
                                         start=True, stop=True).then_inc(up_mm, 1)
                if on(0):
                    wait(pe, sq_done, C * (g + 1))
                    wait(pe, ms_ready, g)
                    for t in range(G):
                        for c in range(C):
                            last = nc.tensor.matmul(SS[:, t:t + 1], sq[k][:, c, t * P:t * P + P], res["ones"][:, 0:1],
                                                    start=(c == 0), stop=(c == C - 1))
                    last.then_inc(ss_mm, 1)
                    wait(pe, added, G * (g - 1))
                    for t in range(G):
                        for c in range(C):
                            last = nc.tensor.matmul(OUT[k][:, t], hT[k][:, c, t * P:t * P + P], wd[:, c],
                                                    start=(c == 0), stop=(c == C - 1))
                    last.then_inc(down_mm, 1)

            pipeline(pe, step, GROUPS, 2)


def quantize(nc, res, name, w, wu, wd):
    with ExitStack() as ctx:
        tmp = Scope(nc, ctx, name + "q")
        ab = tmp.sb("ab", [P, 512])
        total, thr = tmp.sb("total", [P, 2]), tmp.sb("thr", [P, 2, 2])
        above, below = tmp.sb("above", [P, 2, 512]), tmp.sb("below", [P, 2, 512])
        TT = tmp.ps("TT", [P, 512])
        loaded, summed, spread, seq = (tmp.sem(n) for n in "loaded summed spread seq".split())
        block = ctx.enter_context(nc.Block())
        both = (wu, wd)

        @block.sync
        def _(sp):
            sp.dma_start(wu[:], w["up"]).then_inc(loaded, 16)
            sp.dma_start(wd[:], w["down"]).then_inc(loaded, 16)

        @block.scalar
        def _(act):
            act.wait_ge(loaded, 32)
            for i in range(2):
                nc.scalar.activation(ab[:], both[i][:].rearrange("p c n -> p (c n)"), ACT.Abs,
                                     accum_out=total[:, i:i + 1]).then_inc(summed, 1)
                act.wait_ge(summed, i + 1)

        @block.tensor
        def _(pe):
            pe.wait_ge(summed, 2)
            nc.tensor.matmul(TT[:, 0:2], res["ones"][:], total[:], start=True, stop=True).then_inc(spread, 1)

        @block.vector
        def _(v):
            n = 0
            v.wait_ge(spread, 1)
            for sgn in range(2):
                nc.vector.tensor_scalar(thr[:, sgn], TT[:, 0:2], (0.5 - sgn) / (P * 512), None, ALU.mult).then_inc(seq, 1)
                n += 1
            v.wait_ge(seq, n)
            for i in range(2):
                wf = both[i][:].rearrange("p c n -> p (c n)")
                nc.vector.tensor_scalar(above[:, i], wf, thr[:, 0, i:i + 1], None, ALU.is_gt).then_inc(seq, 1)
                nc.vector.tensor_scalar(below[:, i], wf, thr[:, 1, i:i + 1], None, ALU.is_lt).then_inc(seq, 1)
            v.wait_ge(seq, n + 4)
            nc.vector.tensor_tensor(above[:], above[:], below[:], ALU.subtract).then_inc(seq, 1)
            v.wait_ge(seq, n + 5)
            for i in range(2):
                wf = both[i][:].rearrange("p c n -> p (c n)")
                nc.vector.tensor_tensor(below[:, i], above[:, i], wf, ALU.subtract).then_inc(seq, 1)
            v.wait_ge(seq, n + 7)
            for i in range(2):
                wf = both[i][:].rearrange("p c n -> p (c n)")
                nc.vector.tensor_tensor(wf, wf, below[:, i], ALU.add)


def lowrank_ffn(nc, res, name, w):
    x, ident = res["x"], res["ident"]
    C, R = 4, 32
    norm_factors(nc, res, name + "n")
    with ExitStack() as ctx:
        sc = Scope(nc, ctx, name)
        u1 = sc.sb("u1", [P, P])
        v1 = sc.sb("v1", [P, C * P])
        u2 = sc.sb("u2", [P, C, P])
        v2 = sc.sb("v2", [P, P])
        b1 = sc.sb("b1", [P, C])
        b2 = sc.sb("b2", [1, P])
        xn = [sc.sb(f"xn{i}", [P, G, D]) for i in range(2)]
        xnT = sc.sb("xnT", [P, GT])
        pT, qT = sc.sb("pT", [P, GT]), sc.sb("qT", [P, GT])
        hT = [sc.sb(f"hT{i}", [P, C, GT]) for i in range(2)]
        T = sc.ps("T", [P, GT])
        PP, QQ = sc.ps("PP", [P, GT]), sc.ps("QQ", [P, GT])
        U = [sc.ps(f"U{i}", [P, GT]) for i in range(3)]
        OUT = sc.ps("OUT", [P, G, D])
        loaded, xn_ready, xn_used, xt_ready, p_mm, p_ready, up_mm, gelu, q_mm, q_ready, out_mm, added = (
            sc.sem(n) for n in "loaded xn_ready xn_used xt_ready p_mm p_ready up_mm gelu q_mm q_ready out_mm added".split())
        block = ctx.enter_context(nc.Block())
        loads = [(u1, "u1"), (v1, "v1"), (u2, "u2"), (v2, "v2"), (b1, "b1"), (b2, "b2")]

        @block.sync
        def _(sp):
            for dst, n in loads:
                sp.dma_start(dst[:], w[n]).then_inc(loaded, 16)

        @block.vector
        def _(v):
            def step(g, k, on):
                if on(2):
                    wait(v, xn_used, g + 1)
                    normed(nc, v, res, xn[k], g + 2, res["rstd"], xn_ready)
                if on(1):
                    wait(v, p_mm, g + 2)
                    wait(v, up_mm, C * (g + 1))
                    nc.vector.tensor_copy(pT[:], PP[:]).then_inc(p_ready, 1)
                if on(0):
                    wait(v, q_mm, g + 1)
                    wait(v, out_mm, g)
                    nc.vector.tensor_copy(qT[:], QQ[:]).then_inc(q_ready, 1)
                    wait(v, out_mm, g + 1)
                    xs = x[:, bass.ds(G * g, G), :]
                    nc.vector.tensor_tensor(xs, xs, OUT[:], ALU.add).then_inc(added, 1)

            pipeline(v, step, GROUPS, 2)

        @block.scalar
        def _(act):
            act.wait_ge(loaded, 16 * len(loads))

            def step(g, k, on):
                if on(2):
                    wait(act, xn_used, g + 3)
                    wait(act, p_mm, g + 2)
                    nc.scalar.activation(xnT[:], T[:], ACT.Copy).then_inc(xt_ready, 1)
                if on(1):
                    wait(act, q_mm, g)
                    for c in range(C):
                        n = C * (g + 1) + c
                        wait(act, up_mm, n + 1)
                        nc.scalar.activation(hT[(k + 1) % 2][:, c], U[c % 2][:], ACT.Gelu_apprx_tanh,
                                             bias=b1[:, c:c + 1]).then_inc(gelu, 1)

            pipeline(act, step, GROUPS, 2)

        @block.tensor
        def _(pe):
            pe.wait_ge(loaded, 16 * len(loads))

            def step(g, k, on):
                if on(1):
                    wait(pe, xt_ready, g + 2)
                    wait(pe, p_ready, g + 1)
                    nc.tensor.matmul(PP[:], u1[:], xnT[:], start=True, stop=True).then_inc(p_mm, 1)
                if on(2):
                    wait(pe, xn_ready, G * (g + 3))
                    wait(pe, xt_ready, g + 2)
                    for t in range(G):
                        last = nc.tensor.transpose(T[:, t * P:t * P + P], xn[k][:, t], ident[:])
                    last.then_inc(xn_used, 1)
                if on(0):
                    wait(pe, gelu, C * (g + 1))
                    wait(pe, q_ready, g)
                    for c in range(C):
                        last = nc.tensor.matmul(QQ[:], u2[:, c], hT[k][:, c], start=(c == 0), stop=(c == C - 1))
                    last.then_inc(q_mm, 1)
                if on(1):
                    wait(pe, p_ready, g + 2)
                    for c in range(C):
                        n = C * (g + 1) + c
                        wait(pe, gelu, n - 1)
                        nc.tensor.matmul(U[c % 2][:], v1[:, c * P:c * P + P], pT[:],
                                         start=True, stop=True).then_inc(up_mm, 1)
                if on(0):
                    wait(pe, q_ready, g + 1)
                    wait(pe, added, g)
                    for t in range(G):
                        nc.tensor.matmul(OUT[:, t], qT[:, t * P:t * P + P], v2[:], start=True, stop=False)
                        last = nc.tensor.matmul(OUT[:, t], res["ones"][0:1, :], b2[:], start=False, stop=True)
                    last.then_inc(out_mm, 1)

            pipeline(pe, step, GROUPS, 2)



def min_gru(nc, res, name, w):
    x, ident = res["x"], res["ident"]
    NB = GT // S
    norm_factors(nc, res, name + "n")
    with ExitStack() as ctx:
        sc = Scope(nc, ctx, name)
        wz, wh = sc.sb("wz", [P, P]), sc.sb("wh", [P, P])
        bz, bh, swish = sc.sb("bz", [P, 1]), sc.sb("bh", [P, 1]), sc.sb("swish", [P, 1])
        nbz = sc.sb("nbz", [P, 1])
        gamma, beta = sc.sb("gamma", [P, G, P]), sc.sb("beta", [P, G, P])
        xn = [sc.sb(f"xn{i}", [P, G, D]) for i in range(2)]
        xnT = sc.sb("xnT", [P, GT])
        keep, gate = sc.sb("keep", [P, GT]), sc.sb("gate", [P, GT])
        new, h, sg = sc.sb("new", [P, GT]), sc.sb("h", [P, GT]), sc.sb("sg", [P, GT])
        yT = [sc.sb(f"yT{i}", [P, GT]) for i in range(2)]
        st, mv = sc.sb("st", [P, G, 6]), sc.sb("mv", [P, G, 2])
        ve, root, power = sc.sb("ve", [P, G]), sc.sb("root", [P, G]), sc.sb("power", [P, G])
        yn, yg = sc.sb("yn", [P, G, P]), sc.sb("yg", [P, G, P])
        T, Z, HH = sc.ps("T", [P, GT]), sc.ps("Z", [P, GT]), sc.ps("HH", [P, GT])
        Y = [sc.ps(f"Y{i}", [P, G, P]) for i in range(2)]
        names = "loaded nb xn_ready xn_used xt_ready z_mm h_mm gates seq y_ready turned vseq ve_ready root_ready yn_ready yg_ready added".split()
        (loaded, nb, xn_ready, xn_used, xt_ready, z_mm, h_mm, gates, seq, y_ready, turned, vseq, ve_ready, root_ready,
         yn_ready, yg_ready, added) = (sc.sem(n) for n in names)
        block = ctx.enter_context(nc.Block())
        loads = [(wz, "wz"), (wh, "wh"), (bz, "bz"), (bh, "bh"), (swish, "swish"), (gamma, "gamma"), (beta, "beta")]

        @block.sync
        def _(sp):
            for dst, n in loads:
                sp.dma_start(dst[:], w[n]).then_inc(loaded, 16)

        @block.scalar
        def _(act):
            act.wait_ge(nb, 2)

            def step(g, k, on):
                if on(2):
                    wait(act, xn_used, g + 3)
                    wait(act, h_mm, g + 2)
                    nc.scalar.activation(xnT[:], T[:], ACT.Copy).then_inc(xt_ready, 1)
                if on(1):
                    wait(act, z_mm, g + 2)
                    wait(act, y_ready, g + 1)
                    nc.scalar.activation(keep[:], Z[:], ACT.Sigmoid, bias=nbz[:], scale=-1.0).then_inc(gates, 1)
                    nc.scalar.activation(gate[:], Z[:], ACT.Sigmoid, bias=bz[:]).then_inc(gates, 1)
                    wait(act, seq, 3 * (g + 1) + 3)
                    nc.scalar.activation(sg[:], h[:], ACT.Sigmoid, scale=swish[:]).then_inc(gates, 1)

            pipeline(act, step, GROUPS, 2)

        @block.gpsimd
        def _(q):
            q.wait_ge(nb, 2)

            def step(g, k, on):
                if on(0):
                    wait(q, ve_ready, g + 1)
                    nc.gpsimd.tensor_tensor(root[:], ve[:], power[:], ALU.pow).then_inc(root_ready, 1)
                    wait(q, yn_ready, G * (g + 1))
                    nc.gpsimd.tensor_tensor(yg[:], yn[:], gamma[:], ALU.mult).then_inc(yg_ready, 1)
                    wait(q, yg_ready, 2 * g + 1)
                    nc.gpsimd.tensor_tensor(yg[:], yg[:], beta[:], ALU.add).then_inc(yg_ready, 1)

            pipeline(q, step, GROUPS, 2)

        @block.vector
        def _(v):
            nc.vector.memset(power[:], -0.5).then_inc(nb, 1)
            v.wait_ge(loaded, 16 * len(loads))
            nc.vector.tensor_scalar(nbz[:], bz[:], -1.0, None, ALU.mult).then_inc(nb, 1)
            v.wait_ge(nb, 2)

            def step(g, k, on):
                if on(2):
                    wait(v, xn_used, g + 1)
                    normed(nc, v, res, xn[k], g + 2, res["rstd"], xn_ready)
                if on(0):
                    wait(v, turned, g + 1)
                    for t in range(G):
                        nc.vector.bn_stats(st[:, t], Y[k][:, t]).then_inc(vseq, 1)
                    wait(v, vseq, 2 * G * g + G)
                    nc.vector.memset(ve[:], 0.0)
                    for t in range(G):
                        nc.vector.bn_aggr(mv[:, t], st[:, t]).then_inc(vseq, 1)
                    wait(v, vseq, 2 * G * (g + 1))
                    nc.vector.tensor_scalar(ve[:], mv[:, :, 1], EPS, None, ALU.add).then_inc(ve_ready, 1)
                if on(1):
                    n = 3 * (g + 1)
                    wait(v, gates, n + 2)
                    nc.vector.memset(keep[:].rearrange("p (b s) -> p b s", b=NB)[:, :, 0:1], 0.0).then_inc(seq, 1)
                    wait(v, h_mm, g + 2)
                    nc.vector.scalar_tensor_tensor(out=new[:], in0=HH[:], scalar=bh[:], in1=gate[:],
                                                   op0=ALU.add, op1=ALU.mult).then_inc(seq, 1)
                    wait(v, seq, n + 2)
                    nc.vector.tensor_tensor_scan(h[:], keep[:], new[:], 0.0, ALU.mult, ALU.add).then_inc(seq, 1)
                if on(0):
                    wait(v, root_ready, g + 1)
                    wait(v, yg_ready, 2 * g)
                    for t in range(G):
                        nc.vector.tensor_scalar(yn[:, t], Y[k][:, t], mv[:, t, 0:1], root[:, t:t + 1],
                                                ALU.subtract, ALU.mult).then_inc(yn_ready, 1)
                if on(1):
                    wait(v, gates, 3 * (g + 1) + 3)
                    wait(v, turned, g)
                    nc.vector.scalar_tensor_tensor(out=yT[(k + 1) % 2][:], in0=h[:], scalar=swish[:], in1=sg[:],
                                                   op0=ALU.mult, op1=ALU.mult).then_inc(y_ready, 1)
                if on(0):
                    wait(v, yg_ready, 2 * g + 2)
                    xs = x[:, bass.ds(G * g, G), :]
                    nc.vector.tensor_tensor(xs, xs, yg[:], ALU.add).then_inc(added, 1)
                    wait(v, added, g + 1)
                    row_stats(nc, res, g)

            pipeline(v, step, GROUPS, 2)

        @block.tensor
        def _(pe):
            pe.wait_ge(loaded, 16 * len(loads))

            def step(g, k, on):
                if on(1):
                    wait(pe, xt_ready, g + 2)
                    wait(pe, gates, 3 * (g + 1))
                    nc.tensor.matmul(Z[:], wz[:], xnT[:], start=True, stop=True).then_inc(z_mm, 1)
                    wait(pe, seq, 3 * (g + 1))
                    nc.tensor.matmul(HH[:], wh[:], xnT[:], start=True, stop=True).then_inc(h_mm, 1)
                if on(2):
                    wait(pe, xn_ready, G * (g + 3))
                    wait(pe, xt_ready, g + 2)
                    for t in range(G):
                        last = nc.tensor.transpose(T[:, t * P:t * P + P], xn[k][:, t], ident[:])
                    last.then_inc(xn_used, 1)
                if on(1):
                    wait(pe, y_ready, g + 2)
                    wait(pe, yn_ready, G * g)
                    for t in range(G):
                        last = nc.tensor.transpose(Y[(k + 1) % 2][:, t], yT[(k + 1) % 2][:, t * P:t * P + P], ident[:])
                    last.then_inc(turned, 1)

            pipeline(pe, step, GROUPS, 2)


def expert_choice(nc, res, name, w):
    x, ident = res["x"], res["ident"]
    E, C = 8, 4
    K = 2 * TILES * P // E
    norm_factors(nc, res, name + "n")
    with ExitStack() as outer:
        so = Scope(nc, outer, name)
        wts = so.sb("wts", [P, TILES, E])
        w1, w2 = so.sb("w1", [P, E, C * P]), so.sb("w2", [P, E, C, P])
        b1, b2 = so.sb("b1", [P, E, C]), so.sb("b2", [1, E, P])
        big = so.sem("big")
        router_scores(nc, res, so, name, w, wts, E, lambda sp: [
            sp.dma_start(dst[:], w[n]).then_inc(big, 16) for dst, n in ((w1, "w1"), (w2, "w2"), (b1, "b1"), (b2, "b2"))])
        choose(nc, res, name, w, wts, E, K)
        with ExitStack() as ctx:
            sc = Scope(nc, ctx, name + "e")
            xn = sc.sb("xn", [P, G, D])
            xnT = [sc.sb(f"xnT{i}", [P, GT]) for i in range(2)]
            hT = [sc.sb(f"hT{i}", [P, C, GT]) for i in range(2)]
            T = sc.ps("T", [P, GT])
            U = [sc.ps(f"U{i}", [P, GT]) for i in range(3)]
            OUT = [sc.ps(f"OUT{i}", [P, G, D]) for i in range(2)]
            xn_ready, xn_used, xt_ready, up_mm, gelu, down_mm, added = (
                sc.sem(n) for n in "xn_ready xn_used xt_ready up_mm gelu down_mm added".split())
            block = ctx.enter_context(nc.Block())

            @block.vector
            def _(v):
                v.wait_ge(big, 64)

                def norm_group(g):
                    wait(v, xn_used, g)
                    normed(nc, v, res, xn, g, res["rstd"], xn_ready)

                norm_group(0)

                def step(g, j, e, more, nxt):
                    n = g * E + e
                    if e == 2 and more:
                        norm_group(g + 1)
                    wait(v, down_mm, n + 1)
                    wait(v, added, n * G)
                    for t in range(G):
                        xs = x[:, g * G + t]
                        nc.vector.scalar_tensor_tensor(out=xs, in0=OUT[e % 2][:, t],
                                                       scalar=wts[:, g * G + t, e:e + 1], in1=xs,
                                                       op0=ALU.mult, op1=ALU.add).then_inc(added, 1)
                    if e == E - 1:
                        wait(v, added, n * G + G)
                        row_stats(nc, res, g)

                by_group(v, step, GROUPS, E)

            @block.scalar
            def _(act):
                def evac(g, j):
                    wait(act, xn_used, g + 1)
                    wait(act, up_mm, g * (E * C) - E * C)
                    nc.scalar.activation(xnT[j][:], T[:], ACT.Copy).then_inc(xt_ready, 1)

                def gelus(g, e):
                    n = g * E + e
                    wait(act, down_mm, n - 1)
                    for c in range(C):
                        wait(act, up_mm, n * C + (c + 1))
                        nc.scalar.activation(hT[e % 2][:, c], U[c % 2][:], ACT.Gelu,
                                             bias=b1[:, e, c:c + 1]).then_inc(gelu, 1)

                evac(0, 0)
                gelus(0, 0)

                def step(g, j, e, more, nxt):
                    if e == 2 and more:
                        evac(g + 1, 1 - j)
                    if nxt:
                        gelus(nxt[0], nxt[2])

                by_group(act, step, GROUPS, E)

            @block.tensor
            def _(pe):
                def turn(g):
                    wait(pe, xn_ready, g * G + G)
                    wait(pe, xt_ready, g)
                    for t in range(G):
                        last = nc.tensor.transpose(T[:, t * P:t * P + P], xn[:, t], ident[:])
                    last.then_inc(xn_used, 1)

                def up(g, j, e):
                    n = g * E + e
                    if e == 0:
                        wait(pe, xt_ready, g + 1)
                    for c in range(C):
                        wait(pe, gelu, n * C + (c - 1))
                        nc.tensor.matmul(U[c % 2][:], w1[:, e, c * P:c * P + P], xnT[j][:],
                                         start=True, stop=True).then_inc(up_mm, 1)

                turn(0)
                up(0, 0, 0)

                def step(g, j, e, more, nxt):
                    n = g * E + e
                    if e == 2 and more:
                        turn(g + 1)
                    if nxt:
                        up(*nxt)
                    wait(pe, gelu, n * C + C)
                    wait(pe, added, n * G - G)
                    for t in range(G):
                        for c in range(C):
                            nc.tensor.matmul(OUT[e % 2][:, t], hT[e % 2][:, c, t * P:t * P + P], w2[:, e, c],
                                             start=(c == 0), stop=False)
                        last = nc.tensor.matmul(OUT[e % 2][:, t], res["ones"][0:1, :], b2[:, e],
                                                start=False, stop=True)
                    last.then_inc(down_mm, 1)

                by_group(pe, step, GROUPS, E)


def by_group(eng, step, groups, items):
    def group(g, j, more):
        for e in range(items):
            nxt = (g, j, e + 1) if e + 1 < items else (g + 1, 1 - j, 0) if more else None
            step(g, j, e, more, nxt)

    group(0, 0, True)
    group(1, 1, True)
    with eng.Fori(1, groups // 2 - 1) as i:
        group(i * 2, 0, True)
        group(i * 2 + 1, 1, True)
    group(groups - 2, 0, True)
    group(groups - 1, 1, False)


def router_scores(nc, res, so, name, w, wts, E, loads):
    x, ident = res["x"], res["ident"]
    with ExitStack() as ctx:
        sc = Scope(nc, ctx, name + "r")
        wr = sc.sb("wr", [P, E])
        xn = [sc.sb(f"xn{i}", [P, G, D]) for i in range(2)]
        xnT = [sc.sb(f"xnT{i}", [P, GT]) for i in range(2)]
        top, tot = sc.sb("top", [P, TILES]), sc.sb("tot", [P, TILES])
        T = [sc.ps(f"T{i}", [P, GT]) for i in range(2)]
        LG = [sc.ps(f"LG{i}", [P, 512]) for i in range(2)]
        loaded, xn_ready, xn_used, xt_ready, lg_mm, copied, seq, exped = (
            sc.sem(n) for n in "loaded xn_ready xn_used xt_ready lg_mm copied seq exped".split())
        block = ctx.enter_context(nc.Block())

        @block.sync
        def _(sp):
            sp.dma_start(wr[:], w["wr"]).then_inc(loaded, 16)
            loads(sp)

        @block.scalar
        def _(act):
            def step(g, k, on):
                if on(1):
                    wait(act, xn_used, g + 2)
                    wait(act, lg_mm, g)
                    nc.scalar.activation(xnT[(k + 1) % 2][:], T[(k + 1) % 2][:], ACT.Copy).then_inc(xt_ready, 1)

            pipeline(act, step, GROUPS, 2)
            act.wait_ge(seq, 2)
            nc.scalar.activation(wts[:], wts[:], ACT.Exp).then_inc(exped, 1)

        @block.tensor
        def _(pe):
            pe.wait_ge(loaded, 16)

            def step(g, k, on):
                if on(1):
                    wait(pe, xn_ready, G * (g + 2))
                    wait(pe, xt_ready, g)
                    for t in range(G):
                        last = nc.tensor.transpose(T[(k + 1) % 2][:, t * P:t * P + P], xn[(k + 1) % 2][:, t], ident[:])
                    last.then_inc(xn_used, 1)
                if on(0):
                    wait(pe, xt_ready, g + 1)
                    wait(pe, copied, g - 1)
                    for t in range(G):
                        last = nc.tensor.matmul(LG[k][:, t * E:t * E + E], xnT[k][:, t * P:t * P + P], wr[:],
                                                start=True, stop=True)
                    last.then_inc(lg_mm, 1)

            pipeline(pe, step, GROUPS, 2)

        @block.vector
        def _(v):
            def step(g, k, on):
                if on(2):
                    wait(v, xn_used, g + 1)
                    normed(nc, v, res, xn[k], g + 2, res["rstd"], xn_ready)
                if on(0):
                    wait(v, lg_mm, g + 1)
                    nc.vector.tensor_copy(wts[:, bass.ds(g * G, G), :],
                                          LG[k][:, 0:G * E].rearrange("p (t e) -> p t e", t=G)).then_inc(copied, 1)

            pipeline(v, step, GROUPS, 2)
            v.wait_ge(copied, GROUPS)
            shape = [P, TILES, E]
            nc.vector.tensor_reduce(top[:], wts[:], AX.X, ALU.max).then_inc(seq, 1)
            v.wait_ge(seq, 1)
            nc.vector.tensor_tensor(wts[:], wts[:], top[:].unsqueeze(2).to_broadcast(shape), ALU.subtract).then_inc(seq, 1)
            v.wait_ge(exped, 1)
            nc.vector.tensor_reduce(tot[:], wts[:], AX.X, ALU.add).then_inc(seq, 1)
            v.wait_ge(seq, 3)
            nc.vector.reciprocal(top[:], tot[:]).then_inc(seq, 1)
            v.wait_ge(seq, 4)
            nc.vector.tensor_tensor(wts[:], wts[:], top[:].unsqueeze(2).to_broadcast(shape), ALU.mult)


def choose(nc, res, name, w, wts, E, K):
    BL = TILES * E // P
    U32 = mybir.dt.uint32
    with ExitStack() as ctx:
        sc = Scope(nc, ctx, name + "c")
        same, before = sc.sb("same", [P, P]), sc.sb("before", [P, P])
        s, junk, eq, pre = (sc.sb(n, [P, BL, P]) for n in ("s", "junk", "eq", "pre"))
        kth, cand, mask = (sc.sb(n, [P, 1], U32) for n in ("kth", "cand", "mask"))
        cnt, need = sc.sb("cnt", [P, 1]), sc.sb("need", [P, 1])
        ceq, cbef, lim = (sc.sb(n, [P, BL]) for n in ("ceq", "cbef", "lim"))
        TT, CT, BT = sc.ps("TT", [P, BL, P]), sc.ps("CT", [P, 512]), sc.ps("BT", [P, BL, P])
        loaded, turned, seq, counted, total, off_mm, chosen, back = (
            sc.sem(n) for n in "loaded turned seq counted total off_mm chosen back".split())
        block = ctx.enter_context(nc.Block())
        tiles = TILES // BL
        BITS = 30

        @block.sync
        def _(sp):
            sp.dma_start(same[:], w["same"]).then_inc(loaded, 16)
            sp.dma_start(before[:], w["before"]).then_inc(loaded, 16)

        @block.tensor
        def _(pe):
            for j in range(BL):
                last = nc.tensor.transpose(TT[:, j], wts[:, j * tiles:(j + 1) * tiles].rearrange("p t e -> p (t e)"),
                                           res["ident"][:])
            last.then_inc(turned, 1)
            pe.wait_ge(loaded, 32)
            for b in range(BITS + 1):
                pe.wait_ge(counted, b + 1)
                nc.tensor.matmul(CT[:, 0:1], same[:], cnt[:], start=True, stop=True).then_inc(total, 1)
            pe.wait_ge(counted, BITS + 2)
            nc.tensor.matmul(CT[:, 0:BL], before[:], ceq[:], start=True, stop=False)
            nc.tensor.matmul(CT[:, 0:BL], same[:], cbef[:], start=False, stop=True).then_inc(off_mm, 1)
            pe.wait_ge(chosen, 1)
            for j in range(BL):
                last = nc.tensor.transpose(BT[:, j], s[:, j], res["ident"][:])
            last.then_inc(back, 1)

        @block.vector
        def _(v):
            n = [0]

            def then(ins):
                n[0] += 1
                ins.then_inc(seq, 1)
                v.wait_ge(seq, n[0])

            nc.vector.memset(kth[:], 0)
            v.wait_ge(turned, 1)
            then(nc.vector.tensor_copy(s[:], TT[:]))
            for b in range(BITS):
                then(nc.vector.tensor_scalar(cand[:], kth[:], 1 << (BITS - 1 - b), None, ALU.bitwise_or))
                nc.vector.tensor_scalar(junk[:], s[:], cand[:].bitcast(F32), None, ALU.is_ge, ALU.add,
                                        accum_out=cnt[:]).then_inc(counted, 1)
                v.wait_ge(total, b + 1)
                then(nc.vector.tensor_scalar(mask[:], CT[:, 0:1], float(K), None, ALU.is_ge))
                then(nc.vector.copy_predicated(kth[:], mask[:], cand[:]))
            kf = kth[:].bitcast(F32)
            nc.vector.tensor_scalar(junk[:], s[:], kf, None, ALU.is_gt, ALU.add, accum_out=cnt[:]).then_inc(counted, 1)
            v.wait_ge(total, BITS + 1)
            then(nc.vector.tensor_scalar(need[:], CT[:, 0:1], -1.0, float(K), ALU.mult, ALU.add))
            then(nc.vector.tensor_scalar(eq[:], s[:], kf, None, ALU.is_equal))
            for j in range(BL):
                then(nc.vector.tensor_tensor_scan(pre[:, j], res["ones"][:], eq[:, j], 0.0, ALU.mult, ALU.add))
            nc.vector.memset(cbef[:, 0:1], 0.0)
            then(nc.vector.tensor_copy(ceq[:], pre[:, :, P - 1]))
            for j in range(1, BL):
                if j == BL - 1:
                    nc.vector.tensor_tensor(cbef[:, j:j + 1], cbef[:, j - 1:j], ceq[:, j - 1:j], ALU.add)\
                        .then_inc(counted, 1)
                else:
                    then(nc.vector.tensor_tensor(cbef[:, j:j + 1], cbef[:, j - 1:j], ceq[:, j - 1:j], ALU.add))
            v.wait_ge(off_mm, 1)
            then(nc.vector.tensor_scalar(lim[:], CT[:, 0:BL], need[:], -1.0, ALU.subtract, ALU.mult))
            for j in range(BL):
                then(nc.vector.scalar_tensor_tensor(out=pre[:, j], in0=pre[:, j], scalar=lim[:, j:j + 1],
                                                    in1=eq[:, j], op0=ALU.is_le, op1=ALU.mult))
            then(nc.vector.tensor_tensor(pre[:], pre[:], junk[:], ALU.add))
            nc.vector.tensor_tensor(s[:], s[:], pre[:], ALU.mult).then_inc(chosen, 1)
            v.wait_ge(back, 1)
            nc.vector.tensor_copy(wts[:].rearrange("p t e -> p (t e)"), BT[:].rearrange("p j q -> p (j q)"))


def choose_constants():
    r = np.arange(P)
    same = (r[:, None] % 8 == r[None, :] % 8)
    before = same & (r[:, None] < r[None, :])
    return {"same": same.astype(np.float32), "before": before.astype(np.float32)}



def routed_experts(nc, res, name, w):
    x, ident = res["x"], res["ident"]
    E, PAIRS, TOP = 32, 16, 6
    NQ = PAIRS + 1
    norm_factors(nc, res, name + "n")
    with ExitStack() as ctx:
        sc = Scope(nc, ctx, name)
        wg, wu, wd = (sc.sb(n, [P, NQ, P]) for n in ("wg", "wu", "wd"))
        wr, bias, fresh = sc.sb("wr", [P, E]), sc.sb("bias", [P, G, E]), sc.sb("fresh", [P, G, E])
        sel = sc.sb("sel", [3 * E, PAIRS, P], BF16)
        zero = sc.sb("zero", [P, GT], BF16)
        xn = sc.sb("xn", [P, G, D])
        xnT = [sc.sb(f"xnT{i}", [P, GT]) for i in range(2)]
        e, cor, gt, eq, pre = (sc.sb(n, [P, G, E]) for n in ("e", "cor", "gt", "eq", "pre"))
        m8 = sc.sb("m8", [P, G, 8])
        top, tot = sc.sb("top", [P, G]), sc.sb("tot", [P, G])
        comb = sc.sb("comb", [P, G, 3, E])
        cf, cr = sc.sb("cf", [3 * E, GT]), sc.sb("cr", [3 * E, GT])
        c2 = sc.sb("c2", [3 * E, GT], BF16)
        cb = [sc.sb(f"cb{i}", [3 * E, GT], BF16) for i in range(2)]
        sg = [sc.sb(f"sg{i}", [P, GT]) for i in range(2)]
        hm = [sc.sb(f"hm{i}", [P, GT]) for i in range(2)]
        GB = [sc.ps(f"GB{i}", [P, GT]) for i in range(2)]
        UB = [sc.ps(f"UB{i}", [P, GT]) for i in range(2)]
        CB, OUT = sc.ps("CB", [P, GT]), sc.ps("OUT", [P, G, D])
        M0, M1 = sc.ps("M0", [P, GT]), sc.ps("M1", [P, GT])
        names = ("loaded zeroed xn_ready xn_used xt_ready lg_mm rseq exp_in exped comb_ready ct_mm ct_read cseq c_ready "
                 "g_mm u_mm silu mseq mul_done down_mm added").split()
        s = {n: sc.sem(n) for n in names}
        block = ctx.enter_context(nc.Block())
        loads = [(wr, "wr"), (bias, "bias"), (fresh, "fresh"), (sel, "sel"), (wg, "wg"), (wu, "wu"), (wd, "wd")]
        NR = 16

        @block.sync
        def _(sp):
            for dst, n in loads:
                sp.dma_start(dst[:], w[n]).then_inc(s["loaded"], 16)

        @block.vector
        def _(v):
            nc.vector.memset(zero[:], 0.0).then_inc(s["zeroed"], 1)
            v.wait_ge(s["loaded"], 16 * len(loads))
            wide = [P, G, E]
            count = [0]

            def then(b, ins):
                count[0] += 1
                ins.then_inc(s["rseq"], 1)
                wait(v, s["rseq"], b * NR + count[0])

            def norm_group(b):
                wait(v, s["xn_used"], b)
                normed(nc, v, res, xn, b, res["rstd"], s["xn_ready"])

            def router_a(b):
                count[0] = 0
                wait(v, s["lg_mm"], b + 1)
                lg = M1[:, 0:G * E].rearrange("p (t e) -> p t e", t=G)
                then(b, nc.vector.tensor_reduce(top[:], lg, AX.X, ALU.max))
                nc.vector.tensor_tensor(e[:], lg, top[:].unsqueeze(2).to_broadcast(wide), ALU.subtract)\
                    .then_inc(s["exp_in"], 1)

            def router_b(b):
                wait(v, s["exped"], b + 1)
                then(b, nc.vector.tensor_reduce(tot[:], e[:], AX.X, ALU.add))
                then(b, nc.vector.reciprocal(top[:], tot[:]))
                then(b, nc.vector.tensor_tensor(e[:], e[:], top[:].unsqueeze(2).to_broadcast(wide), ALU.mult))
                then(b, nc.vector.tensor_tensor(cor[:], e[:], bias[:], ALU.add))
                nc.vector.memset(pre[:, :, 0:1], 0.0)
                for t in range(G):
                    ins = nc.vector.max(m8[:, t], cor[:, t])
                then(b, ins)

            def router_c(b):
                sixth = m8[:, :, TOP - 1:TOP].to_broadcast(wide)
                nc.vector.tensor_tensor(eq[:], cor[:], sixth, ALU.is_equal)
                then(b, nc.vector.tensor_tensor(gt[:], cor[:], sixth, ALU.is_gt))
                then(b, nc.vector.tensor_reduce(tot[:], gt[:], AX.X, ALU.add))
                then(b, nc.vector.tensor_tensor_scan(pre[:].rearrange("p t e -> p (t e)"),
                                                     fresh[:].rearrange("p t e -> p (t e)"),
                                                     eq[:].rearrange("p t e -> p (t e)"), 0.0, ALU.mult, ALU.add))
                then(b, nc.vector.tensor_tensor(pre[:], pre[:], tot[:].unsqueeze(2).to_broadcast(wide), ALU.add))
                then(b, nc.vector.scalar_tensor_tensor(out=pre[:], in0=pre[:], scalar=float(TOP), in1=eq[:],
                                                       op0=ALU.is_le, op1=ALU.mult))
                then(b, nc.vector.tensor_tensor(gt[:], gt[:], pre[:], ALU.add))
                then(b, nc.vector.tensor_tensor(gt[:], gt[:], e[:], ALU.mult))

            def router_d(b):
                then(b, nc.vector.tensor_reduce(tot[:], gt[:], AX.X, ALU.add))
                then(b, nc.vector.tensor_scalar(tot[:], tot[:], 1e-12, None, ALU.max))
                then(b, nc.vector.reciprocal(top[:], tot[:]))
                assert count[0] == NR, count[0]
                wait(v, s["ct_mm"], b)
                for i in range(3):
                    nc.vector.tensor_tensor(comb[:, :, i], gt[:], top[:].unsqueeze(2).to_broadcast(wide),
                                            ALU.mult).then_inc(s["comb_ready"], 1)

            norm_group(0)
            for part in (router_a, router_b, router_c, router_d):
                part(0)

            def step(g, j, q, more, nxt):
                n, k = g * NQ + q, (j + q) % 2
                if more:
                    if q == 0:
                        norm_group(g + 1)
                    if q in (4, 6, 8, 10):
                        (router_a, router_b, router_c, router_d)[q // 2 - 2](g + 1)
                wait(v, s["silu"], n + 1)
                wait(v, s["u_mm"], n + 1)
                wait(v, s["down_mm"], n - 1)
                if q < PAIRS:
                    nc.vector.tensor_tensor(sg[k][:], sg[k][:], UB[k][:], ALU.mult).then_inc(s["mseq"], 1)
                    wait(v, s["mseq"], g * PAIRS + (q + 1))
                    nc.vector.tensor_tensor(hm[k][:], sg[k][:], CB[:], ALU.mult).then_inc(s["mul_done"], 1)
                else:
                    nc.vector.tensor_tensor(hm[k][:], sg[k][:], UB[k][:], ALU.mult).then_inc(s["mul_done"], 1)
                    wait(v, s["down_mm"], n + 1)
                    xs = x[:, bass.ds(g * G, G), :]
                    nc.vector.tensor_tensor(xs, xs, OUT[:], ALU.add).then_inc(s["added"], 1)
                    wait(v, s["added"], g + 1)
                    row_stats(nc, res, g)

            by_group(v, step, GROUPS, NQ)

        @block.gpsimd
        def _(pool):
            def split(b, j):
                wait(pool, s["ct_read"], 2 * b + 2)
                wait(pool, s["down_mm"], b * NQ - NQ)
                lo, hi = slice(E, 2 * E), slice(2 * E, 3 * E)
                c1 = cb[j]
                nc.gpsimd.tensor_tensor(cr[hi], cf[hi], c1[hi], ALU.subtract).then_inc(s["cseq"], 1)
                nc.gpsimd.tensor_tensor(c2[hi], cf[hi], c1[hi], ALU.subtract).then_inc(s["cseq"], 1)
                wait(pool, s["cseq"], 2 * b + 2)
                nc.gpsimd.tensor_tensor(c1[hi], cr[hi], c2[hi], ALU.subtract).then_inc(s["c_ready"], 1)
                nc.gpsimd.tensor_tensor(c1[lo], cf[lo], c1[lo], ALU.subtract).then_inc(s["c_ready"], 1)

            split(0, 0)

            def step(g, j, q, more, nxt):
                if q == 12 and more:
                    split(g + 1, 1 - j)

            by_group(pool, step, GROUPS, NQ)

        @block.scalar
        def _(act):
            def evac(b, j):
                wait(act, s["xn_used"], b + 1)
                wait(act, s["u_mm"], b * NQ - NQ)
                nc.scalar.activation(xnT[j][:], M0[:], ACT.Copy).then_inc(s["xt_ready"], 1)

            def exps(b):
                wait(act, s["exp_in"], b + 1)
                nc.scalar.activation(e[:], e[:], ACT.Exp).then_inc(s["exped"], 1)

            def weights(b, j):
                wait(act, s["ct_mm"], b + 1)
                wait(act, s["c_ready"], 2 * b)
                wait(act, s["u_mm"], b * NQ - NQ)
                nc.scalar.activation(cf[:], M0[0:3 * E, :], ACT.Copy).then_inc(s["ct_read"], 1)
                nc.scalar.activation(cb[j][:], M0[0:3 * E, :], ACT.Copy).then_inc(s["ct_read"], 1)

            def silus(g, j, q):
                n, k = g * NQ + q, (j + q) % 2
                wait(act, s["g_mm"], n + 1)
                wait(act, s["mul_done"], n - 1)
                nc.scalar.activation(sg[k][:], GB[k][:], ACT.Silu).then_inc(s["silu"], 1)

            evac(0, 0)
            exps(0)
            weights(0, 0)
            silus(0, 0, 0)

            def step(g, j, q, more, nxt):
                if more:
                    if q == 1:
                        evac(g + 1, 1 - j)
                    if q == 5:
                        exps(g + 1)
                    if q == 11:
                        weights(g + 1, 1 - j)
                if nxt:
                    silus(*nxt)

            by_group(act, step, GROUPS, NQ)

        @block.tensor
        def _(pe):
            pe.wait_ge(s["loaded"], 16 * len(loads))
            pe.wait_ge(s["zeroed"], 1)

            def turn(b):
                wait(pe, s["xn_ready"], b * G + G)
                wait(pe, s["ct_read"], 2 * b)
                for t in range(G):
                    last = nc.tensor.transpose(M0[:, t * P:t * P + P], xn[:, t], ident[:])
                last.then_inc(s["xn_used"], 1)

            def logits(b, j):
                wait(pe, s["xt_ready"], b + 1)
                for t in range(G):
                    last = nc.tensor.matmul(M1[:, t * E:t * E + E], xnT[j][:, t * P:t * P + P], wr[:],
                                            start=True, stop=True)
                last.then_inc(s["lg_mm"], 1)

            def turn_weights(b):
                wait(pe, s["comb_ready"], 3 * b + 3)
                wait(pe, s["xt_ready"], b + 1)
                for t in range(G):
                    last = nc.tensor.transpose(M0[0:3 * E, t * P:t * P + P],
                                               comb[:, t].rearrange("p i e -> p (i e)"), ident[:])
                last.then_inc(s["ct_mm"], 1)

            def up(g, j, q):
                n, k = g * NQ + q, (j + q) % 2
                wait(pe, s["silu"], n - 1)
                nc.tensor.matmul(GB[k][:], wg[:, q], xnT[j][:], start=True, stop=True).then_inc(s["g_mm"], 1)
                wait(pe, s["mul_done"], n - 1)
                last = nc.tensor.matmul(UB[k][:], wu[:, q], xnT[j][:], start=True, stop=True)
                if q < PAIRS:
                    if q == 0:
                        wait(pe, s["c_ready"], 2 * g + 2)
                    wait(pe, s["mul_done"], n)
                    last = nc.tensor.matmul(CB[:], sel[:, q], cb[j][:], start=True, stop=True)
                last.then_inc(s["u_mm"], 1)

            turn(0)
            logits(0, 0)
            turn_weights(0)
            up(0, 0, 0)

            def step(g, j, q, more, nxt):
                n, k = g * NQ + q, (j + q) % 2
                if more:
                    if q == 1:
                        turn(g + 1)
                    if q == 3:
                        logits(g + 1, 1 - j)
                    if q == 11:
                        turn_weights(g + 1)
                if nxt:
                    up(*nxt)
                if q == 0:
                    wait(pe, s["added"], g)
                    nc.tensor.matmul(OUT[:].rearrange("p t d -> p (t d)"), zero[:, 0:P], zero[:], start=True, stop=False)
                wait(pe, s["mul_done"], n + 1)
                for t in range(G):
                    last = nc.tensor.matmul(OUT[:, t], hm[k][:, t * P:t * P + P], wd[:, q], start=False,
                                            stop=(q == NQ - 1 and t == G - 1))
                last.then_inc(s["down_mm"], 1)

            by_group(pe, step, GROUPS, NQ)


def routed_constants():
    sel = np.zeros((96, 16, P), HOST_BF16)
    for r in range(96):
        q, half = (r % 32) // 2, (r % 32) % 2
        sel[r, q, 64 * half:64 * half + 64] = 1.0
    fresh = np.ones((P, G, 32), np.float32)
    fresh[:, :, 0] = 0.0
    return {"sel": sel, "fresh": fresh}


def state_space(nc, res, name, w):
    x, ident = res["x"], res["ident"]
    NB, N, CH = GT // S, 16, 2
    norm_factors(nc, res, name + "n", then="norm")
    with ExitStack() as ctx:
        sc = Scope(nc, ctx, name)
        win, cw, wk = sc.sb("win", [P, 4, P]), sc.sb("cw", [P, 4, CH * P]), sc.sb("wk", [P, 4, CH * P])
        wdl, wbc, wdt, wout = (sc.sb(n, [P, CH, P]) for n in ("wdl", "wbc", "wdt", "wout"))
        cbias, bdt, dpar = (sc.sb(n, [P, CH]) for n in ("cbias", "bdt", "dpar"))
        lnw, lnb = sc.sb("lnw", [P, 1]), sc.sb("lnb", [P, 1])
        la, A = sc.sb("la", [P, CH, N]), sc.sb("A", [P, CH, N])
        sel = sc.sb("sel", [P, 2 * N, P], BF16)
        PADW = S + 3
        xn = sc.sb("xn", [P, G, D])
        xnp = sc.sb("xnp", [P, NB, PADW])
        u = [sc.sb(f"u{i}", [P, CH, GT]) for i in range(2)]
        sz = [sc.sb(f"sz{i}", [P, CH, GT]) for i in range(2)]
        dtA = [sc.sb(f"dtA{i}", [P, CH, GT]) for i in range(2)]
        dtu = [sc.sb(f"dtu{i}", [P, CH, GT]) for i in range(2)]
        et = sc.sb("et", [P, CH, GT])
        dtl, bf, br = sc.sb("dtl", [P, GT]), sc.sb("bf", [P, GT]), sc.sb("br", [P, GT])
        b2 = sc.sb("b2", [P, GT], BF16)
        bc = [sc.sb(f"bc{i}", [P, GT], BF16) for i in range(2)]
        dA = [[sc.sb(f"dA{i}{c}", [P, GT]) for c in range(CH)] for i in range(2)]
        inp = [sc.sb(f"inp{c}", [P, GT]) for c in range(CH)]
        h = [sc.sb(f"h{c}", [P, GT]) for c in range(CH)]
        hc = [[sc.sb(f"hc{i}{c}", [P, GT]) for c in range(CH)] for i in range(2)]
        yy = sc.sb("yy", [P, CH, GT])
        tmp = sc.sb("tmp", [P, G, D])
        Y = [sc.ps(f"Y{c}", [P, GT]) for c in range(CH)]
        BB = [sc.ps(f"BB{i}", [P, GT]) for i in range(2)]
        CC = [sc.ps(f"CC{i}", [P, GT]) for i in range(2)]
        M = [sc.ps(f"M{i}", [P, GT]) for i in range(2)]
        names = ("loaded set_up seta xn_ready f_mm m_read pseq bc_ready fseq ln_done dt_ready bb_mm cc_mm "
                 "dA_done mulB scanned mulC y_mm y_read yseq y_ready out_mm oseq").split()
        s = {n: sc.sem(n) for n in names}
        block = ctx.enter_context(nc.Block())
        loads = [(win, "win"), (cw, "cw"), (wdl, "wdl"), (wbc, "wbc"), (wdt, "wdt"), (wout, "wout"), (cbias, "cbias"),
                 (bdt, "bdt"), (dpar, "dpar"), (lnw, "lnw"), (lnb, "lnb"), (la, "la"), (sel, "sel")]
        U = 9
        W2 = CH * N

        @block.sync
        def _(sp):
            for dst, n in loads:
                sp.dma_start(dst[:], w[n]).then_inc(s["loaded"], 16)

        @block.gpsimd
        def _(pool):
            def split(b, j):
                wait(pool, s["m_read"], U * b + 7)
                lo, hi = slice(32, 64), slice(64, 96)
                nc.gpsimd.tensor_tensor(br[hi], bf[hi], bc[j][hi], ALU.subtract).then_inc(s["pseq"], 1)
                nc.gpsimd.tensor_tensor(b2[hi], bf[hi], bc[j][hi], ALU.subtract).then_inc(s["pseq"], 1)
                wait(pool, s["pseq"], 2 * b + 2)
                nc.gpsimd.tensor_tensor(bc[j][hi], br[hi], b2[hi], ALU.subtract).then_inc(s["bc_ready"], 1)
                nc.gpsimd.tensor_tensor(bc[j][lo], bf[lo], bc[j][lo], ALU.subtract).then_inc(s["bc_ready"], 1)

            def step(g, k, on):
                if on(1):
                    split(g + 1, (k + 1) % 2)

            pipeline(pool, step, GROUPS, 1)

        @block.scalar
        def _(act):
            act.wait_ge(s["loaded"], 16 * len(loads))
            nc.scalar.activation(A[:], la[:], ACT.Exp).then_inc(s["seta"], 1)
            act.wait_ge(s["set_up"], 3)

            def front(g, k, n):
                b, j = g + 1, (k + 1) % 2
                if n == 1:
                    wait(act, s["f_mm"], U * b + 1)
                    nc.scalar.activation(xnp[:, :, 3:PADW], M[0][:].rearrange("p (b s) -> p b s", b=NB), ACT.Identity,
                                         bias=lnb[:], scale=lnw[:]).then_inc(s["m_read"], 1)
                if n == 4:
                    wait(act, s["y_ready"], g)
                    for c in range(CH):
                        wait(act, s["f_mm"], U * b + 2 + c)
                        nc.scalar.activation(u[j][:, c], M[(1 + c) % 2][:], ACT.Silu, bias=cbias[:, c:c + 1])\
                            .then_inc(s["m_read"], 1)
                    for c in range(CH):
                        wait(act, s["f_mm"], U * b + 4 + c)
                        nc.scalar.activation(sz[j][:, c], M[(1 + c) % 2][:], ACT.Silu).then_inc(s["m_read"], 1)
                if n == 7:
                    wait(act, s["f_mm"], U * b + 6)
                    nc.scalar.activation(dtl[:], M[1][:], ACT.Copy).then_inc(s["m_read"], 1)
                    wait(act, s["f_mm"], U * b + 7)
                    wait(act, s["bc_ready"], 2 * b)
                    nc.scalar.activation(bf[:], M[0][:], ACT.Copy)
                    nc.scalar.activation(bc[j][:], M[0][:], ACT.Copy).then_inc(s["m_read"], 1)
                if n in (9, 10):
                    c = n - 9
                    wait(act, s["f_mm"], U * b + 8 + c)
                    wait(act, s["dt_ready"], b)
                    nc.scalar.activation(et[:, c], M[(1 + c) % 2][:], ACT.Exp, bias=bdt[:, c:c + 1])\
                        .then_inc(s["m_read"], 1)
                if n == 12:
                    wait(act, s["fseq"], 4 * b + 1)
                    nc.scalar.activation(et[:], et[:], ACT.Ln, bias=1.0).then_inc(s["ln_done"], 1)

            def step(g, k, on):
                if on(0):
                    wait(act, s["dt_ready"], g + 1)
                for n in range(N):
                    if on(0):
                        for c in range(CH):
                            wait(act, s["scanned"], g * W2 + (2 * (n - 2) + c + 1))
                            nc.scalar.activation(dA[n % 2][c][:], dtA[k][:, c], ACT.Exp, scale=A[:, c, n:n + 1])\
                                .then_inc(s["dA_done"], 1)
                    if on(1):
                        front(g, k, n)

            pipeline(act, step, GROUPS, 1)

        @block.vector
        def _(v):
            nc.vector.memset(xnp[:], 0.0).then_inc(s["set_up"], 1)
            v.wait_ge(s["loaded"], 16 * len(loads))
            for c in range(CH):
                for t in range(4):
                    last = nc.vector.tensor_tensor(wk[:, t, c * P:c * P + P], win[:, c], cw[:, t, c * P:c * P + P], ALU.mult)
            last.then_inc(s["set_up"], 1)
            v.wait_ge(s["seta"], 1)
            nc.vector.tensor_scalar(A[:], A[:], -1.0, None, ALU.mult).then_inc(s["set_up"], 1)

            def front(g, k, n):
                b, j = g + 1, (k + 1) % 2
                if n == 0:
                    wait(v, s["f_mm"], U * (b - 1) + 1)
                    normed(nc, v, res, xn, b, res["rstd2"], s["xn_ready"])
                if n == 11:
                    wait(v, s["m_read"], U * b + 9)
                    nc.vector.tensor_scalar(et[:], et[:], 1.0, None, ALU.min).then_inc(s["fseq"], 1)
                if n == 14:
                    wait(v, s["ln_done"], b + 1)
                    nc.vector.tensor_scalar(et[:], et[:], 0.001, 0.001, ALU.add, ALU.max).then_inc(s["fseq"], 1)
                    wait(v, s["fseq"], 4 * b + 2)
                    nc.vector.scalar_tensor_tensor(out=dtu[j][:], in0=et[:], scalar=0.1, in1=u[j][:],
                                                   op0=ALU.min, op1=ALU.mult).then_inc(s["fseq"], 1)
                    nc.vector.tensor_scalar(dtA[j][:], et[:], 0.1, None, ALU.min).then_inc(s["fseq"], 1)
                    wait(v, s["fseq"], 4 * b + 4)
                    nc.vector.memset(dtA[j][:].rearrange("p c (b s) -> p (c b) s", b=NB)[:, :, 0:1], 1e25)\
                        .then_inc(s["dt_ready"], 1)

            def finish(g, k):
                wait(v, s["y_mm"], g * W2 + W2)
                wait(v, s["out_mm"], g)
                for c in range(CH):
                    nc.vector.scalar_tensor_tensor(out=yy[:, c], in0=u[k][:, c], scalar=dpar[:, c:c + 1], in1=Y[c][:],
                                                   op0=ALU.mult, op1=ALU.add).then_inc(s["y_read"], 1)
                for t in range(G):
                    nc.vector.tensor_scalar(tmp[:, t], x[:, g * G + t], res["mean"][:, bass.ds(g * G + t, 1)],
                                            res["rstd"][:, bass.ds(g * G + t, 1)], ALU.subtract, ALU.mult)\
                        .then_inc(s["oseq"], 1)
                wait(v, s["y_read"], g * CH + CH)
                nc.vector.tensor_tensor(yy[:], yy[:], sz[k][:], ALU.mult).then_inc(s["y_ready"], 1)
                xs = x[:, bass.ds(g * G, G), :]
                wait(v, s["oseq"], g * 6 + 4)
                nc.vector.tensor_tensor(xs, xs, tmp[:], ALU.add).then_inc(s["oseq"], 1)
                wait(v, s["out_mm"], g + 1)
                wait(v, s["oseq"], g * 6 + 5)
                nc.vector.tensor_tensor(xs, xs, M[1][:].rearrange("p (t d) -> p t d", t=G), ALU.add).then_inc(s["oseq"], 1)
                wait(v, s["oseq"], g * 6 + 6)
                row_stats(nc, res, g)

            def step(g, k, on):
                if on(0):
                    wait(v, s["dt_ready"], g + 1)
                for n in range(N):
                    if on(0):
                        m = g * W2 + 2 * n
                        wait(v, s["bb_mm"], g * N + (n + 1))
                        for c in range(CH):
                            nc.vector.tensor_tensor(inp[c][:], dtu[k][:, c], BB[n % 2][:], ALU.mult).then_inc(s["mulB"], 1)
                        for c in range(CH):
                            wait(v, s["mulB"], m + (c + 1))
                            wait(v, s["dA_done"], m + (c + 1))
                            nc.vector.tensor_tensor_scan(h[c][:], dA[n % 2][c][:], inp[c][:], 0.0, ALU.mult, ALU.add)\
                                .then_inc(s["scanned"], 1)
                        wait(v, s["cc_mm"], g * N + (n + 1))
                        for c in range(CH):
                            wait(v, s["scanned"], m + (c + 1))
                            wait(v, s["y_mm"], g * W2 + (2 * (n - 2) + c + 1))
                            nc.vector.tensor_tensor(hc[n % 2][c][:], h[c][:], CC[n % 2][:], ALU.mult)\
                                .then_inc(s["mulC"], 1)
                    if on(1):
                        front(g, k, n)
                if on(0):
                    finish(g, k)

            pipeline(v, step, GROUPS, 1)

        @block.tensor
        def _(pe):
            pe.wait_ge(s["set_up"], 2)

            def claim(b, i):
                if i == 1:
                    wait(pe, s["oseq"], 6 * (b - 1))
                wait(pe, s["m_read"], U * b + max(i - 1, 0))

            def front(g, k, n):
                b, j = g + 1, (k + 1) % 2
                if n == 0:
                    wait(pe, s["xn_ready"], G * (b + 1))
                    claim(b, 0)
                    for t in range(G):
                        last = nc.tensor.transpose(M[0][:, t * P:t * P + P], xn[:, t], ident[:])
                    last.then_inc(s["f_mm"], 1)
                if n in (1, 2):
                    c = n - 1
                    claim(b, 1 + c)
                    wait(pe, s["m_read"], U * b + 1)
                    out = M[(1 + c) % 2][:].rearrange("p (b s) -> p b s", b=NB)
                    for t in range(4):
                        last = nc.tensor.matmul(out, wk[:, t, c * P:c * P + P], xnp[:, :, t:t + S],
                                                start=(t == 0), stop=(t == 3))
                    last.then_inc(s["f_mm"], 1)
                if n == 4:
                    for c in range(CH):
                        claim(b, 3 + c)
                        out = M[(1 + c) % 2][:].rearrange("p (b s) -> p b s", b=NB)
                        nc.tensor.matmul(out, win[:, CH + c], xnp[:, :, 3:PADW], start=True, stop=True)\
                            .then_inc(s["f_mm"], 1)
                if n == 6:
                    for i, wt in ((5, wdl), (6, wbc)):
                        claim(b, i)
                        wait(pe, s["m_read"], U * b + 5)
                        for c in range(CH):
                            last = nc.tensor.matmul(M[i % 2][:], wt[:, c], u[j][:, c], start=(c == 0), stop=(c == CH - 1))
                        last.then_inc(s["f_mm"], 1)
                if n in (8, 9):
                    c = n - 8
                    claim(b, 7 + c)
                    nc.tensor.matmul(M[(7 + c) % 2][:], wdt[:, c], dtl[:], start=True, stop=True).then_inc(s["f_mm"], 1)

            def spread(g, k, n):
                wait(pe, s["mulB"], g * W2 + 2 * (n - 1))
                nc.tensor.matmul(BB[n % 2][:], sel[:, n], bc[k][:], start=True, stop=True).then_inc(s["bb_mm"], 1)
                wait(pe, s["mulC"], g * W2 + 2 * (n - 1))
                nc.tensor.matmul(CC[n % 2][:], sel[:, N + n], bc[k][:], start=True, stop=True).then_inc(s["cc_mm"], 1)

            def step(g, k, on):
                if on(0):
                    wait(pe, s["bc_ready"], 2 * g + 2)
                    spread(g, k, 0)
                for n in range(N):
                    if on(0) and n + 1 < N:
                        spread(g, k, n + 1)
                    if on(1):
                        front(g, k, n)
                    if on(0):
                        if n == 0:
                            wait(pe, s["y_read"], CH * g)
                        for c in range(CH):
                            wait(pe, s["mulC"], g * W2 + (2 * n + c + 1))
                            nc.tensor.matmul(Y[c][:], ident[:], hc[n % 2][c][:], start=(n == 0), stop=(n == N - 1))\
                                .then_inc(s["y_mm"], 1)
                if on(0):
                    wait(pe, s["y_ready"], g + 1)
                    if on(1):
                        wait(pe, s["m_read"], U * (g + 1) + 8)
                    for t in range(G):
                        for c in range(CH):
                            last = nc.tensor.matmul(M[1][:, t * P:t * P + P], yy[:, c, t * P:t * P + P], wout[:, c],
                                                    start=(c == 0), stop=(c == CH - 1))
                    last.then_inc(s["out_mm"], 1)

            pipeline(pe, step, GROUPS, 1)


def state_constants():
    sel = np.zeros((P, 32, P), HOST_BF16)
    for r in range(96):
        sel[r, r % 32] = 1.0
    return {"bsel": sel}


def load_x(nc, res, x_in):
    x, stats = res["x"], res["stats"]
    rows = x_in.rearrange("b (t p) d -> p (b t) d", p=P)
    step = 8
    with ExitStack() as ctx:
        sc = Scope(nc, ctx, "load")
        loaded = [sc.sem(f"loaded{i}") for i in range(TILES // step)]
        c = sc.sem("c")
        block = ctx.enter_context(nc.Block())

        @block.sync
        def _(sp):
            for i in range(TILES // step):
                sp.dma_start(x[:, i * step:(i + 1) * step], rows[:, i * step:(i + 1) * step]).then_inc(loaded[i], 16)

        @block.scalar
        def _(act):
            act.dma_start(res["ident"][:], res["ident_in"]).then_inc(c, 16)
            act.dma_start(res["identb"][:], res["identb_in"]).then_inc(c, 16)
            act.wait_ge(c, 32)

        @block.vector
        def _(v):
            nc.vector.memset(res["ones"][:], 1.0)
            for i in range(TILES // step):
                v.wait_ge(loaded[i], 16)
                for t in range(i * step, (i + 1) * step):
                    nc.vector.bn_stats(stats[:, t, :], x[:, t, :])


def store_x(nc, res, out):
    x = res["x"]
    with ExitStack() as ctx:
        sc = Scope(nc, ctx, "store")
        stored = sc.sem("stored")
        block = ctx.enter_context(nc.Block())

        @block.sync
        def _(sp):
            rows = out.rearrange("b (t p) d -> p (b t) d", p=P)
            for i in range(8):
                sp.dma_start(rows[:, 8 * i:8 * i + 8], x[:, 8 * i:8 * i + 8]).then_inc(stored, 16)
            sp.wait_ge(stored, 8 * 16)


def program(nc, a, out, stages=range(8)):
    with ExitStack() as ctx:
        sc = Scope(nc, ctx, "g")
        res = {"x": sc.sb("x", [P, TILES, D]), "stats": sc.sb("stats", [P, TILES, 6]),
               "mean": sc.sb("mean", [P, TILES]), "rstd": sc.sb("rstd", [P, TILES]), "rstd2": sc.sb("rstd2", [P, TILES]),
               "ident": sc.sb("ident", [P, P]), "identb": sc.sb("identb", [P, P], BF16),
               "ones": sc.sb("ones", [P, P]),
               "ident_in": a["c_ident"], "identb_in": a["c_identb"]}
        load_x(nc, res, a["x"])
        for n in stages:
            STAGES[n](nc, res, a)
        store_x(nc, res, out)


def l0_attn(nc, res, a):
    norm_factors(nc, res, "n0")
    attention(nc, res, "a0", {"wqkv": a["L0_qkv"], "bqk": a["L0_bqk"], "bv": a["L0_bv"], "rel": a["L0_attn_rel_bias"],
                              "hot": a["c_hot"], "flip": a["c_flip"], "krows": a["c_krows"]}, False)


def l1_attn(nc, res, a):
    norm_factors(nc, res, "n2")
    attention(nc, res, "a2", {"wqkv": a["L1_qkv"], "bqk": a["L1_bqk"], "bv": a["L1_bv"], "krows": a["c_krows"],
                              "maskq": a["c_maskq"], "maskk": a["c_maskk"], "wproj": a["L1_attn_w_proj"],
                              "bproj": a["L1_bproj"]}, True)


def l0_ffn(nc, res, a):
    ternary_ffn(nc, res, "f1", {"up": a["L0_up"], "down": a["L0_down"]})


def l3_ffn(nc, res, a):
    lowrank_ffn(nc, res, "f7", {n: a["L3_" + n] for n in ("u1", "v1", "u2", "v2", "b1", "b2")})


def l1_ffn(nc, res, a):
    expert_choice(nc, res, "f3", {"wr": a["L1_ffn_Wr"], "w1": a["L1_w1"], "b1": a["L1_b1"], "w2": a["L1_w2"],
                                  "b2": a["L1_b2"], "same": a["c_same"], "before": a["c_before"]})


def l3_attn(nc, res, a):
    min_gru(nc, res, "a6", {"wz": a["L3_attn_Wz"], "wh": a["L3_attn_Wh"], "bz": a["L3_bz"], "bh": a["L3_bh"],
                            "swish": a["L3_swish"], "gamma": a["L3_gamma"], "beta": a["L3_beta"]})


def l2_attn(nc, res, a):
    w = {n: a["L2_" + n] for n in "win cw wdl wbc wdt wout cbias bdt dpar lnw lnb la".split()}
    state_space(nc, res, "a4", {**w, "sel": a["c_bsel"]})


def l2_ffn(nc, res, a):
    w = {n: a["L2f_" + n] for n in "wr bias wg wu wd".split()}
    routed_experts(nc, res, "f5", {**w, "sel": a["c_sel"], "fresh": a["c_fresh"]})


STAGES = [l0_attn, l0_ffn, l1_attn, l1_ffn, l2_attn, l2_ffn, l3_attn, l3_ffn]


def padded(a, rows, cols):
    out = np.zeros((rows, cols), a.dtype)
    out[:a.shape[0], :a.shape[1]] = a
    return out


def layout(i):
    def dh(w):
        return w.reshape(w.shape[0], H, DH).transpose(0, 2, 1).reshape(w.shape[0], D)

    def rows(v, n=P):
        return np.broadcast_to(v.reshape(1, -1), (n, v.size))

    o = {"x": i["L0_attn_hidden_states"]}
    wa, ba = i["L1_attn_w_attn"], i["L1_attn_b_attn"].reshape(1, -1)
    for n, (wq, wk, wv, bq, bk, bvv) in {
            "L0": (i["L0_attn_Wq"], i["L0_attn_Wk"], i["L0_attn_Wv"], i["L0_attn_bq"].reshape(1, -1),
                   i["L0_attn_bk"].reshape(1, -1), i["L0_attn_bv"]),
            "L1": (wa[:, 0:D], wa[:, D:2 * D], wa[:, 2 * D:], ba[:, 0:D], ba[:, D:2 * D], ba[0, 2 * D:])}.items():
        o[f"{n}_qkv"] = np.stack([dh(wq), dh(wk), wv], 1)
        o[f"{n}_bqk"] = np.concatenate([dh(bq), dh(bk)], 0).T
        o[f"{n}_bv"] = rows(bvv)
    o["L0_attn_rel_bias"] = i["L0_attn_rel_bias"]
    o["L1_attn_w_proj"] = i["L1_attn_w_proj"]
    o["L1_bproj"] = i["L1_attn_b_proj"].reshape(1, -1)
    o["L0_up"] = i["L0_ffn_w_up"].T.reshape(D, 4, P)
    o["L0_down"] = i["L0_ffn_w_down"].T.reshape(4, P, D).transpose(1, 0, 2)
    o["L3_u1"] = padded(i["L3_ffn_U1"], P, P)
    o["L3_v1"] = padded(i["L3_ffn_V1"], P, 4 * P)
    o["L3_u2"] = padded(i["L3_ffn_U2"], 4 * P, P).reshape(4, P, P).transpose(1, 0, 2)
    o["L3_v2"] = padded(i["L3_ffn_V2"], P, P)
    o["L3_b1"] = i["L3_ffn_b1"].reshape(4, P).T
    o["L3_b2"] = i["L3_ffn_b2"].reshape(1, P)
    o["L1_ffn_Wr"] = i["L1_ffn_Wr"]
    o["L1_w1"] = i["L1_ffn_W1"].transpose(1, 0, 2)
    o["L1_b1"] = i["L1_ffn_b1"].reshape(8, 4, P).transpose(2, 0, 1)
    o["L1_w2"] = i["L1_ffn_W2"].reshape(8, 4, P, D).transpose(2, 0, 1, 3)
    o["L1_b2"] = i["L1_ffn_b2"].reshape(1, 8, D)
    for n in ("Wz", "Wh"):
        o["L3_attn_" + n] = i["L3_attn_" + n]
    o["L3_bz"], o["L3_bh"] = i["L3_attn_bz"].reshape(P, 1), i["L3_attn_bh"].reshape(P, 1)
    o["L3_swish"] = np.broadcast_to(i["L3_attn_swish_beta"].reshape(1, 1), (P, 1))
    for n in ("gamma", "beta"):
        o["L3_" + n] = np.broadcast_to(i["L3_attn_ln_" + n].reshape(1, 1, D), (P, G, D))
    def halves(v):
        return v.reshape(2, P).T

    o["L2_win"] = i["L2_attn_W_in"].T.reshape(D, 4, P)
    o["L2_cw"] = np.broadcast_to(i["L2_attn_conv_w"][:, 0, :].T.reshape(1, 4, 2 * P), (P, 4, 2 * P))
    wx = i["L2_attn_W_x"].T.reshape(2, P, 96).transpose(1, 0, 2)
    low, bcs = np.zeros((P, 2, P), wx.dtype), np.zeros((P, 2, P), wx.dtype)
    low[:, :, 0:64] = wx[:, :, 0:64]
    for r in range(3):
        bcs[:, :, 32 * r:32 * r + 32] = wx[:, :, 64:96]
    o["L2_wdl"], o["L2_wbc"] = low, bcs
    o["L2_wdt"] = padded(i["L2_attn_W_dt"].T, P, 2 * P).reshape(P, 2, P)
    o["L2_wout"] = i["L2_attn_W_out"].T.reshape(2, P, D).transpose(1, 0, 2)
    o["L2_cbias"], o["L2_bdt"], o["L2_dpar"] = (halves(i["L2_attn_" + n]) for n in ("conv_b", "b_dt", "D_param"))
    o["L2_lnw"], o["L2_lnb"] = i["L2_attn_ln_w"].reshape(P, 1), i["L2_attn_ln_b"].reshape(P, 1)
    o["L2_la"] = i["L2_attn_log_A"].reshape(2, P, 16).transpose(1, 0, 2)
    gu = i["L2_ffn_gate_up_proj"].reshape(16, 2, 2, 64, D)
    for n, part, shared in (("wg", 0, "gate"), ("wu", 1, "up")):
        pairs = gu[:, :, part].transpose(3, 0, 1, 2).reshape(D, 16, P)
        o["L2f_" + n] = np.concatenate([pairs, i[f"L2_ffn_shared_{shared}_w"].T.reshape(D, 1, P)], 1)
    down = i["L2_ffn_down_proj"].reshape(16, 2, D, 64).transpose(1, 3, 0, 2).reshape(P, 16, D)
    o["L2f_wd"] = np.concatenate([down, i["L2_ffn_shared_down_w"].T.reshape(P, 1, D)], 1)
    o["L2f_wr"] = i["L2_ffn_router_weight"].T
    o["L2f_bias"] = np.broadcast_to(i["L2_ffn_e_score_bias"].reshape(1, 1, 32), (P, G, 32))
    for n, c in {**attention_constants(), **choose_constants(), **routed_constants(), **state_constants()}.items():
        o["c_" + n] = c
    return {k: np.ascontiguousarray(v) for k, v in o.items()}


def kernel(**inputs):
    import concourse.bacc as _bacc
    from concourse.bass_utils import run_bass_kernel_spmd as _run

    nc = _bacc.Bacc("TRN2", target_bir_lowering=False, num_devices=1)
    arrays = layout({name: np.asarray(value) for name, value in inputs.items()})
    args = {name: nc.dram_tensor(name, v.shape, mybir.dt.from_np(v.dtype), kind="ExternalInput").ap()
            for name, v in arrays.items()}
    out = nc.dram_tensor("out", (B, S, D), F32, kind="ExternalOutput").ap()
    program(nc, args, out)
    r = _run(nc, [arrays], core_ids=[0])
    return r.results[0]["out"]
```

```python
import math
from contextlib import ExitStack

import numpy as np
import concourse.bass as bass
from concourse import mybir

F32 = mybir.dt.float32
BF16 = mybir.dt.bfloat16
HOST_BF16 = mybir.dt.np(BF16)
ALU = mybir.AluOpType
ACT = mybir.ActivationFunctionType
AX = mybir.AxisListType

P = 128
B, S, D = 32, 256, 128
TILES = B * S // P
TB = S // P
H, DH = 16, 8
EPS = 1e-5


def wait(eng, sem, value):
    if not isinstance(value, int) or value > 0:
        eng.wait_ge(sem, value)


def waits(eng, *pairs):
    pairs = [(sem, v if isinstance(v, int) else eng.snap(v)) for sem, v in pairs]
    for sem, v in pairs:
        wait(eng, sem, v)


class Scope:

    def __init__(self, nc, ctx, name):
        self.nc, self.ctx, self.name, self.sems = nc, ctx, name, []
        ctx.callback(self.close)

    def sb(self, name, shape, dt=F32):
        return self.ctx.enter_context(self.nc.sbuf_tensor(f"{self.name}_{name}", shape, dt))

    def ps(self, name, shape, dt=F32):
        return self.ctx.enter_context(self.nc.psum_tensor(f"{self.name}_{name}", shape, dt))

    def sem(self, name):
        self.sems.append(self.nc.alloc_semaphore(name=f"{self.name}_{name}"))
        return self.sems[-1]

    def close(self):
        if self.sems:
            self.nc.clear_and_free_semaphores(self.sems)
            self.nc.all_engine_barrier()


def norm_factors(nc, res, name, then=None):
    st, mean, rstd, rstd2 = res["stats"], res["mean"], res["rstd"], res["rstd2"]
    with ExitStack() as ctx:
        sc = Scope(nc, ctx, name)
        tmp, dif, var, nvar = (sc.sb(n, [P, TILES]) for n in ("tmp", "dif", "var", "nvar"))
        step, var_ready, root_ready = sc.sem("step"), sc.sem("var_ready"), sc.sem("root_ready")
        block = ctx.enter_context(nc.Block())
        me, ce, mo, co = st[:, :, 1], st[:, :, 2], st[:, :, 4], st[:, :, 5]

        @block.vector
        def _(v):
            nc.vector.tensor_tensor(tmp[:], me, mo, ALU.add).then_inc(step, 1)
            nc.vector.tensor_tensor(dif[:], me, mo, ALU.subtract).then_inc(step, 1)
            nc.vector.tensor_tensor(var[:], ce, co, ALU.add).then_inc(step, 1)
            v.wait_ge(step, 3)
            nc.vector.tensor_scalar(mean[:], tmp[:], 0.5, None, ALU.mult).then_inc(step, 1)
            nc.vector.scalar_tensor_tensor(out=dif[:], in0=dif[:], scalar=0.25, in1=dif[:],
                                           op0=ALU.mult, op1=ALU.mult).then_inc(step, 1)
            v.wait_ge(step, 5)
            nc.vector.scalar_tensor_tensor(out=var[:], in0=var[:], scalar=1.0 / D, in1=dif[:],
                                           op0=ALU.mult, op1=ALU.add).then_inc(step, 1)
            v.wait_ge(step, 6)
            nc.vector.tensor_scalar(nvar[:], var[:], EPS, None, ALU.add).then_inc(var_ready, 1)
            v.wait_ge(root_ready, 1)
            nc.vector.reciprocal(rstd[:], tmp[:]).then_inc(step, 1)
            if then:
                v.wait_ge(step, 7)
                nc.vector.tensor_tensor(dif[:], rstd[:], rstd[:], ALU.mult).then_inc(step, 1)
                v.wait_ge(step, 8)
                nc.vector.tensor_tensor(dif[:], dif[:], var[:], ALU.mult).then_inc(step, 1)
                v.wait_ge(step, 9)
                nc.vector.tensor_scalar(var[:], dif[:], EPS if then == "norm" else 0.0, None, ALU.add)\
                    .then_inc(var_ready, 1)
                v.wait_ge(root_ready, 2)
                nc.vector.tensor_scalar(dif[:], tmp[:], 0.0 if then == "norm" else 1e-8, None, ALU.add)\
                    .then_inc(step, 1)
                v.wait_ge(step, 10)
                nc.vector.reciprocal(var[:], dif[:]).then_inc(step, 1)
                v.wait_ge(step, 11)
                nc.vector.tensor_tensor(rstd2[:], var[:], rstd[:], ALU.mult)

        @block.scalar
        def _(a):
            a.wait_ge(var_ready, 1)
            nc.scalar.activation(tmp[:], nvar[:], ACT.Sqrt).then_inc(root_ready, 1)
            if then:
                a.wait_ge(var_ready, 2)
                nc.scalar.activation(tmp[:], var[:], ACT.Sqrt).then_inc(root_ready, 1)


def pipeline(eng, step, n, lead, unroll=2, back=0, peel=1):
    def static(g):
        step(g, g % unroll, lambda off: 0 <= g + off < n)

    start = peel + back + (n - lead - back - peel) % unroll
    rounds = (n - lead - start) // unroll
    for g in range(-lead, start):
        static(g)
    with eng.Fori(0, rounds) as i:
        for k in range(unroll):
            step(i * unroll + (start + k), (start + k) % unroll, lambda off: True)
    for g in range(n - lead, n + back):
        static(g)


G = 4
GT = G * P
GROUPS = TILES // G


def attention(nc, res, name, w, causal):
    x, mean, rstd, stats = res["x"], res["mean"], res["rstd"], res["stats"]
    scale = 1.0 / math.sqrt(DH)
    ROWS, MROW, KM = 3 * 3 * DH, 96, 96
    NPART, BUF, NP = 3, 4, 4
    BAND = 160
    K0Q, K1Q = S, (P if causal else S)
    with ExitStack() as ctx:
        sc = Scope(nc, ctx, name)
        wqkv = sc.sb("wqkv", [P, 3, P])
        bqk = sc.sb("bqk", [P, 2])
        bqs = sc.sb("bqs", [P, 1])
        bv = sc.sb("bv", [P, P])
        xn = [sc.sb(f"xn{i}", [P, TB, D]) for i in range(2)]
        xnT = sc.sb("xnT", [P, S])
        qk32 = sc.sb("qk32", [P, 2 * S])
        rest = sc.sb("rest", [P, 2 * S])
        parts = sc.sb("parts", [P, NPART, 2 * S], BF16)
        Qp = [sc.sb(f"Qp{i}", [P, H, S], BF16) for i in range(BUF)]
        Kp = [sc.sb(f"Kp{i}", [P, H, S], BF16) for i in range(BUF)]
        V = [sc.sb(f"V{i}", [P, TB, H, 32]) for i in range(BUF)]
        Mx = [sc.sb(f"Mx{i}", [P, TB, H]) for i in range(2)]
        mrest = sc.sb("mrest", [P, TB, H])
        mparts = [sc.sb(f"mparts{i}", [P, TB, P // H, H], BF16) for i in range(2)]
        mrow = [sc.sb(f"mrow{i}", [NPART * H, S], BF16) for i in range(2)]
        Pr = [sc.sb(f"Pr{i}", [P, 2 * S]) for i in range(NP)]
        osb = [sc.sb(f"osb{i}", [P, S]) for i in range(2)]
        rc = [sc.sb(f"rc{i}", [P, TB, 4]) for i in range(2)]
        prod = [sc.sb(f"prod{i}", [P, TB, 4, DH]) for i in range(2)]
        Sx = [sc.ps(f"Sx{i}", [P, 2 * S]) for i in range(2)]
        Se = [sc.ps(f"Se{i}", [P, 2 * S]) for i in range(2)]
        O = [sc.ps(f"O{i}", [P, 2 * S]) for i in range(2)]
        OT = sc.ps("OT", [P, 2 * S])[:, 0:S]
        TURN = sc.ps("TURN", [P, 2 * S])
        mps = TURN[:, 0:P].bitcast(BF16)
        if causal:
            y = [sc.sb(f"y{i}", [P, TB, D]) for i in range(2)]
            yT = sc.sb("yT", [P, S])
            wproj = sc.sb("wproj", [P, P])
            bproj = sc.sb("bproj", [1, P])
            maskq = sc.sb("maskq", [P, P], BF16)
            maskk = sc.sb("maskk", [P, P], BF16)
        else:
            bmax = sc.sb("bmax", [P, H, 3 * P], BF16)
            bexp = sc.sb("bexp", [P, NPART, H, BAND], BF16)
            flip = sc.sb("flip", [P, P], BF16)

        SEMS = ("w v_zero cleared k_cleared ones consts xn_ready xn_used xt_ready qk_mm qk_ev first_part v_mm v_ready seq split_done written packed "
                "mx_mm red_done mseq mp_ready mt_mm mrow_ready mpacked se_mm exp_done pv_done "
                "o_ev ot_mm cseq fin rseq yt_mm yt_ev pr_mm pr_done").split()
        s = {n: sc.sem(n) for n in SEMS}
        LATE = 2

        def slot(b, j):
            return (b + 2, j - LATE) if j >= LATE else (b + 1, j + 8 - LATE)

        PART = DH * H * S
        packing = nc.dram_tensor(name + "_packing", [NPART, 2, DH, H, S], BF16, kind="Internal").ap()
        loads = [(wqkv[:], w["wqkv"]), (bqk[:], w["bqk"]), (bv[:], w["bv"])]
        if causal:
            loads += [(maskq[:], w["maskq"]), (maskk[:], w["maskk"]), (wproj[:], w["wproj"]), (bproj[:], w["bproj"])]
        ident, identb = res["ident"], res["identb"]
        if not causal:
            loads += [(flip[:], w["flip"])]
            bias = BiasSetup(nc, sc, w, bmax, bexp, BAND, [Sx[0], Sx[1], Se[0]])

        with nc.Block() as block:

            @block.sync
            def _(sp):
                if not causal:
                    bias.load(sp)
                for dst, src in loads:
                    sp.dma_start(dst, src).then_inc(s["w"], 16)
                if not causal:
                    bias.place(sp)
                    sp.wait_ge(bias.crows_stored, NPART * 16)
                sp.wait_ge(s["cleared"], 1)
                sp.wait_ge(s["k_cleared"], 1)
                for k in range(BUF):
                    sp.dma_start(Kp[k][MROW:MROW + 9], w["krows"]).then_inc(s["consts"], 16)
                    if not causal:
                        sp.dma_start(Qp[k][MROW + 3:MROW + 9], bias.crows).then_inc(s["consts"], 16)

                def step(b, k, a, x_, m, c, p):
                    if m:
                        kb = (k + 1) % BUF
                        wait(sp, s["mrow_ready"], b + 2)
                        sp.dma_start(Qp[kb][MROW:MROW + 3, :, :], mrow[kb % 2][:, :]).then_inc(s["mpacked"], 16)
                    if a:
                        kb = (k + 3) % BUF
                        wait(sp, s["split_done"], b + 4)
                        sp.dma_start(packing.rearrange("i c e h q -> (e h) (i c) q"),
                                     parts[:].rearrange("p i (c q) -> p (i c) q", c=2)).then_inc(s["written"], 16)
                        wait(sp, s["written"], 16 * (b + 4))
                        row = [[H * S, DH], [1, H * S]]
                        for j in range(3):
                            r = slice(j * 3 * DH, (j + 1) * 3 * DH)
                            sp.dma_start(Qp[kb][r], bass.AP(packing.tensor, 0, [[2 * PART, 3], *row]))\
                                .then_inc(s["packed"], 16)
                            sp.dma_start(Kp[kb][r], bass.AP(packing.tensor, (2 * j + 1) * PART, [[0, 3], *row]))\
                                .then_inc(s["packed"], 16)

                run_steps(sp, step)

            @block.gpsimd
            def _(g):
                for k in range(BUF):
                    nc.gpsimd.memset(V[k][:], 0.0).then_inc(s["v_zero"], 1)
                g.wait_ge(s["v_zero"], BUF)
                for k in range(BUF):
                    last = nc.gpsimd.memset(V[k][:, :, :, DH:DH + 1], 1.0)
                last.then_inc(s["ones"], 1)
                g.wait_ge(s["ones"], 1)
                for k in range(BUF):
                    last = nc.gpsimd.memset(Kp[k][64:128].rearrange("p h q -> p (h q)").bitcast(F32), 0.0)
                last.then_inc(s["k_cleared"], 1)
                g.wait_ge(s["k_cleared"], 1)

                def step(b, k, a, x_, m, c, p):
                    if not a:
                        return
                    bb = b + 3
                    wait(g, s["written"], 16 * bb)
                    wait(g, s["first_part"], bb + 1)
                    for out, name in ((rest[:], "seq"), (parts[:, 1, :], "seq")):
                        nc.gpsimd.tensor_tensor(out, qk32[:], parts[:, 0, :], ALU.subtract).then_inc(s[name], 1)
                    wait(g, s["seq"], 2 * bb + 2)
                    wait(g, s["packed"], 6 * 16 * bb)
                    wait(g, s["pv_done"], 16 * b)
                    nc.gpsimd.tensor_tensor(parts[:, 2, :], rest[:], parts[:, 1, :], ALU.subtract)\
                        .then_inc(s["split_done"], 1)

                run_steps(g, step)

            @block.scalar
            def _(act):
                act.wait_ge(s["ones"], 1)
                act.wait_ge(s["w"], len(loads) * 16)
                nc.scalar.activation(bqs[:], bqk[:, 0:1], ACT.Copy, scale=scale).then_inc(s["rseq"], 1)
                act.wait_ge(s["rseq"], 1)

                def project(bb):
                    wait(act, s["xn_used"], bb + 1)
                    wait(act, s["v_mm"], bb)
                    nc.scalar.activation(xnT[:], TURN[:, 0:S], ACT.Copy).then_inc(s["xt_ready"], 1)

                def split(bb):
                    wait(act, s["qk_mm"], bb + 1)
                    wait(act, s["split_done"], bb)
                    wait(act, s["written"], 16 * bb)
                    nc.scalar.activation(qk32[:, 0:S], TURN[:, 0:S], ACT.Identity, bias=bqs[:], scale=scale)\
                        .then_inc(s["qk_ev"], 1)
                    nc.scalar.activation(qk32[:, S:2 * S], TURN[:, S:2 * S], ACT.Identity, bias=bqk[:, 1:2])\
                        .then_inc(s["qk_ev"], 1)
                    wait(act, s["qk_ev"], 2 * bb + 2)
                    nc.scalar.activation(parts[:, 0], qk32[:], ACT.Copy).then_inc(s["first_part"], 1)

                def evac(b, c):
                    wait(act, s["pv_done"], 16 * b + 4 * c + 4)
                    wait(act, s["ot_mm"], 4 * b + c - 1)
                    nc.scalar.activation(osb[c % 2][:], O[c % 2][:, 0:S], ACT.Copy).then_inc(s["o_ev"], 1)

                def step(b, k, a, x_, m, c, p):
                    for j in range(8):
                        if m and j == 3:
                            wait(act, s["mt_mm"], b + 2)
                            wait(act, s["mpacked"], 16 * b)
                            nc.scalar.activation(mrow[(k + 1) % 2][:], mps[0:NPART * H, :], ACT.Copy).then_inc(s["mrow_ready"], 1)
                        if causal and p and j == 4:
                            wait(act, s["yt_mm"], b)
                            nc.scalar.activation(yT[:], TURN[:, 0:S], ACT.Copy).then_inc(s["yt_ev"], 1)
                        if c:
                            for h in (2 * j, 2 * j + 1):
                                wait(act, s["se_mm"], 16 * b + h + 1)
                                wait(act, s["pv_done"], 16 * b + h + 1 - NP)
                                nc.scalar.activation(Pr[h % NP][:, 0:K0Q + K1Q], Se[h % 2][:, 0:K0Q + K1Q],
                                                     ACT.Exp).then_inc(s["exp_done"], 1)
                            if j % 2 == 0 and j:
                                evac(b, j // 2 - 1)
                        if p and j == 0:
                            evac(b - 1, 3)
                        if a and j == 0:
                            project(b + 3)
                        if a and j == 1:
                            split(b + 3)

                run_steps(act, step)

            @block.vector
            def _(v):
                for i in range(2):
                    nc.vector.memset(mparts[i][:], 0.0)
                for k in range(BUF):
                    last = nc.vector.memset(Qp[k][64:128].rearrange("p h q -> p (h q)").bitcast(F32), 0.0)
                last.then_inc(s["cleared"], 1)
                if not causal:
                    bias.split(v)
                nc.vector.memset(Mx[0][:, 0, 0:1], 0.0).then_inc(s["pr_done"], 1)
                v.wait_ge(s["cleared"], 1)
                v.wait_ge(s["w"], len(loads) * 16)
                v.wait_ge(s["ones"], 1)

                def finish(b, k, c):
                    wait(v, s["ot_mm"], 4 * b + c + 1)
                    q = c % 2
                    o4 = OT.rearrange("p (t h e) -> p t h e", t=TB, h=4)
                    n = 3 * (4 * b + c)
                    nc.vector.reciprocal(rc[q][:], o4[:, :, :, DH]).then_inc(s["cseq"], 1)
                    wait(v, s["cseq"], n + 1)
                    for t in range(TB):
                        dst = y[k % 2][:, t, 32 * c:32 * c + 32].rearrange("p (h e) -> p h e", h=4) if causal \
                            else prod[q][:, t]
                        nc.vector.tensor_tensor(dst, o4[:, t, :, 0:DH],
                                                rc[q][:, t].unsqueeze(2).to_broadcast([P, 4, DH]),
                                                ALU.mult).then_inc(s["cseq"], 1)
                    if not causal:
                        wait(v, s["cseq"], n + 3)
                        xs = x[:, bass.ds(TB * b, TB), 32 * c:32 * c + 32]
                        nc.vector.tensor_tensor(xs, xs, prod[q][:].rearrange("p t h e -> p t (h e)"),
                                                ALU.add).then_inc(s["fin"], 1)

                def split_maxima(bb, kb):
                    wait(v, s["red_done"], 16 * bb + 16)
                    wait(v, s["mt_mm"], bb - 1)
                    mp = mparts[kb]
                    nc.vector.tensor_scalar(mp[:, :, 0], Mx[kb][:], -1.0, None, ALU.mult).then_inc(s["mseq"], 1)
                    wait(v, s["mseq"], 3 * bb + 1)
                    nc.vector.scalar_tensor_tensor(out=mrest[:], in0=Mx[kb][:], scalar=-1.0, in1=mp[:, :, 0],
                                                   op0=ALU.mult, op1=ALU.subtract).then_inc(s["mseq"], 1)
                    wait(v, s["mseq"], 3 * bb + 2)
                    nc.vector.tensor_copy(mp[:, :, 1], mrest[:]).then_inc(s["mseq"], 1)
                    wait(v, s["mseq"], 3 * bb + 3)
                    nc.vector.tensor_tensor(mp[:, :, 2], mrest[:], mp[:, :, 1], ALU.subtract)\
                        .then_inc(s["mp_ready"], 1)

                def step(b, k, a, x_, m, c, p):
                    if a:
                        bb = b + 3
                        wait(v, s["xn_used"], bb - 1)
                        for t in range(TB):
                            nc.vector.tensor_scalar(xn[(k + 3) % 2][:, t], x[:, TB * bb + t],
                                                    mean[:, bass.ds(TB * bb + t, 1)],
                                                    rstd[:, bass.ds(TB * bb + t, 1)],
                                                    ALU.subtract, ALU.mult).then_inc(s["xn_ready"], 1)
                    for j in range(8):
                        bb, jj = slot(b, j)
                        if (x_ if j >= LATE else m):
                            for t in range(TB):
                                wait(v, s["mx_mm"], 16 * bb + (2 * jj + t + 1))
                                wd = P * (t + 1) if causal else S
                                nc.vector.tensor_reduce(
                                    Mx[(k + 2 - (j < LATE)) % 2][:, t, 2 * jj:2 * jj + 2],
                                    Sx[t][:, 0:2 * wd].rearrange("p (h q) -> p h q", h=2), AX.X, ALU.max
                                ).then_inc(s["red_done"], 1)
                        if m and j == LATE - 1:
                            split_maxima(b + 1, (k + 1) % 2)
                        if a and j == 5:
                            bb = b + 3
                            wait(v, s["v_mm"], bb + 1)
                            wait(v, s["pv_done"], 16 * (bb - 3))
                            for t in range(TB):
                                nc.vector.tensor_tensor(
                                    V[(k + 3) % BUF][:, t, :, 0:DH],
                                    TURN[:, t * P:t * P + P].rearrange("p (h e) -> p h e", h=H),
                                    bv[:].rearrange("p (h e) -> p h e", h=H), ALU.add).then_inc(s["v_ready"], 1)
                        if c and j % 2 == 1 and j > 1:
                            finish(b, k, (j - 3) // 2)
                        if p and j == 1:
                            finish(b - 1, k + 3, 3)
                            if not causal:
                                wait(v, s["fin"], 4 * b)
                                for t in range(TB):
                                    nc.vector.bn_stats(stats[:, TB * (b - 1) + t, :], x[:, TB * (b - 1) + t, :])
                        if causal and p and j == 6:
                            wait(v, s["pr_mm"], b)
                            xs = x[:, bass.ds(TB * (b - 1), TB), :]
                            nc.vector.tensor_tensor(xs, xs, TURN[:, 0:S].rearrange("p (t d) -> p t d", t=TB), ALU.add)\
                                .then_inc(s["pr_done"], 1)
                            wait(v, s["pr_done"], b + 1)
                            for t in range(TB):
                                nc.vector.bn_stats(stats[:, TB * (b - 1) + t, :], x[:, TB * (b - 1) + t, :])

                run_steps(v, step)

            @block.tensor
            def _(pe):
                if not causal:
                    bias.look_up(pe)
                pe.wait_ge(s["w"], len(loads) * 16)

                def maxima(b, kb, j):
                    for t in range(TB):
                        n = 16 * b + 2 * j + t
                        wait(pe, s["red_done"], n - 1)
                        wd = P * (t + 1) if causal else S
                        if not causal:
                            nc.tensor.matmul(Sx[t][:].rearrange("p (u q) -> p u q", u=2), flip[:],
                                             bmax[:, 2 * j:2 * j + 2, P * (1 - t):P * (1 - t) + S],
                                             start=True, stop=False)
                        for u in range(2):
                            h = 2 * j + u
                            last = nc.tensor.matmul(Sx[t][:, u * wd:u * wd + wd], Qp[kb][0:KM, h, t * P:t * P + P],
                                                    Kp[kb][0:KM, h, 0:wd], start=causal, stop=(not causal and u == 1))
                            if causal:
                                last = nc.tensor.matmul(Sx[t][:, u * wd + wd - P:u * wd + wd], identb[:], maskq[:],
                                                        start=False, stop=True)
                        last.then_inc(s["mx_mm"], 1)

                def scores(b, k, h):
                    wait(pe, s["exp_done"], 16 * b + h - 1)
                    Q, K, out = Qp[k], Kp[k], Se[h % 2]
                    nc.tensor.matmul(out[:, 0:S], K[:, h, 0:P], Q[:, h, :], start=True, stop=False)
                    if causal:
                        nc.tensor.matmul(out[:, 0:P], identb[:], maskk[:], start=False, stop=True)
                    else:
                        for i in range(NPART):
                            nc.tensor.matmul(out[:, 0:BAND], flip[:], bexp[:, i, h, :], start=False,
                                             stop=(i == NPART - 1))
                    nc.tensor.matmul(out[:, K0Q:K0Q + K1Q], K[:, h, P:2 * P], Q[:, h, S - K1Q:S],
                                     start=True, stop=False)
                    if causal:
                        last = nc.tensor.matmul(out[:, K0Q:K0Q + P], identb[:], maskk[:], start=False, stop=True)
                    else:
                        for i in range(NPART):
                            last = nc.tensor.matmul(out[:, S + P:2 * S], flip[:], bexp[:, i, h, 0:P], start=False,
                                                    stop=(i == NPART - 1))
                    last.then_inc(s["se_mm"], 1)

                def values(b, k, h):
                    c, r = h // 4, 32 * (h % 4)
                    if h % 4 == 0:
                        wait(pe, s["o_ev"], 4 * b + c - 1)
                    wait(pe, s["exp_done"], 16 * b + h + 1)
                    nc.tensor.matmul(O[c % 2][r:r + 32, 0:S], V[k][:, 0, h, :], Pr[h % NP][:, 0:S],
                                     start=True, stop=False)
                    nc.tensor.matmul(O[c % 2][r:r + 32, S - K1Q:S], V[k][:, 1, h, :],
                                     Pr[h % NP][:, K0Q:K0Q + K1Q], start=False, stop=True)\
                        .then_inc(s["pv_done"], 1)

                def turn(b, c):
                    wait(pe, s["o_ev"], 4 * b + c + 1)
                    wait(pe, s["cseq"], 3 * (4 * b + c))
                    for t in range(TB):
                        last = nc.tensor.transpose(OT[:, t * P:t * P + P], osb[c % 2][:, t * P:t * P + P], ident[:])
                    last.then_inc(s["ot_mm"], 1)

                uses = {"T": (3, "xt_ready", 1), "K": (3, "qk_ev", 2), "M": (1, "mrow_ready", 1),
                        "Y": (-1, "yt_ev", 1), "V": (3, "v_ready", 2), "R": (-1, "pr_done", 1)}
                order = [u for u in uses if causal or u not in "YR"]

                def claim(use, b):
                    at = order.index(use)
                    for n, u in enumerate(order):
                        off, sem, times = uses[u]
                        done = b + off + (1 if n < at else 0)
                        ahead = 1 if u == "R" else 0
                        if isinstance(b, int):
                            wait(pe, s[sem], times * max(0, min(done, B)) + ahead)
                        elif n == (at - 1) % len(order) or (use == "T" and u == "V"):
                            wait(pe, s[sem], times * done + ahead)

                def step(b, k, a, x_, m, c, p):
                    bb = b + 3
                    if c:
                        wait(pe, s["mpacked"], 16 * (b + 1))
                        wait(pe, s["v_ready"], 2 * (b + 1))
                    for j in range(8):
                        if m and j == 3:
                            wait(pe, s["mp_ready"], b + 2)
                            claim("M", b)
                            for t in range(TB):
                                last = nc.tensor.transpose(
                                    mps[:, t * P:t * P + P],
                                    mparts[(k + 1) % 2][:, t].rearrange("p i h -> p (i h)"), identb[:])
                            last.then_inc(s["mt_mm"], 1)
                        if causal and p and j == 4:
                            wait(pe, s["cseq"], 3 * 4 * b)
                            claim("Y", b)
                            for t in range(TB):
                                last = nc.tensor.transpose(TURN[:, t * P:t * P + P], y[(k + 1) % 2][:, t], ident[:])
                            last.then_inc(s["yt_mm"], 1)
                        if a and j == 5:
                            claim("V", b)
                            for t in range(TB):
                                last = nc.tensor.matmul(TURN[:, t * P:t * P + P], xnT[:, t * P:t * P + P],
                                                        wqkv[:, 2, :], start=True, stop=True)
                            last.then_inc(s["v_mm"], 1)
                        if causal and p and j == 6:
                            wait(pe, s["yt_ev"], b)
                            claim("R", b)
                            for t in range(TB):
                                nc.tensor.matmul(TURN[:, t * P:t * P + P], yT[:, t * P:t * P + P], wproj[:],
                                                 start=True, stop=False)
                                last = nc.tensor.matmul(TURN[:, t * P:t * P + P], res["ones"][0:1, :], bproj[:],
                                                        start=False, stop=True)
                            last.then_inc(s["pr_mm"], 1)
                        if isinstance(b, int) and b == -2 and j == LATE:
                            pe.wait_ge(s["consts"], (BUF if causal else 2 * BUF) * 16)
                            if not causal:
                                pe.wait_ge(bias.placed, 4 * 16)
                        if x_ and j == LATE:
                            wait(pe, s["packed"], 6 * 16 * (b + 3))
                        if (x_ if j >= LATE else m):
                            maxima(slot(b, j)[0], (k + 2 - (j < LATE)) % BUF, slot(b, j)[1])
                        for h in (2 * j, 2 * j + 1):
                            if c:
                                scores(b, k, h)
                                if h >= 2:
                                    values(b, k, h - 2)
                            if p and j == 0:
                                values(b - 1, (k + 3) % BUF, h + H - 2)
                        if a and j == 0:
                            wait(pe, s["xn_ready"], 2 * bb + 2)
                            claim("T", b)
                            for t in range(TB):
                                last = nc.tensor.transpose(TURN[:, t * P:t * P + P], xn[(k + 3) % 2][:, t], ident[:])
                            last.then_inc(s["xn_used"], 1)
                        if a and j == 1:
                            wait(pe, s["xt_ready"], bb + 1)
                            claim("K", b)
                            for i in range(2):
                                last = nc.tensor.matmul(TURN[:, i * S:i * S + S], wqkv[:, i, :], xnT[:],
                                                        start=True, stop=True)
                            last.then_inc(s["qk_mm"], 1)
                        if c and j % 2 == 1 and j > 1:
                            turn(b, (j - 3) // 2)
                        if p and j == 1:
                            turn(b - 1, 3)

                run_steps(pe, step)


def run_steps(eng, step):
    def static(b):
        step(b, b % 4, b + 3 < B, 0 <= b + 2 < B, 0 <= b + 1 < B, 0 <= b < B, b >= 1)

    for b in range(-3, 1):
        static(b)
    with eng.Fori(0, B // 4 - 1) as i:
        for k in range(4):
            step(i * 4 + (k + 1), (k + 1) % 4, True, True, True, True, True)
    for b in range(B - 3, B + 1):
        static(b)


class BiasSetup:

    def __init__(self, nc, sc, w, bmax, bexp, BAND, banks):
        self.nc, self.w, self.bmax, self.bexp, self.BAND = nc, w, bmax, bexp, BAND
        self.NPART, self.N = NPART, N = 3, 512
        self.rel = sc.sb("rel", [32, H])
        self.hot = sc.sb("hot", [32, 3, N])
        self.line = sc.sb("line", [H, 3 * N])
        self.lrest = sc.sb("lrest", [H, 3 * N])
        self.lparts = sc.sb("lparts", [H, NPART, 3 * N], BF16)
        self.lines = nc.dram_tensor(sc.name + "_lines", [NPART, H, 3 * N], BF16, kind="Internal").ap()
        crows = nc.dram_tensor(sc.name + "_crows", [2, NPART, H, S], BF16, kind="Internal").ap()
        self.crows_by_part, self.crows = crows, crows.rearrange("c i h q -> (c i) h q")
        (self.loaded, self.made, self.got, self.seq, self.stored, self.placed, self.crows_stored) = (
            sc.sem("bias_" + n) for n in "loaded made got seq stored placed crows_stored".split())
        self.LP = [bank[0:H, :] for bank in banks]

    def load(self, sp):
        sp.dma_start(self.rel[:], self.w["rel"]).then_inc(self.loaded, 16)
        sp.dma_start(self.hot[:], self.w["hot"]).then_inc(self.loaded, 16)

    def place(self, sp):
        NPART, N, lparts = self.NPART, self.N, self.lparts
        sp.wait_ge(self.seq, 5)
        sp.dma_start(self.lines.rearrange("i h n -> h i n"), lparts[:]).then_inc(self.stored, 16)
        for i in range(NPART):
            sp.dma_start(self.crows_by_part[:, i].rearrange("c h q -> h c q"),
                         lparts[:, i, 2 * N:3 * N].rearrange("h (c q) -> h c q", c=2)).then_inc(self.crows_stored, 16)
        sp.wait_ge(self.stored, 16)
        sp.dma_start(self.bmax[:], bass.AP(self.lines.tensor, N,
                                           [[1, P], [3 * N, H], [1, 3 * P]])).then_inc(self.placed, 16)
        for i in range(NPART):
            sp.dma_start(self.bexp[:, i], bass.AP(self.lines.tensor, i * H * 3 * N + S - P,
                                                  [[1, P], [3 * N, H], [1, self.BAND]])).then_inc(self.placed, 16)

    def look_up(self, pe):
        pe.wait_ge(self.loaded, 32)
        for i in range(3):
            self.nc.tensor.matmul(self.LP[i], self.rel[:], self.hot[:, i, :], start=True, stop=True)\
                .then_inc(self.made, 1)

    def split(self, v):
        N, line, lrest, lparts, seq = self.N, self.line, self.lrest, self.lparts, self.seq
        vector = self.nc.vector
        v.wait_ge(self.made, 3)
        for i in range(3):
            vector.tensor_copy(line[:, i * N:i * N + N], self.LP[i]).then_inc(self.got, 1)
        v.wait_ge(self.got, 3)
        vector.tensor_copy(lparts[:, 0], line[:]).then_inc(seq, 1)
        v.wait_ge(seq, 1)
        vector.tensor_tensor(lrest[:], line[:], lparts[:, 0], ALU.subtract).then_inc(seq, 1)
        v.wait_ge(seq, 2)
        vector.tensor_copy(lparts[:, 1], lrest[:]).then_inc(seq, 1)
        v.wait_ge(seq, 3)
        vector.tensor_tensor(line[:], lrest[:], lparts[:, 1], ALU.subtract).then_inc(seq, 1)
        v.wait_ge(seq, 4)
        vector.tensor_copy(lparts[:, 2], line[:]).then_inc(seq, 1)


def bucket(n):
    n = max(n, 0)
    return n if n < 16 else min(16 + int(math.log(n / 16) / math.log(2) * 16), 31)


def attention_constants():
    bf = HOST_BF16
    n = 512
    hot = np.zeros((32, 3, n), np.float32)
    for c in range(2 * S - 1):
        hot[bucket(c - (S - 1)), 0, c] = 1.0
        hot[bucket((S - 1) - c), 1, c] = 1.0
    hot[31, 2, 160:S] = 1.0
    hot[0, 2, S:S + P] = 1.0
    krows = np.zeros((9, H, S), bf)
    krows[0:3] = 1.0
    krows[3:6, :, 0:P] = 1.0
    krows[6:9, :, P:] = 1.0
    keep = np.tril(np.ones((P, P), bool))
    maskq = np.where(keep, 0.0, -1e30).astype(bf)
    return {"hot": hot, "krows": krows, "maskq": maskq, "maskk": np.ascontiguousarray(maskq.T),
            "ident": np.eye(P, dtype=np.float32), "identb": np.eye(P, dtype=bf),
            "flip": np.ascontiguousarray(np.eye(P, dtype=bf)[::-1])}



def normed(nc, v, res, out, g, rstd, inc):
    for t in range(G):
        nc.vector.tensor_scalar(out[:, t], res["x"][:, G * g + t], res["mean"][:, bass.ds(G * g + t, 1)],
                                rstd[:, bass.ds(G * g + t, 1)], ALU.subtract, ALU.mult).then_inc(inc, 1)


def row_stats(nc, res, g):
    for t in range(G):
        nc.vector.bn_stats(res["stats"][:, G * g + t, :], res["x"][:, G * g + t, :])


def ternary_ffn(nc, res, name, w):
    x, ident = res["x"], res["ident"]
    C = 4
    norm_factors(nc, res, name + "n", then="rms")
    with ExitStack() as ctx:
        sc = Scope(nc, ctx, name)
        wu, wd = sc.sb("wu", [P, C, P]), sc.sb("wd", [P, C, P])
        quantize(nc, res, name, w, wu, wd)
        half = sc.sb("half", [P, G])
        xn = [sc.sb(f"xn{i}", [P, G, D]) for i in range(2)]
        xnT = [sc.sb(f"xnT{i}", [P, GT]) for i in range(2)]
        hT = [sc.sb(f"hT{i}", [P, C, GT]) for i in range(2)]
        sq = [sc.sb(f"sq{i}", [P, C, GT]) for i in range(2)]
        ssum = sc.sb("ssum", [P, GT])
        ms, rms, inv = sc.sb("ms", [P, G]), sc.sb("rms", [P, G]), sc.sb("inv", [P, G])
        T = sc.ps("T", [P, GT])
        U = [sc.ps(f"U{i}", [P, GT]) for i in range(3)]
        OUT = [sc.ps(f"OUT{i}", [P, G, D]) for i in range(2)]
        SS = sc.ps("SS", [P, 512])
        xn_ready, xn_used, xt_ready, up_mm, gelu, sq_done, ss_mm, ms_ready, rms_ready, inv_ready, down_mm, added, half_ready, summed = (
            sc.sem(n) for n in "xn_ready xn_used xt_ready up_mm gelu sq_done ss_mm ms_ready rms_ready inv_ready down_mm added half_ready summed".split())
        block = ctx.enter_context(nc.Block())

        @block.vector
        def _(v):
            nc.vector.memset(half[:], 0.5).then_inc(half_ready, 1)

            def step(g, k, on):
                if on(0):
                    wait(v, sq_done, C * (g + 1))
                    nc.vector.tensor_tensor(sq[k][:, 0:2], sq[k][:, 0:2], sq[k][:, 2:4], ALU.add).then_inc(summed, 1)
                    wait(v, summed, 2 * g + 1)
                    nc.vector.tensor_tensor(ssum[:], sq[k][:, 0], sq[k][:, 1], ALU.add).then_inc(summed, 1)
                    wait(v, ss_mm, g + 1)
                    nc.vector.tensor_scalar(ms[:], SS[:, 0:G], 1.0 / (C * P), None, ALU.mult).then_inc(ms_ready, 1)
                    wait(v, rms_ready, g + 1)
                    nc.vector.tensor_scalar(ms[:], rms[:], 1e-8, None, ALU.add).then_inc(inv_ready, 1)
                    wait(v, inv_ready, 2 * g + 1)
                    nc.vector.reciprocal(inv[:], ms[:]).then_inc(inv_ready, 1)
                if on(3):
                    wait(v, xn_used, g + 2)
                    normed(nc, v, res, xn[(k + 1) % 2], g + 3, res["rstd2"], xn_ready)
                if on(0):
                    wait(v, inv_ready, 2 * g + 2)
                    wait(v, down_mm, g + 1)
                    for t in range(G):
                        xs = x[:, G * g + t]
                        nc.vector.scalar_tensor_tensor(out=xs, in0=OUT[k][:, t], scalar=inv[:, t:t + 1], in1=xs,
                                                       op0=ALU.mult, op1=ALU.add).then_inc(added, 1)
                    wait(v, added, G * (g + 1))
                    row_stats(nc, res, g)

            pipeline(v, step, GROUPS, 3)

        @block.gpsimd
        def _(q):
            q.wait_ge(half_ready, 1)

            def step(g, k, on):
                if on(1):
                    wait(q, summed, 2 * g)
                    for c in range(C):
                        h = hT[(k + 1) % 2][:, c]
                        wait(q, gelu, C * (g + 1) + c + 1)
                        nc.gpsimd.tensor_tensor(sq[(k + 1) % 2][:, c], h, h, ALU.mult).then_inc(sq_done, 1)
                if on(0):
                    wait(q, ms_ready, g + 1)
                    nc.gpsimd.tensor_tensor(rms[:], ms[:], half[:], ALU.pow).then_inc(rms_ready, 1)

            pipeline(q, step, GROUPS, 2)

        @block.scalar
        def _(act):
            def step(g, k, on):
                if on(2):
                    wait(act, xn_used, g + 3)
                    wait(act, up_mm, C * (g + 1))
                    nc.scalar.activation(xnT[k][:], T[:], ACT.Copy).then_inc(xt_ready, 1)
                if on(1):
                    wait(act, sq_done, C * g)
                    wait(act, down_mm, g)
                    for c in range(C):
                        n = C * (g + 1) + c
                        wait(act, up_mm, n + 1)
                        nc.scalar.activation(hT[(k + 1) % 2][:, c], U[(C * (k + 1) + c) % 2][:],
                                             ACT.Gelu).then_inc(gelu, 1)

            pipeline(act, step, GROUPS, 2)

        @block.tensor
        def _(pe):
            def step(g, k, on):
                if on(2):
                    wait(pe, xn_ready, G * (g + 3))
                    wait(pe, xt_ready, g + 2)
                    for t in range(G):
                        last = nc.tensor.transpose(T[:, t * P:t * P + P], xn[k][:, t], ident[:])
                    last.then_inc(xn_used, 1)
                if on(1):
                    wait(pe, xt_ready, g + 2)
                    for c in range(C):
                        n = C * (g + 1) + c
                        wait(pe, gelu, n - 1)
                        nc.tensor.matmul(U[(C * (k + 1) + c) % 2][:], wu[:, c], xnT[(k + 1) % 2][:],
                                         start=True, stop=True).then_inc(up_mm, 1)
                if on(0):
                    wait(pe, summed, 2 * g + 2)
                    wait(pe, ms_ready, g)
                    for t in range(G):
                        last = nc.tensor.matmul(SS[:, t:t + 1], ssum[:, t * P:t * P + P], res["ones"][:, 0:1],
                                                start=True, stop=True)
                    last.then_inc(ss_mm, 1)
                    wait(pe, added, G * (g - 1))
                    for t in range(G):
                        for c in range(C):
                            last = nc.tensor.matmul(OUT[k][:, t], hT[k][:, c, t * P:t * P + P], wd[:, c],
                                                    start=(c == 0), stop=(c == C - 1))
                    last.then_inc(down_mm, 1)

            pipeline(pe, step, GROUPS, 2)


def quantize(nc, res, name, w, wu, wd):
    with ExitStack() as ctx:
        tmp = Scope(nc, ctx, name + "q")
        ab = tmp.sb("ab", [P, 512])
        total, thr = tmp.sb("total", [P, 2]), tmp.sb("thr", [P, 2, 2])
        above, below = tmp.sb("above", [P, 2, 512]), tmp.sb("below", [P, 2, 512])
        TT = tmp.ps("TT", [P, 512])
        loaded, summed, spread, seq = (tmp.sem(n) for n in "loaded summed spread seq".split())
        block = ctx.enter_context(nc.Block())
        both = (wu, wd)

        @block.sync
        def _(sp):
            sp.dma_start(wu[:], w["up"]).then_inc(loaded, 16)
            sp.dma_start(wd[:], w["down"]).then_inc(loaded, 16)

        @block.scalar
        def _(act):
            act.wait_ge(loaded, 32)
            for i in range(2):
                nc.scalar.activation(ab[:], both[i][:].rearrange("p c n -> p (c n)"), ACT.Abs,
                                     accum_out=total[:, i:i + 1]).then_inc(summed, 1)
                act.wait_ge(summed, i + 1)

        @block.tensor
        def _(pe):
            pe.wait_ge(summed, 2)
            nc.tensor.matmul(TT[:, 0:2], res["ones"][:], total[:], start=True, stop=True).then_inc(spread, 1)

        @block.vector
        def _(v):
            n = 0
            v.wait_ge(spread, 1)
            for sgn in range(2):
                nc.vector.tensor_scalar(thr[:, sgn], TT[:, 0:2], (0.5 - sgn) / (P * 512), None, ALU.mult).then_inc(seq, 1)
                n += 1
            v.wait_ge(seq, n)
            for i in range(2):
                wf = both[i][:].rearrange("p c n -> p (c n)")
                nc.vector.tensor_scalar(above[:, i], wf, thr[:, 0, i:i + 1], None, ALU.is_gt).then_inc(seq, 1)
                nc.vector.tensor_scalar(below[:, i], wf, thr[:, 1, i:i + 1], None, ALU.is_lt).then_inc(seq, 1)
            v.wait_ge(seq, n + 4)
            nc.vector.tensor_tensor(above[:], above[:], below[:], ALU.subtract).then_inc(seq, 1)
            v.wait_ge(seq, n + 5)
            for i in range(2):
                wf = both[i][:].rearrange("p c n -> p (c n)")
                nc.vector.tensor_tensor(below[:, i], above[:, i], wf, ALU.subtract).then_inc(seq, 1)
            v.wait_ge(seq, n + 7)
            for i in range(2):
                wf = both[i][:].rearrange("p c n -> p (c n)")
                nc.vector.tensor_tensor(wf, wf, below[:, i], ALU.add)


def lowrank_ffn(nc, res, name, w, out):
    x, ident = res["x"], res["ident"]
    C, R = 4, 32
    norm_factors(nc, res, name + "n")
    with ExitStack() as ctx:
        sc = Scope(nc, ctx, name)
        u1 = sc.sb("u1", [P, P])
        v1 = sc.sb("v1", [P, C * P])
        u2 = sc.sb("u2", [P, C, P])
        v2 = sc.sb("v2", [P, P])
        b1 = sc.sb("b1", [P, C])
        b2 = sc.sb("b2", [1, P])
        xn = [sc.sb(f"xn{i}", [P, G, D]) for i in range(2)]
        xnT = sc.sb("xnT", [P, GT])
        pT, qT = sc.sb("pT", [P, GT]), sc.sb("qT", [P, GT])
        hT = [sc.sb(f"hT{i}", [P, C, GT]) for i in range(2)]
        T = sc.ps("T", [P, GT])
        PP, QQ = sc.ps("PP", [P, GT]), sc.ps("QQ", [P, GT])
        U = [sc.ps(f"U{i}", [P, GT]) for i in range(3)]
        OUT = sc.ps("OUT", [P, G, D])
        loaded, xn_ready, xn_used, xt_ready, p_mm, p_ready, up_mm, gelu, q_mm, q_ready, out_mm, added, stored = (
            sc.sem(n) for n in "loaded xn_ready xn_used xt_ready p_mm p_ready up_mm gelu q_mm q_ready out_mm added stored".split())
        block = ctx.enter_context(nc.Block())
        loads = [(u1, "u1"), (v1, "v1"), (u2, "u2"), (v2, "v2"), (b1, "b1"), (b2, "b2")]

        @block.sync
        def _(sp):
            for dst, n in loads:
                sp.dma_start(dst[:], w[n]).then_inc(loaded, 16)
            rows = out.rearrange("b (t p) d -> p (b t) d", p=P)
            for g in range(GROUPS):
                sp.wait_ge(added, g + 1)
                sp.dma_start(rows[:, G * g:G * g + G], x[:, G * g:G * g + G]).then_inc(stored, 16)
            sp.wait_ge(stored, GROUPS * 16)

        @block.vector
        def _(v):
            def step(g, k, on):
                if on(1):
                    wait(v, p_mm, g + 2)
                    wait(v, up_mm, C * (g + 1))
                    nc.vector.tensor_copy(pT[:], PP[:]).then_inc(p_ready, 1)
                if on(0):
                    wait(v, q_mm, g + 1)
                    wait(v, out_mm, g)
                    nc.vector.tensor_copy(qT[:], QQ[:]).then_inc(q_ready, 1)
                if on(3):
                    wait(v, xn_used, g + 2)
                    normed(nc, v, res, xn[(k + 1) % 2], g + 3, res["rstd"], xn_ready)
                if on(0):
                    wait(v, out_mm, g + 1)
                    xs = x[:, bass.ds(G * g, G), :]
                    nc.vector.tensor_tensor(xs, xs, OUT[:], ALU.add).then_inc(added, 1)

            pipeline(v, step, GROUPS, 3)

        @block.scalar
        def _(act):
            act.wait_ge(loaded, 16 * len(loads))

            def step(g, k, on):
                if on(2):
                    wait(act, xn_used, g + 3)
                    wait(act, p_mm, g + 2)
                    nc.scalar.activation(xnT[:], T[:], ACT.Copy).then_inc(xt_ready, 1)
                if on(1):
                    wait(act, q_mm, g)
                    for c in range(C):
                        n = C * (g + 1) + c
                        wait(act, up_mm, n + 1)
                        nc.scalar.activation(hT[(k + 1) % 2][:, c], U[c % 2][:], ACT.Gelu_apprx_tanh,
                                             bias=b1[:, c:c + 1]).then_inc(gelu, 1)

            pipeline(act, step, GROUPS, 2)

        @block.tensor
        def _(pe):
            pe.wait_ge(loaded, 16 * len(loads))

            def step(g, k, on):
                if on(1):
                    wait(pe, xt_ready, g + 2)
                    wait(pe, p_ready, g + 1)
                    nc.tensor.matmul(PP[:], u1[:], xnT[:], start=True, stop=True).then_inc(p_mm, 1)
                if on(2):
                    wait(pe, xn_ready, G * (g + 3))
                    wait(pe, xt_ready, g + 2)
                    for t in range(G):
                        last = nc.tensor.transpose(T[:, t * P:t * P + P], xn[k][:, t], ident[:])
                    last.then_inc(xn_used, 1)
                if on(0):
                    wait(pe, gelu, C * (g + 1))
                    wait(pe, q_ready, g)
                    for c in range(C):
                        last = nc.tensor.matmul(QQ[:], u2[:, c], hT[k][:, c], start=(c == 0), stop=(c == C - 1))
                    last.then_inc(q_mm, 1)
                if on(1):
                    wait(pe, p_ready, g + 2)
                    for c in range(C):
                        n = C * (g + 1) + c
                        wait(pe, gelu, n - 1)
                        nc.tensor.matmul(U[c % 2][:], v1[:, c * P:c * P + P], pT[:],
                                         start=True, stop=True).then_inc(up_mm, 1)
                if on(0):
                    wait(pe, q_ready, g + 1)
                    wait(pe, added, g)
                    for t in range(G):
                        nc.tensor.matmul(OUT[:, t], qT[:, t * P:t * P + P], v2[:], start=True, stop=False)
                        last = nc.tensor.matmul(OUT[:, t], res["ones"][0:1, :], b2[:], start=False, stop=True)
                    last.then_inc(out_mm, 1)

            pipeline(pe, step, GROUPS, 2)



def min_gru(nc, res, name, w):
    x, ident = res["x"], res["ident"]
    NB = GT // S
    norm_factors(nc, res, name + "n")
    with ExitStack() as ctx:
        sc = Scope(nc, ctx, name)
        wz, wh = sc.sb("wz", [P, P]), sc.sb("wh", [P, P])
        bz, bh, swish = sc.sb("bz", [P, 1]), sc.sb("bh", [P, 1]), sc.sb("swish", [P, 1])
        nbz = sc.sb("nbz", [P, 1])
        gamma, beta = sc.sb("gamma", [P, G, P]), sc.sb("beta", [P, G, P])
        xn = [sc.sb(f"xn{i}", [P, G, D]) for i in range(2)]
        xnT = sc.sb("xnT", [P, GT])
        keep, gate = ([sc.sb(f"{n}{i}", [P, GT]) for i in range(2)] for n in ("keep", "gate"))
        new, h, sg = sc.sb("new", [P, GT]), sc.sb("h", [P, GT]), sc.sb("sg", [P, GT])
        yT = [sc.sb(f"yT{i}", [P, GT]) for i in range(2)]
        st, mv = sc.sb("st", [P, G, 6]), sc.sb("mv", [P, G, 2])
        ve, root, power = sc.sb("ve", [P, G]), sc.sb("root", [P, G]), sc.sb("power", [P, G])
        yn, yg = sc.sb("yn", [P, G, P]), sc.sb("yg", [P, G, P])
        T = sc.ps("T", [P, GT])
        Z, HH = ([sc.ps(f"{n}{i}", [P, GT]) for i in range(2)] for n in ("Z", "HH"))
        Y = [sc.ps(f"Y{i}", [P, G, P]) for i in range(2)]
        names = "loaded nb xn_ready xn_used xt_ready z_mm h_mm gates swished seq y_ready turned vseq ve_ready root_ready yn_ready yg_ready added".split()
        (loaded, nb, xn_ready, xn_used, xt_ready, z_mm, h_mm, gates, swished, seq, y_ready, turned, vseq, ve_ready, root_ready,
         yn_ready, yg_ready, added) = (sc.sem(n) for n in names)
        block = ctx.enter_context(nc.Block())
        loads = [(wz, "wz"), (wh, "wh"), (bz, "bz"), (bh, "bh"), (swish, "swish"), (gamma, "gamma"), (beta, "beta")]

        @block.sync
        def _(sp):
            for dst, n in loads:
                sp.dma_start(dst[:], w[n]).then_inc(loaded, 16)

        @block.scalar
        def _(act):
            act.wait_ge(nb, 2)

            def step(g, k, on):
                if on(2):
                    wait(act, xn_used, g + 3)
                    wait(act, h_mm, g + 2)
                    nc.scalar.activation(xnT[:], T[:], ACT.Copy).then_inc(xt_ready, 1)
                if on(1):
                    wait(act, seq, 3 * (g + 1) + 3)
                    nc.scalar.activation(sg[:], h[:], ACT.Sigmoid, scale=swish[:]).then_inc(swished, 1)
                if on(2):
                    wait(act, z_mm, g + 3)
                    wait(act, y_ready, g + 1)
                    nc.scalar.activation(keep[k][:], Z[k][:], ACT.Sigmoid, bias=nbz[:], scale=-1.0).then_inc(gates, 1)
                    nc.scalar.activation(gate[k][:], Z[k][:], ACT.Sigmoid, bias=bz[:]).then_inc(gates, 1)

            pipeline(act, step, GROUPS, 2)

        @block.gpsimd
        def _(q):
            q.wait_ge(nb, 2)

            def step(g, k, on):
                if on(0):
                    wait(q, ve_ready, g + 1)
                    nc.gpsimd.tensor_tensor(root[:], ve[:], power[:], ALU.pow).then_inc(root_ready, 1)
                    wait(q, yn_ready, G * (g + 1))
                    nc.gpsimd.tensor_tensor(yg[:], yn[:], gamma[:], ALU.mult).then_inc(yg_ready, 1)
                    wait(q, yg_ready, 2 * g + 1)
                    nc.gpsimd.tensor_tensor(yg[:], yg[:], beta[:], ALU.add).then_inc(yg_ready, 1)

            pipeline(q, step, GROUPS, 2)

        @block.vector
        def _(v):
            nc.vector.memset(power[:], -0.5).then_inc(nb, 1)
            v.wait_ge(loaded, 16 * len(loads))
            nc.vector.tensor_scalar(nbz[:], bz[:], -1.0, None, ALU.mult).then_inc(nb, 1)
            v.wait_ge(nb, 2)

            def step(g, k, on):
                if on(2):
                    wait(v, xn_used, g + 1)
                    normed(nc, v, res, xn[k], g + 2, res["rstd"], xn_ready)
                if on(1):
                    n, j = 3 * (g + 1), (k + 1) % 2
                    wait(v, gates, 2 * (g + 2))
                    nc.vector.memset(keep[j][:].rearrange("p (b s) -> p b s", b=NB)[:, :, 0:1], 0.0).then_inc(seq, 1)
                    wait(v, h_mm, g + 2)
                    nc.vector.scalar_tensor_tensor(out=new[:], in0=HH[j][:], scalar=bh[:], in1=gate[j][:],
                                                   op0=ALU.add, op1=ALU.mult).then_inc(seq, 1)
                    wait(v, seq, n + 2)
                    nc.vector.tensor_tensor_scan(h[:], keep[j][:], new[:], 0.0, ALU.mult, ALU.add).then_inc(seq, 1)
                if on(-1):
                    wait(v, yg_ready, 2 * g)
                    xs = x[:, bass.ds(G * (g - 1), G), :]
                    nc.vector.tensor_tensor(xs, xs, yg[:], ALU.add).then_inc(added, 1)
                if on(0):
                    wait(v, turned, g + 1)
                    for t in range(G):
                        nc.vector.bn_stats(st[:, t], Y[k][:, t]).then_inc(vseq, 1)
                    wait(v, vseq, 2 * G * g + G)
                    nc.vector.memset(ve[:], 0.0)
                    for t in range(G):
                        nc.vector.bn_aggr(mv[:, t], st[:, t]).then_inc(vseq, 1)
                    wait(v, vseq, 2 * G * (g + 1))
                    nc.vector.tensor_scalar(ve[:], mv[:, :, 1], EPS, None, ALU.add).then_inc(ve_ready, 1)
                if on(-1):
                    wait(v, added, g)
                    row_stats(nc, res, g - 1)
                if on(1):
                    wait(v, swished, g + 2)
                    wait(v, turned, g)
                    nc.vector.scalar_tensor_tensor(out=yT[(k + 1) % 2][:], in0=h[:], scalar=swish[:], in1=sg[:],
                                                   op0=ALU.mult, op1=ALU.mult).then_inc(y_ready, 1)
                if on(0):
                    wait(v, root_ready, g + 1)
                    wait(v, yg_ready, 2 * g)
                    for t in range(G):
                        nc.vector.tensor_scalar(yn[:, t], Y[k][:, t], mv[:, t, 0:1], root[:, t:t + 1],
                                                ALU.subtract, ALU.mult).then_inc(yn_ready, 1)

            pipeline(v, step, GROUPS, 2, back=1)

        @block.tensor
        def _(pe):
            pe.wait_ge(loaded, 16 * len(loads))

            def step(g, k, on):
                if on(2):
                    wait(pe, xn_ready, G * (g + 3))
                    wait(pe, xt_ready, g + 2)
                    for t in range(G):
                        last = nc.tensor.transpose(T[:, t * P:t * P + P], xn[k][:, t], ident[:])
                    last.then_inc(xn_used, 1)
                    wait(pe, xt_ready, g + 3)
                    wait(pe, gates, 2 * (g + 1))
                    nc.tensor.matmul(Z[k][:], wz[:], xnT[:], start=True, stop=True).then_inc(z_mm, 1)
                    wait(pe, seq, 3 * g + 2)
                    nc.tensor.matmul(HH[k][:], wh[:], xnT[:], start=True, stop=True).then_inc(h_mm, 1)
                if on(1):
                    wait(pe, y_ready, g + 2)
                    wait(pe, yn_ready, G * g)
                    for t in range(G):
                        last = nc.tensor.transpose(Y[(k + 1) % 2][:, t], yT[(k + 1) % 2][:, t * P:t * P + P], ident[:])
                    last.then_inc(turned, 1)

            pipeline(pe, step, GROUPS, 2)


def expert_choice(nc, res, name, w):
    x, ident = res["x"], res["ident"]
    E, C = 8, 4
    K = 2 * TILES * P // E
    norm_factors(nc, res, name + "n")
    with ExitStack() as outer:
        so = Scope(nc, outer, name)
        wts = so.sb("wts", [P, TILES, E])
        w1, w2 = so.sb("w1", [P, E, C * P]), so.sb("w2", [P, E, C, P])
        b1, b2 = so.sb("b1", [P, E, C]), so.sb("b2", [1, E, P])
        big = so.sem("big")
        router_scores(nc, res, so, name, w, wts, E, lambda sp: [
            sp.dma_start(dst[:], w[n]).then_inc(big, 16) for dst, n in ((w1, "w1"), (w2, "w2"), (b1, "b1"), (b2, "b2"))])
        choose(nc, res, name, w, wts, E, K)
        with ExitStack() as ctx:
            sc = Scope(nc, ctx, name + "e")
            xn = sc.sb("xn", [P, G, D])
            xnT = [sc.sb(f"xnT{i}", [P, GT]) for i in range(2)]
            hT = [sc.sb(f"hT{i}", [P, C, GT]) for i in range(2)]
            part = [sc.sb(f"part{i}", [1, E, P], BF16) for i in range(3)]
            brest = sc.sb("brest", [1, E, P])
            b2p, onesb = sc.sb("b2p", [3, E, P], BF16), sc.sb("onesb", [3, P], BF16)
            T = sc.ps("T", [P, GT])
            U = [sc.ps(f"U{i}", [P, GT]) for i in range(3)]
            OUT = [sc.ps(f"OUT{i}", [P, G, D]) for i in range(2)]
            xn_ready, xn_used, xt_ready, up_mm, gelu, down_mm, added, bsplit, bias_ready = (
                sc.sem(n) for n in "xn_ready xn_used xt_ready up_mm gelu down_mm added bsplit bias_ready".split())
            block = ctx.enter_context(nc.Block())

            @block.sync
            def _(sp):
                sp.wait_ge(bsplit, 5)
                for i in range(3):
                    sp.dma_start(b2p[i:i + 1], part[i][:]).then_inc(bias_ready, 16)

            @block.vector
            def _(v):
                v.wait_ge(big, 64)

                def norm_group(g):
                    wait(v, xn_used, g)
                    normed(nc, v, res, xn, g, res["rstd"], xn_ready)

                norm_group(0)
                nc.vector.memset(onesb[:], 1.0).then_inc(bsplit, 1)
                nc.vector.tensor_copy(part[0][:], b2[:]).then_inc(bsplit, 1)
                v.wait_ge(bsplit, 2)
                nc.vector.tensor_tensor(brest[:], b2[:], part[0][:], ALU.subtract).then_inc(bsplit, 1)
                v.wait_ge(bsplit, 3)
                nc.vector.tensor_copy(part[1][:], brest[:]).then_inc(bsplit, 1)
                v.wait_ge(bsplit, 4)
                nc.vector.tensor_tensor(part[2][:], brest[:], part[1][:], ALU.subtract).then_inc(bsplit, 1)

                def step(g, j, e, more, nxt):
                    n = g * E + e
                    if e == 2 and more:
                        norm_group(g + 1)
                    wait(v, down_mm, n + 1)
                    wait(v, added, n * G)
                    for t in range(G):
                        xs = x[:, g * G + t]
                        nc.vector.scalar_tensor_tensor(out=xs, in0=OUT[e % 2][:, t],
                                                       scalar=wts[:, g * G + t, e:e + 1], in1=xs,
                                                       op0=ALU.mult, op1=ALU.add).then_inc(added, 1)
                    if e == E - 1:
                        wait(v, added, n * G + G)
                        row_stats(nc, res, g)

                by_group(v, step, GROUPS, E)

            @block.scalar
            def _(act):
                def evac(g, j):
                    wait(act, xn_used, g + 1)
                    wait(act, up_mm, g * (E * C) - E * C)
                    nc.scalar.activation(xnT[j][:], T[:], ACT.Copy).then_inc(xt_ready, 1)

                def gelus(g, e):
                    n = g * E + e
                    wait(act, down_mm, n - 1)
                    for c in range(C):
                        wait(act, up_mm, n * C + (c + 1))
                        nc.scalar.activation(hT[e % 2][:, c], U[c % 2][:], ACT.Gelu,
                                             bias=b1[:, e, c:c + 1]).then_inc(gelu, 1)

                evac(0, 0)
                gelus(0, 0)

                def step(g, j, e, more, nxt):
                    if e == 2 and more:
                        evac(g + 1, 1 - j)
                    if nxt:
                        gelus(nxt[0], nxt[2])

                by_group(act, step, GROUPS, E)

            @block.tensor
            def _(pe):
                def turn(g):
                    wait(pe, xn_ready, g * G + G)
                    wait(pe, xt_ready, g)
                    for t in range(G):
                        last = nc.tensor.transpose(T[:, t * P:t * P + P], xn[:, t], ident[:])
                    last.then_inc(xn_used, 1)

                def up(g, j, e):
                    n = g * E + e
                    if e == 0:
                        wait(pe, xt_ready, g + 1)
                    for c in range(C):
                        wait(pe, gelu, n * C + (c - 1))
                        nc.tensor.matmul(U[c % 2][:], w1[:, e, c * P:c * P + P], xnT[j][:],
                                         start=True, stop=True).then_inc(up_mm, 1)

                turn(0)
                up(0, 0, 0)
                pe.wait_ge(bias_ready, 3 * 16)

                def step(g, j, e, more, nxt):
                    n = g * E + e
                    if e == 2 and more:
                        turn(g + 1)
                    if nxt:
                        up(*nxt)
                    wait(pe, gelu, n * C + C)
                    wait(pe, added, n * G - G)
                    nc.tensor.matmul(OUT[e % 2][:], onesb[:], b2p[:, e:e + 1].to_broadcast([3, G, P]),
                                     start=True, stop=False)
                    for t in range(G):
                        for c in range(C):
                            last = nc.tensor.matmul(OUT[e % 2][:, t], hT[e % 2][:, c, t * P:t * P + P], w2[:, e, c],
                                                    start=False, stop=(t == G - 1 and c == C - 1))
                    last.then_inc(down_mm, 1)

                by_group(pe, step, GROUPS, E)


def by_group(eng, step, groups, items):
    def group(g, j, more):
        for e in range(items):
            nxt = (g, j, e + 1) if e + 1 < items else (g + 1, 1 - j, 0) if more else None
            step(g, j, e, more, nxt)

    group(0, 0, True)
    group(1, 1, True)
    with eng.Fori(1, groups // 2 - 1) as i:
        group(i * 2, 0, True)
        group(i * 2 + 1, 1, True)
    group(groups - 2, 0, True)
    group(groups - 1, 1, False)


def router_scores(nc, res, so, name, w, wts, E, loads):
    x, ident = res["x"], res["ident"]
    with ExitStack() as ctx:
        sc = Scope(nc, ctx, name + "r")
        wr = sc.sb("wr", [P, E])
        xn = [sc.sb(f"xn{i}", [P, G, D]) for i in range(2)]
        xnT = [sc.sb(f"xnT{i}", [P, GT]) for i in range(2)]
        top, tot = sc.sb("top", [P, TILES]), sc.sb("tot", [P, TILES])
        T = [sc.ps(f"T{i}", [P, GT]) for i in range(2)]
        LG = [sc.ps(f"LG{i}", [P, 512]) for i in range(2)]
        loaded, xn_ready, xn_used, xt_ready, lg_mm, copied, seq, exped = (
            sc.sem(n) for n in "loaded xn_ready xn_used xt_ready lg_mm copied seq exped".split())
        block = ctx.enter_context(nc.Block())

        @block.sync
        def _(sp):
            sp.dma_start(wr[:], w["wr"]).then_inc(loaded, 16)
            loads(sp)

        @block.scalar
        def _(act):
            def step(g, k, on):
                if on(1):
                    wait(act, xn_used, g + 2)
                    wait(act, lg_mm, g)
                    nc.scalar.activation(xnT[(k + 1) % 2][:], T[(k + 1) % 2][:], ACT.Copy).then_inc(xt_ready, 1)

            pipeline(act, step, GROUPS, 2)
            act.wait_ge(seq, 2)
            nc.scalar.activation(wts[:], wts[:], ACT.Exp).then_inc(exped, 1)

        @block.tensor
        def _(pe):
            pe.wait_ge(loaded, 16)

            def step(g, k, on):
                if on(1):
                    wait(pe, xn_ready, G * (g + 2))
                    wait(pe, xt_ready, g)
                    for t in range(G):
                        last = nc.tensor.transpose(T[(k + 1) % 2][:, t * P:t * P + P], xn[(k + 1) % 2][:, t], ident[:])
                    last.then_inc(xn_used, 1)
                if on(0):
                    wait(pe, xt_ready, g + 1)
                    wait(pe, copied, g - 1)
                    for t in range(G):
                        last = nc.tensor.matmul(LG[k][:, t * E:t * E + E], xnT[k][:, t * P:t * P + P], wr[:],
                                                start=True, stop=True)
                    last.then_inc(lg_mm, 1)

            pipeline(pe, step, GROUPS, 2)

        @block.vector
        def _(v):
            def step(g, k, on):
                if on(2):
                    wait(v, xn_used, g + 1)
                    normed(nc, v, res, xn[k], g + 2, res["rstd"], xn_ready)
                if on(0):
                    wait(v, lg_mm, g + 1)
                    nc.vector.tensor_copy(wts[:, bass.ds(g * G, G), :],
                                          LG[k][:, 0:G * E].rearrange("p (t e) -> p t e", t=G)).then_inc(copied, 1)

            pipeline(v, step, GROUPS, 2)
            v.wait_ge(copied, GROUPS)
            shape = [P, TILES, E]
            nc.vector.tensor_reduce(top[:], wts[:], AX.X, ALU.max).then_inc(seq, 1)
            v.wait_ge(seq, 1)
            nc.vector.tensor_tensor(wts[:], wts[:], top[:].unsqueeze(2).to_broadcast(shape), ALU.subtract).then_inc(seq, 1)
            v.wait_ge(exped, 1)
            nc.vector.tensor_reduce(tot[:], wts[:], AX.X, ALU.add).then_inc(seq, 1)
            v.wait_ge(seq, 3)
            nc.vector.reciprocal(top[:], tot[:]).then_inc(seq, 1)
            v.wait_ge(seq, 4)
            nc.vector.tensor_tensor(wts[:], wts[:], top[:].unsqueeze(2).to_broadcast(shape), ALU.mult)


def choose(nc, res, name, w, wts, E, K):
    BL = TILES * E // P
    U32 = mybir.dt.uint32
    with ExitStack() as ctx:
        sc = Scope(nc, ctx, name + "c")
        same, before = sc.sb("same", [P, P]), sc.sb("before", [P, P])
        s, junk, eq, pre = (sc.sb(n, [P, BL, P]) for n in ("s", "junk", "eq", "pre"))
        kth, cand, mask = (sc.sb(n, [P, 1], U32) for n in ("kth", "cand", "mask"))
        cnt, need = sc.sb("cnt", [P, 1]), sc.sb("need", [P, 1])
        ceq, cbef, lim = (sc.sb(n, [P, BL]) for n in ("ceq", "cbef", "lim"))
        TT, CT, BT = sc.ps("TT", [P, BL, P]), sc.ps("CT", [P, 512]), sc.ps("BT", [P, BL, P])
        loaded, turned, seq, counted, total, off_mm, chosen, back = (
            sc.sem(n) for n in "loaded turned seq counted total off_mm chosen back".split())
        block = ctx.enter_context(nc.Block())
        tiles = TILES // BL
        BITS = 30

        @block.sync
        def _(sp):
            sp.dma_start(same[:], w["same"]).then_inc(loaded, 16)
            sp.dma_start(before[:], w["before"]).then_inc(loaded, 16)

        @block.tensor
        def _(pe):
            for j in range(BL):
                last = nc.tensor.transpose(TT[:, j], wts[:, j * tiles:(j + 1) * tiles].rearrange("p t e -> p (t e)"),
                                           res["ident"][:])
            last.then_inc(turned, 1)
            pe.wait_ge(loaded, 32)
            for b in range(BITS + 1):
                pe.wait_ge(counted, b + 1)
                nc.tensor.matmul(CT[:, 0:1], same[:], cnt[:], start=True, stop=True).then_inc(total, 1)
            pe.wait_ge(counted, BITS + 2)
            nc.tensor.matmul(CT[:, 0:BL], before[:], ceq[:], start=True, stop=False)
            nc.tensor.matmul(CT[:, 0:BL], same[:], cbef[:], start=False, stop=True).then_inc(off_mm, 1)
            pe.wait_ge(chosen, 1)
            for j in range(BL):
                last = nc.tensor.transpose(BT[:, j], s[:, j], res["ident"][:])
            last.then_inc(back, 1)

        @block.vector
        def _(v):
            n = [0]

            def then(ins):
                n[0] += 1
                ins.then_inc(seq, 1)
                v.wait_ge(seq, n[0])

            nc.vector.memset(kth[:], 0)
            v.wait_ge(turned, 1)
            then(nc.vector.tensor_copy(s[:], TT[:]))
            for b in range(BITS):
                then(nc.vector.tensor_scalar(cand[:], kth[:], 1 << (BITS - 1 - b), None, ALU.bitwise_or))
                nc.vector.tensor_scalar(junk[:], s[:], cand[:].bitcast(F32), None, ALU.is_ge, ALU.add,
                                        accum_out=cnt[:]).then_inc(counted, 1)
                v.wait_ge(total, b + 1)
                then(nc.vector.tensor_scalar(mask[:], CT[:, 0:1], float(K), None, ALU.is_ge))
                then(nc.vector.copy_predicated(kth[:], mask[:], cand[:]))
            kf = kth[:].bitcast(F32)
            nc.vector.tensor_scalar(junk[:], s[:], kf, None, ALU.is_gt, ALU.add, accum_out=cnt[:]).then_inc(counted, 1)
            v.wait_ge(total, BITS + 1)
            then(nc.vector.tensor_scalar(need[:], CT[:, 0:1], -1.0, float(K), ALU.mult, ALU.add))
            then(nc.vector.tensor_scalar(eq[:], s[:], kf, None, ALU.is_equal))
            for j in range(BL):
                then(nc.vector.tensor_tensor_scan(pre[:, j], res["ones"][:], eq[:, j], 0.0, ALU.mult, ALU.add))
            nc.vector.memset(cbef[:, 0:1], 0.0)
            then(nc.vector.tensor_copy(ceq[:], pre[:, :, P - 1]))
            for j in range(1, BL):
                if j == BL - 1:
                    nc.vector.tensor_tensor(cbef[:, j:j + 1], cbef[:, j - 1:j], ceq[:, j - 1:j], ALU.add)\
                        .then_inc(counted, 1)
                else:
                    then(nc.vector.tensor_tensor(cbef[:, j:j + 1], cbef[:, j - 1:j], ceq[:, j - 1:j], ALU.add))
            v.wait_ge(off_mm, 1)
            then(nc.vector.tensor_scalar(lim[:], CT[:, 0:BL], need[:], -1.0, ALU.subtract, ALU.mult))
            for j in range(BL):
                then(nc.vector.scalar_tensor_tensor(out=pre[:, j], in0=pre[:, j], scalar=lim[:, j:j + 1],
                                                    in1=eq[:, j], op0=ALU.is_le, op1=ALU.mult))
            then(nc.vector.tensor_tensor(pre[:], pre[:], junk[:], ALU.add))
            nc.vector.tensor_tensor(s[:], s[:], pre[:], ALU.mult).then_inc(chosen, 1)
            v.wait_ge(back, 1)
            nc.vector.tensor_copy(wts[:].rearrange("p t e -> p (t e)"), BT[:].rearrange("p j q -> p (j q)"))


def choose_constants():
    r = np.arange(P)
    same = (r[:, None] % 8 == r[None, :] % 8)
    before = same & (r[:, None] < r[None, :])
    return {"same": same.astype(np.float32), "before": before.astype(np.float32)}



def routed_experts(nc, res, name, w):
    x, ident = res["x"], res["ident"]
    E, PAIRS, TOP = 32, 16, 6
    NQ = PAIRS + 1
    norm_factors(nc, res, name + "n")
    with ExitStack() as ctx:
        sc = Scope(nc, ctx, name)
        wg, wu, wd = (sc.sb(n, [P, NQ, P]) for n in ("wg", "wu", "wd"))
        wr, bias, fresh = sc.sb("wr", [P, E]), sc.sb("bias", [P, G, E]), sc.sb("fresh", [P, G, E])
        sel = sc.sb("sel", [3 * E, PAIRS, P], BF16)
        zero = sc.sb("zero", [P, GT], BF16)
        xn = sc.sb("xn", [P, G, D])
        xnT = [sc.sb(f"xnT{i}", [P, GT]) for i in range(2)]
        e, cor, gt, eq, pre = (sc.sb(n, [P, G, E]) for n in ("e", "cor", "gt", "eq", "pre"))
        m8 = sc.sb("m8", [P, G, 8])
        top, tot = sc.sb("top", [P, G]), sc.sb("tot", [P, G])
        comb = sc.sb("comb", [P, G, 3, E])
        cf, cr = sc.sb("cf", [3 * E, GT]), sc.sb("cr", [3 * E, GT])
        c2 = sc.sb("c2", [3 * E, GT], BF16)
        cb = [sc.sb(f"cb{i}", [3 * E, GT], BF16) for i in range(2)]
        sg = [sc.sb(f"sg{i}", [P, GT]) for i in range(2)]
        hm = [sc.sb(f"hm{i}", [P, GT]) for i in range(2)]
        GB = [sc.ps(f"GB{i}", [P, GT]) for i in range(2)]
        UB = [sc.ps(f"UB{i}", [P, GT]) for i in range(2)]
        CB, M0 = sc.ps("CB", [P, GT]), sc.ps("M0", [P, GT])
        OUT = [sc.ps(f"OUT{i}", [P, G, D]) for i in range(2)]
        names = ("loaded weights zeroed xn_ready xn_used xt_ready lg_mm rseq exp_in exped comb_ready ct_mm ct_read cseq c_ready "
                 "g_mm u_mm silu mseq mul_done down_mm added").split()
        s = {n: sc.sem(n) for n in names}
        block = ctx.enter_context(nc.Block())
        loads = [(wr, "wr"), (bias, "bias"), (fresh, "fresh"), (sel, "sel")]
        NR = 16

        @block.sync
        def _(sp):
            for dst, n in loads:
                sp.dma_start(dst[:], w[n]).then_inc(s["loaded"], 16)
            for dst, n in ((wg, "wg"), (wu, "wu"), (wd, "wd")):
                sp.dma_start(dst[:], w[n]).then_inc(s["weights"], 16)

        @block.vector
        def _(v):
            nc.vector.memset(zero[:], 0.0).then_inc(s["zeroed"], 1)
            v.wait_ge(s["loaded"], 16 * len(loads))
            wide = [P, G, E]
            count = [0]

            def then(b, ins):
                count[0] += 1
                ins.then_inc(s["rseq"], 1)
                wait(v, s["rseq"], b * NR + count[0])

            def norm_group(b):
                wait(v, s["xn_used"], b)
                normed(nc, v, res, xn, b, res["rstd"], s["xn_ready"])

            def router_a(b):
                count[0] = 0
                wait(v, s["lg_mm"], b + 1)
                lg = M0[:, 0:G * E].rearrange("p (t e) -> p t e", t=G)
                then(b, nc.vector.tensor_reduce(top[:], lg, AX.X, ALU.max))
                nc.vector.tensor_tensor(e[:], lg, top[:].unsqueeze(2).to_broadcast(wide), ALU.subtract)\
                    .then_inc(s["exp_in"], 1)

            def router_b(b):
                wait(v, s["exped"], b + 1)
                then(b, nc.vector.tensor_reduce(tot[:], e[:], AX.X, ALU.add))
                then(b, nc.vector.reciprocal(top[:], tot[:]))
                then(b, nc.vector.tensor_tensor(e[:], e[:], top[:].unsqueeze(2).to_broadcast(wide), ALU.mult))
                then(b, nc.vector.tensor_tensor(cor[:], e[:], bias[:], ALU.add))
                nc.vector.memset(pre[:, :, 0:1], 0.0)
                for t in range(G):
                    ins = nc.vector.max(m8[:, t], cor[:, t])
                then(b, ins)

            def router_c(b):
                sixth = m8[:, :, TOP - 1:TOP].to_broadcast(wide)
                nc.vector.tensor_tensor(eq[:], cor[:], sixth, ALU.is_equal)
                then(b, nc.vector.tensor_tensor(gt[:], cor[:], sixth, ALU.is_gt))
                then(b, nc.vector.tensor_reduce(tot[:], gt[:], AX.X, ALU.add))
                then(b, nc.vector.tensor_tensor_scan(pre[:].rearrange("p t e -> p (t e)"),
                                                     fresh[:].rearrange("p t e -> p (t e)"),
                                                     eq[:].rearrange("p t e -> p (t e)"), 0.0, ALU.mult, ALU.add))
                then(b, nc.vector.tensor_tensor(pre[:], pre[:], tot[:].unsqueeze(2).to_broadcast(wide), ALU.add))
                then(b, nc.vector.scalar_tensor_tensor(out=pre[:], in0=pre[:], scalar=float(TOP), in1=eq[:],
                                                       op0=ALU.is_le, op1=ALU.mult))
                then(b, nc.vector.tensor_tensor(gt[:], gt[:], pre[:], ALU.add))
                then(b, nc.vector.tensor_tensor(gt[:], gt[:], e[:], ALU.mult))

            def router_d(b):
                then(b, nc.vector.tensor_reduce(tot[:], gt[:], AX.X, ALU.add))
                then(b, nc.vector.tensor_scalar(tot[:], tot[:], 1e-12, None, ALU.max))
                then(b, nc.vector.reciprocal(top[:], tot[:]))
                assert count[0] == NR, count[0]
                wait(v, s["ct_mm"], b)
                for i in range(3):
                    nc.vector.tensor_tensor(comb[:, :, i], gt[:], top[:].unsqueeze(2).to_broadcast(wide),
                                            ALU.mult).then_inc(s["comb_ready"], 1)

            def finish(g, j):
                wait(v, s["down_mm"], g * NQ + NQ)
                xs = x[:, bass.ds(g * G, G), :]
                nc.vector.tensor_tensor(xs, xs, OUT[j][:], ALU.add).then_inc(s["added"], 1)
                wait(v, s["added"], g + 1)
                row_stats(nc, res, g)

            norm_group(0)
            for part in (router_a, router_b, router_c, router_d):
                part(0)

            def step(g, j, q, more, nxt):
                n, k = g * NQ + q, (j + q) % 2
                if more:
                    if q == 0:
                        norm_group(g + 1)
                    if q in (4, 6, 8, 10):
                        (router_a, router_b, router_c, router_d)[q // 2 - 2](g + 1)
                wait(v, s["silu"], n + 1)
                wait(v, s["u_mm"], n + 1)
                wait(v, s["down_mm"], n - 1)
                if q < PAIRS:
                    nc.vector.tensor_tensor(sg[k][:], sg[k][:], UB[k][:], ALU.mult).then_inc(s["mseq"], 1)
                    wait(v, s["mseq"], g * PAIRS + (q + 1))
                    nc.vector.tensor_tensor(hm[k][:], sg[k][:], CB[:], ALU.mult).then_inc(s["mul_done"], 1)
                else:
                    nc.vector.tensor_tensor(hm[k][:], sg[k][:], UB[k][:], ALU.mult).then_inc(s["mul_done"], 1)
                if q == 1 and not (isinstance(g, int) and g == 0):
                    finish(g - 1, 1 - j)

            by_group(v, step, GROUPS, NQ)
            finish(GROUPS - 1, (GROUPS - 1) % 2)

        @block.gpsimd
        def _(pool):
            def split(b, j):
                wait(pool, s["ct_read"], 2 * b + 2)
                wait(pool, s["down_mm"], b * NQ - NQ)
                lo, hi = slice(E, 2 * E), slice(2 * E, 3 * E)
                c1 = cb[j]
                nc.gpsimd.tensor_tensor(cr[hi], cf[hi], c1[hi], ALU.subtract).then_inc(s["cseq"], 1)
                nc.gpsimd.tensor_tensor(c2[hi], cf[hi], c1[hi], ALU.subtract).then_inc(s["cseq"], 1)
                wait(pool, s["cseq"], 2 * b + 2)
                nc.gpsimd.tensor_tensor(c1[hi], cr[hi], c2[hi], ALU.subtract).then_inc(s["c_ready"], 1)
                nc.gpsimd.tensor_tensor(c1[lo], cf[lo], c1[lo], ALU.subtract).then_inc(s["c_ready"], 1)

            split(0, 0)

            def step(g, j, q, more, nxt):
                if q == 12 and more:
                    split(g + 1, 1 - j)

            by_group(pool, step, GROUPS, NQ)

        @block.scalar
        def _(act):
            def evac(b, j):
                wait(act, s["xn_used"], b + 1)
                wait(act, s["u_mm"], b * NQ - NQ)
                nc.scalar.activation(xnT[j][:], M0[:], ACT.Copy).then_inc(s["xt_ready"], 1)

            def exps(b):
                wait(act, s["exp_in"], b + 1)
                nc.scalar.activation(e[:], e[:], ACT.Exp).then_inc(s["exped"], 1)

            def weights(b, j):
                wait(act, s["ct_mm"], b + 1)
                wait(act, s["c_ready"], 2 * b)
                wait(act, s["u_mm"], b * NQ - NQ)
                nc.scalar.activation(cf[:], M0[0:3 * E, :], ACT.Copy).then_inc(s["ct_read"], 1)
                nc.scalar.activation(cb[j][:], M0[0:3 * E, :], ACT.Copy).then_inc(s["ct_read"], 1)

            def silus(g, j, q):
                n, k = g * NQ + q, (j + q) % 2
                wait(act, s["g_mm"], n + 1)
                wait(act, s["mul_done"], n - 1)
                nc.scalar.activation(sg[k][:], GB[k][:], ACT.Silu).then_inc(s["silu"], 1)

            evac(0, 0)
            exps(0)
            weights(0, 0)
            silus(0, 0, 0)

            def step(g, j, q, more, nxt):
                if more:
                    if q == 1:
                        evac(g + 1, 1 - j)
                    if q == 5:
                        exps(g + 1)
                    if q == 11:
                        weights(g + 1, 1 - j)
                if nxt:
                    silus(*nxt)

            by_group(act, step, GROUPS, NQ)

        @block.tensor
        def _(pe):
            pe.wait_ge(s["loaded"], 16 * len(loads))
            pe.wait_ge(s["zeroed"], 1)

            def turn(b):
                wait(pe, s["xn_ready"], b * G + G)
                wait(pe, s["ct_read"], 2 * b)
                for t in range(G):
                    last = nc.tensor.transpose(M0[:, t * P:t * P + P], xn[:, t], ident[:])
                last.then_inc(s["xn_used"], 1)

            def logits(b, j):
                wait(pe, s["xt_ready"], b + 1)
                for t in range(G):
                    last = nc.tensor.matmul(M0[:, t * E:t * E + E], xnT[j][:, t * P:t * P + P], wr[:],
                                            start=True, stop=True)
                last.then_inc(s["lg_mm"], 1)

            def turn_weights(b):
                wait(pe, s["comb_ready"], 3 * b + 3)
                wait(pe, s["xt_ready"], b + 1)
                for t in range(G):
                    last = nc.tensor.transpose(M0[0:3 * E, t * P:t * P + P],
                                               comb[:, t].rearrange("p i e -> p (i e)"), ident[:])
                last.then_inc(s["ct_mm"], 1)

            def up(g, j, q):
                n, k = g * NQ + q, (j + q) % 2
                wait(pe, s["silu"], n - 1)
                nc.tensor.matmul(GB[k][:], wg[:, q], xnT[j][:], start=True, stop=True).then_inc(s["g_mm"], 1)
                wait(pe, s["mul_done"], n - 1)
                last = nc.tensor.matmul(UB[k][:], wu[:, q], xnT[j][:], start=True, stop=True)
                if q < PAIRS:
                    if q == 0:
                        wait(pe, s["c_ready"], 2 * g + 2)
                    wait(pe, s["mul_done"], n)
                    last = nc.tensor.matmul(CB[:], sel[:, q], cb[j][:], start=True, stop=True)
                last.then_inc(s["u_mm"], 1)

            turn(0)
            logits(0, 0)
            turn_weights(0)
            pe.wait_ge(s["weights"], 3 * 16)
            up(0, 0, 0)

            def step(g, j, q, more, nxt):
                n, k = g * NQ + q, (j + q) % 2
                if more:
                    if q == 1:
                        turn(g + 1)
                    if q == 3:
                        logits(g + 1, 1 - j)
                    if q == 11:
                        turn_weights(g + 1)
                if nxt:
                    up(*nxt)
                if q == 0:
                    wait(pe, s["added"], g - 1)
                    nc.tensor.matmul(OUT[j][:].rearrange("p t d -> p (t d)"), zero[:, 0:P], zero[:], start=True, stop=False)
                wait(pe, s["mul_done"], n + 1)
                for t in range(G):
                    last = nc.tensor.matmul(OUT[j][:, t], hm[k][:, t * P:t * P + P], wd[:, q], start=False,
                                            stop=(q == NQ - 1 and t == G - 1))
                last.then_inc(s["down_mm"], 1)

            by_group(pe, step, GROUPS, NQ)


def routed_constants():
    sel = np.zeros((96, 16, P), HOST_BF16)
    for r in range(96):
        q, half = (r % 32) // 2, (r % 32) % 2
        sel[r, q, 64 * half:64 * half + 64] = 1.0
    fresh = np.ones((P, G, 32), np.float32)
    fresh[:, :, 0] = 0.0
    return {"sel": sel, "fresh": fresh}


def state_space(nc, res, name, w):
    x, ident = res["x"], res["ident"]
    NB, N, CH = GT // S, 16, 2
    norm_factors(nc, res, name + "n", then="norm")
    with ExitStack() as ctx:
        sc = Scope(nc, ctx, name)
        win, cw, wk = sc.sb("win", [P, 4, P]), sc.sb("cw", [P, 4, CH * P]), sc.sb("wk", [P, 4, CH * P])
        wdl, wbc, wdt, wout = (sc.sb(n, [P, CH, P]) for n in ("wdl", "wbc", "wdt", "wout"))
        cbias, bdt, dpar = (sc.sb(n, [P, CH]) for n in ("cbias", "bdt", "dpar"))
        lnw, lnb = sc.sb("lnw", [P, 1]), sc.sb("lnb", [P, 1])
        la, A = sc.sb("la", [P, CH, N]), sc.sb("A", [P, CH, N])
        sel = sc.sb("sel", [P, 2 * N, P], BF16)
        PADW = S + 3
        xn = sc.sb("xn", [P, G, D])
        xnp = sc.sb("xnp", [P, NB, PADW])
        u = [sc.sb(f"u{i}", [P, CH, GT]) for i in range(2)]
        sz = [sc.sb(f"sz{i}", [P, CH, GT]) for i in range(2)]
        dtA = [sc.sb(f"dtA{i}", [P, CH, GT]) for i in range(2)]
        dtu = [sc.sb(f"dtu{i}", [P, CH, GT]) for i in range(2)]
        et = sc.sb("et", [P, CH, GT])
        dtl, bf, br = sc.sb("dtl", [P, GT]), sc.sb("bf", [P, GT]), sc.sb("br", [P, GT])
        b2 = sc.sb("b2", [P, GT], BF16)
        bc = [sc.sb(f"bc{i}", [P, GT], BF16) for i in range(2)]
        Q = 4
        dA = [[sc.sb(f"dA{i}{c}", [P, GT]) for c in range(CH)] for i in range(Q)]
        inp = [[sc.sb(f"inp{i}{c}", [P, GT]) for c in range(CH)] for i in range(Q)]
        Bs = [sc.sb(f"Bs{i}", [P, GT]) for i in range(Q)]
        h = [[sc.sb(f"h{i}{c}", [P, GT]) for c in range(CH)] for i in range(2)]
        hc = [[sc.sb(f"hc{i}{c}", [P, GT]) for c in range(CH)] for i in range(Q)]
        yy = sc.sb("yy", [P, CH, GT])
        tmp = sc.sb("tmp", [P, G, D])
        Y = [sc.ps(f"Y{c}", [P, GT]) for c in range(CH)]
        BB = [sc.ps(f"BB{i}", [P, GT]) for i in range(2)]
        CC = [sc.ps(f"CC{i}", [P, GT]) for i in range(2)]
        M = [sc.ps(f"M{i}", [P, GT]) for i in range(2)]
        names = ("loaded set_up seta xn_ready f_mm m_read pseq bc_ready fseq ln_done dt_ready bb_mm b_ev cc_mm "
                 "dA_done mulB scanned mulC y_mm y_read yseq y_ready out_mm oseq").split()
        s = {n: sc.sem(n) for n in names}
        block = ctx.enter_context(nc.Block())
        loads = [(win, "win"), (cw, "cw"), (wdl, "wdl"), (wbc, "wbc"), (wdt, "wdt"), (wout, "wout"), (cbias, "cbias"),
                 (bdt, "bdt"), (dpar, "dpar"), (lnw, "lnw"), (lnb, "lnb"), (la, "la"), (sel, "sel")]
        U = 9
        W2 = CH * N

        @block.sync
        def _(sp):
            for dst, n in loads:
                sp.dma_start(dst[:], w[n]).then_inc(s["loaded"], 16)

        @block.gpsimd
        def _(pool):
            def split(b, j):
                wait(pool, s["m_read"], U * b + 5)
                wait(pool, s["mulB"], 2 * (N * (b - 1) + 11))
                lo, hi = slice(32, 64), slice(64, 96)
                nc.gpsimd.tensor_tensor(br[hi], bf[hi], bc[j][hi], ALU.subtract).then_inc(s["pseq"], 1)
                nc.gpsimd.tensor_tensor(b2[hi], bf[hi], bc[j][hi], ALU.subtract).then_inc(s["pseq"], 1)
                wait(pool, s["pseq"], 2 * b + 2)
                nc.gpsimd.tensor_tensor(bc[j][hi], br[hi], b2[hi], ALU.subtract).then_inc(s["bc_ready"], 1)
                nc.gpsimd.tensor_tensor(bc[j][lo], bf[lo], bc[j][lo], ALU.subtract).then_inc(s["bc_ready"], 1)
                wait(pool, s["bc_ready"], 2 * b + 2)

            def mulB(m, n, k):
                wait(pool, s["b_ev"], m + 1)
                for c in range(CH):
                    wait(pool, s["scanned"], 2 * m + (c + 1 - 2 * Q))
                    nc.gpsimd.tensor_tensor(inp[n % Q][c][:], dtu[k][:, c], Bs[n % Q][:], ALU.mult)\
                        .then_inc(s["mulB"], 1)

            def step(g, k, on):
                for n in range(N):
                    if on(1) and n == 9:
                        split(g + 1, (k + 1) % 2)
                    if n < N - 2 and on(0):
                        mulB(g * N + (n + 2), n + 2, k)
                    if n >= N - 2 and on(1):
                        if n == N - 2:
                            wait(pool, s["dt_ready"], g + 2)
                        mulB(g * N + (n + 2), n + 2 - N, (k + 1) % 2)

            pipeline(pool, step, GROUPS, 1, back=1)

        @block.scalar
        def _(act):
            act.wait_ge(s["loaded"], 16 * len(loads))
            nc.scalar.activation(A[:], la[:], ACT.Exp).then_inc(s["seta"], 1)
            act.wait_ge(s["set_up"], 3)

            def front(g, k, n):
                b, j = g + 1, (k + 1) % 2
                if n == 1:
                    wait(act, s["f_mm"], U * b + 1)
                    nc.scalar.activation(xnp[:, :, 3:PADW], M[0][:].rearrange("p (b s) -> p b s", b=NB), ACT.Identity,
                                         bias=lnb[:], scale=lnw[:]).then_inc(s["m_read"], 1)
                if n == 6:
                    wait(act, s["y_ready"], g)
                    for c in range(CH):
                        wait(act, s["f_mm"], U * b + 2 + c)
                        nc.scalar.activation(u[j][:, c], M[(1 + c) % 2][:], ACT.Silu, bias=cbias[:, c:c + 1])\
                            .then_inc(s["m_read"], 1)
                if n == 7:
                    wait(act, s["f_mm"], U * b + 4)
                    nc.scalar.activation(dtl[:], M[1][:], ACT.Copy).then_inc(s["m_read"], 1)
                if n == 8:
                    wait(act, s["f_mm"], U * b + 5)
                    wait(act, s["bc_ready"], 2 * b)
                    nc.scalar.activation(bf[:], M[0][:], ACT.Copy)
                    nc.scalar.activation(bc[j][:], M[0][:], ACT.Copy).then_inc(s["m_read"], 1)
                if n in (9, 10):
                    c = n - 9
                    wait(act, s["f_mm"], U * b + 6 + c)
                    wait(act, s["dt_ready"], b)
                    nc.scalar.activation(et[:, c], M[(1 + c) % 2][:], ACT.Exp, bias=bdt[:, c:c + 1])\
                        .then_inc(s["m_read"], 1)
                if n == 13:
                    for c in range(CH):
                        wait(act, s["f_mm"], U * b + 8 + c)
                        nc.scalar.activation(sz[j][:, c], M[(1 + c) % 2][:], ACT.Silu).then_inc(s["m_read"], 1)
                if n == 12:
                    wait(act, s["fseq"], 4 * b + 1)
                    nc.scalar.activation(et[:], et[:], ACT.Ln, bias=1.0).then_inc(s["ln_done"], 1)

            def step(g, k, on):
                for n in range(N):
                    if on(0) if n < N - 2 else on(1):
                        m = g * N + (n + 2)
                        wait(act, s["bb_mm"], m + 1)
                        wait(act, s["mulB"], 2 * (m + 1 - Q))
                        nc.scalar.activation(Bs[(n + 2) % Q][:], BB[n % 2][:], ACT.Copy).then_inc(s["b_ev"], 1)
                    if on(0) if n < N - 1 else on(1):
                        kk, nn = (k, n + 1) if n < N - 1 else ((k + 1) % 2, 0)
                        if nn == 0:
                            wait(act, s["dt_ready"], g + 2)
                        for c in range(CH):
                            wait(act, s["scanned"], g * W2 + (2 * (n + 1 - Q) + c + 1))
                            nc.scalar.activation(dA[nn % Q][c][:], dtA[kk][:, c], ACT.Exp, scale=A[:, c, nn:nn + 1])\
                                .then_inc(s["dA_done"], 1)
                    if on(1):
                        front(g, k, n)

            pipeline(act, step, GROUPS, 1, back=1)

        @block.vector
        def _(v):
            nc.vector.memset(xnp[:], 0.0).then_inc(s["set_up"], 1)
            v.wait_ge(s["loaded"], 16 * len(loads))
            for c in range(CH):
                for t in range(4):
                    last = nc.vector.tensor_tensor(wk[:, t, c * P:c * P + P], win[:, c], cw[:, t, c * P:c * P + P], ALU.mult)
            last.then_inc(s["set_up"], 1)
            v.wait_ge(s["seta"], 1)
            nc.vector.tensor_scalar(A[:], A[:], -1.0, None, ALU.mult).then_inc(s["set_up"], 1)

            def front(g, k, n):
                b, j = g + 1, (k + 1) % 2
                if n == 0:
                    wait(v, s["f_mm"], U * (b - 1) + 1)
                    normed(nc, v, res, xn, b, res["rstd2"], s["xn_ready"])
                if n == 11:
                    wait(v, s["m_read"], U * b + 7)
                    nc.vector.tensor_scalar(et[:], et[:], 1.0, None, ALU.min).then_inc(s["fseq"], 1)
                if n == 13:
                    wait(v, s["ln_done"], b + 1)
                    nc.vector.tensor_scalar(et[:], et[:], 0.001, 0.001, ALU.add, ALU.max).then_inc(s["fseq"], 1)
                    wait(v, s["fseq"], 4 * b + 2)
                    nc.vector.scalar_tensor_tensor(out=dtu[j][:], in0=et[:], scalar=0.1, in1=u[j][:],
                                                   op0=ALU.min, op1=ALU.mult).then_inc(s["fseq"], 1)
                    nc.vector.tensor_scalar(dtA[j][:], et[:], 0.1, None, ALU.min).then_inc(s["fseq"], 1)
                    wait(v, s["fseq"], 4 * b + 4)
                    nc.vector.memset(dtA[j][:].rearrange("p c (b s) -> p (c b) s", b=NB)[:, :, 0:1], 1e25)\
                        .then_inc(s["dt_ready"], 1)

            def finish(g, k, n):
                xs = x[:, bass.ds(g * G, G), :]
                if n == 0:
                    wait(v, s["y_mm"], g * W2 + W2)
                    wait(v, s["out_mm"], g)
                    for c in range(CH):
                        nc.vector.scalar_tensor_tensor(out=yy[:, c], in0=u[k][:, c], scalar=dpar[:, c:c + 1],
                                                       in1=Y[c][:], op0=ALU.mult, op1=ALU.add).then_inc(s["y_read"], 1)
                if n == 1:
                    wait(v, s["y_read"], g * CH + CH)
                    nc.vector.tensor_tensor(yy[:], yy[:], sz[k][:], ALU.mult).then_inc(s["y_ready"], 1)
                if n == 3:
                    for t in range(G):
                        nc.vector.tensor_scalar(tmp[:, t], x[:, g * G + t], res["mean"][:, bass.ds(g * G + t, 1)],
                                                res["rstd"][:, bass.ds(g * G + t, 1)], ALU.subtract, ALU.mult)\
                            .then_inc(s["oseq"], 1)
                if n == 4:
                    wait(v, s["oseq"], g * 6 + 4)
                    nc.vector.tensor_tensor(xs, xs, tmp[:], ALU.add).then_inc(s["oseq"], 1)
                if n == 15:
                    wait(v, s["out_mm"], g + 1)
                    wait(v, s["oseq"], g * 6 + 5)
                    nc.vector.tensor_tensor(xs, xs, M[1][:].rearrange("p (t d) -> p t d", t=G), ALU.add)\
                        .then_inc(s["oseq"], 1)
                    wait(v, s["oseq"], g * 6 + 6)
                    row_stats(nc, res, g)

            def step(g, k, on):
                if on(0):
                    wait(v, s["dt_ready"], g + 1)
                for n in range(N):
                    m = g * W2 + 2 * n
                    if on(0):
                        for c in range(CH):
                            wait(v, s["mulB"], m + (c + 1))
                            wait(v, s["dA_done"], m + (c + 1))
                            wait(v, s["mulC"], m + (c - 3))
                            nc.vector.tensor_tensor_scan(h[n % 2][c][:], dA[n % Q][c][:], inp[n % Q][c][:], 0.0,
                                                         ALU.mult, ALU.add).then_inc(s["scanned"], 1)
                    if on(-1):
                        finish(g - 1, (k + 1) % 2, n)
                    if on(0):
                        wait(v, s["cc_mm"], g * N + (n + 1))
                        for c in range(CH):
                            wait(v, s["scanned"], m + (c + 1))
                            wait(v, s["y_mm"], m + (c + 1 - 2 * Q))
                            nc.vector.tensor_tensor(hc[n % Q][c][:], h[n % 2][c][:], CC[n % 2][:], ALU.mult)\
                                .then_inc(s["mulC"], 1)
                    if on(1):
                        front(g, k, n)

            pipeline(v, step, GROUPS, 1, back=1)

        @block.tensor
        def _(pe):
            pe.wait_ge(s["set_up"], 2)

            def claim(b, i):
                if i == 1:
                    wait(pe, s["oseq"], 6 * (b - 2))
                wait(pe, s["m_read"], U * b + max(i - 1, 0))

            def front(g, k, n):
                b, j = g + 1, (k + 1) % 2
                if n == 1:
                    wait(pe, s["xn_ready"], G * (b + 1))
                    claim(b, 0)
                    for t in range(G):
                        last = nc.tensor.transpose(M[0][:, t * P:t * P + P], xn[:, t], ident[:])
                    last.then_inc(s["f_mm"], 1)
                if n in (2, 3, 4, 5):
                    c, half = divmod(n - 2, 2)
                    if not half:
                        claim(b, 1 + c)
                        wait(pe, s["m_read"], U * b + 1)
                    out = M[(1 + c) % 2][:].rearrange("p (b s) -> p b s", b=NB)
                    for t in (2 * half, 2 * half + 1):
                        last = nc.tensor.matmul(out, wk[:, t, c * P:c * P + P], xnp[:, :, t:t + S],
                                                start=(t == 0), stop=(t == 3))
                    if half:
                        last.then_inc(s["f_mm"], 1)
                if n in (7, 8):
                    i, wt = ((3, wdl), (4, wbc))[n - 7]
                    wait(pe, s["m_read"], U * b + 3)
                    claim(b, i)
                    for c in range(CH):
                        last = nc.tensor.matmul(M[i % 2][:], wt[:, c], u[j][:, c], start=(c == 0), stop=(c == CH - 1))
                    last.then_inc(s["f_mm"], 1)
                if n in (9, 10):
                    c = n - 9
                    claim(b, 5 + c)
                    nc.tensor.matmul(M[(5 + c) % 2][:], wdt[:, c], dtl[:], start=True, stop=True).then_inc(s["f_mm"], 1)
                if n in (11, 12):
                    c = n - 11
                    claim(b, 7 + c)
                    out = M[(7 + c) % 2][:].rearrange("p (b s) -> p b s", b=NB)
                    nc.tensor.matmul(out, win[:, CH + c], xnp[:, :, 3:PADW], start=True, stop=True)\
                        .then_inc(s["f_mm"], 1)

            def spread_B(m, n, k):
                wait(pe, s["b_ev"], m - 1)
                nc.tensor.matmul(BB[n % 2][:], sel[:, n], bc[k][:], start=True, stop=True).then_inc(s["bb_mm"], 1)

            def spread_C(m, n, k):
                wait(pe, s["mulC"], 2 * (m - 1))
                nc.tensor.matmul(CC[n % 2][:], sel[:, N + n], bc[k][:], start=True, stop=True).then_inc(s["cc_mm"], 1)

            def step(g, k, on):
                for n in range(N):
                    if on(0) and n < N - 3:
                        spread_B(g * N + (n + 3), n + 3, k)
                    if on(1) and n >= N - 3:
                        if n == N - 3:
                            wait(pe, s["bc_ready"], 2 * g + 4)
                        spread_B(g * N + (n + 3), n + 3 - N, (k + 1) % 2)
                    if on(0) and n < N - 1:
                        spread_C(g * N + (n + 1), n + 1, k)
                    if on(1) and n == N - 1:
                        spread_C(g * N + N, 0, (k + 1) % 2)
                    if on(1):
                        front(g, k, n)
                    if on(-1) and n == 14:
                        wait(pe, s["y_ready"], g)
                        if on(1):
                            wait(pe, s["m_read"], U * (g + 1) + 8)
                        for t in range(G):
                            for c in range(CH):
                                last = nc.tensor.matmul(M[1][:, t * P:t * P + P], yy[:, c, t * P:t * P + P],
                                                        wout[:, c], start=(c == 0), stop=(c == CH - 1))
                        last.then_inc(s["out_mm"], 1)
                    if on(0):
                        if n == 0:
                            wait(pe, s["y_read"], CH * g)
                        for c in range(CH):
                            wait(pe, s["mulC"], g * W2 + (2 * n + c + 1))
                            nc.tensor.matmul(Y[c][:], ident[:], hc[n % Q][c][:], start=(n == 0), stop=(n == N - 1))\
                                .then_inc(s["y_mm"], 1)

            pipeline(pe, step, GROUPS, 1, back=1)


def state_constants():
    sel = np.zeros((P, 32, P), HOST_BF16)
    for r in range(96):
        sel[r, r % 32] = 1.0
    return {"bsel": sel}


def load_x(nc, res, x_in):
    x, stats = res["x"], res["stats"]
    rows = x_in.rearrange("b (t p) d -> p (b t) d", p=P)
    step = 8
    with ExitStack() as ctx:
        sc = Scope(nc, ctx, "load")
        loaded = [sc.sem(f"loaded{i}") for i in range(TILES // step)]
        c = sc.sem("c")
        block = ctx.enter_context(nc.Block())

        @block.sync
        def _(sp):
            for i in range(TILES // step):
                sp.dma_start(x[:, i * step:(i + 1) * step], rows[:, i * step:(i + 1) * step]).then_inc(loaded[i], 16)

        @block.scalar
        def _(act):
            act.dma_start(res["ident"][:], res["ident_in"]).then_inc(c, 16)
            act.dma_start(res["identb"][:], res["identb_in"]).then_inc(c, 16)
            act.wait_ge(c, 32)

        @block.vector
        def _(v):
            nc.vector.memset(res["ones"][:], 1.0)
            for i in range(TILES // step):
                v.wait_ge(loaded[i], 16)
                for t in range(i * step, (i + 1) * step):
                    nc.vector.bn_stats(stats[:, t, :], x[:, t, :])


def program(nc, a, out):
    with ExitStack() as ctx:
        sc = Scope(nc, ctx, "g")
        res = {"x": sc.sb("x", [P, TILES, D]), "stats": sc.sb("stats", [P, TILES, 6]),
               "mean": sc.sb("mean", [P, TILES]), "rstd": sc.sb("rstd", [P, TILES]), "rstd2": sc.sb("rstd2", [P, TILES]),
               "ident": sc.sb("ident", [P, P]), "identb": sc.sb("identb", [P, P], BF16),
               "ones": sc.sb("ones", [P, P]),
               "ident_in": a["c_ident"], "identb_in": a["c_identb"], "out": out}
        load_x(nc, res, a["x"])
        for stage in STAGES:
            stage(nc, res, a)


def l0_attn(nc, res, a):
    norm_factors(nc, res, "n0")
    attention(nc, res, "a0", {"wqkv": a["L0_qkv"], "bqk": a["L0_bqk"], "bv": a["L0_bv"], "rel": a["L0_attn_rel_bias"],
                              "hot": a["c_hot"], "flip": a["c_flip"], "krows": a["c_krows"]}, False)


def l1_attn(nc, res, a):
    norm_factors(nc, res, "n2")
    attention(nc, res, "a2", {"wqkv": a["L1_qkv"], "bqk": a["L1_bqk"], "bv": a["L1_bv"], "krows": a["c_krows"],
                              "maskq": a["c_maskq"], "maskk": a["c_maskk"], "wproj": a["L1_attn_w_proj"],
                              "bproj": a["L1_bproj"]}, True)


def l0_ffn(nc, res, a):
    ternary_ffn(nc, res, "f1", {"up": a["L0_up"], "down": a["L0_down"]})


def l3_ffn(nc, res, a):
    lowrank_ffn(nc, res, "f7", {n: a["L3_" + n] for n in ("u1", "v1", "u2", "v2", "b1", "b2")}, res["out"])


def l1_ffn(nc, res, a):
    expert_choice(nc, res, "f3", {"wr": a["L1_ffn_Wr"], "w1": a["L1_w1"], "b1": a["L1_b1"], "w2": a["L1_w2"],
                                  "b2": a["L1_b2"], "same": a["c_same"], "before": a["c_before"]})


def l3_attn(nc, res, a):
    min_gru(nc, res, "a6", {"wz": a["L3_attn_Wz"], "wh": a["L3_attn_Wh"], "bz": a["L3_bz"], "bh": a["L3_bh"],
                            "swish": a["L3_swish"], "gamma": a["L3_gamma"], "beta": a["L3_beta"]})


def l2_attn(nc, res, a):
    w = {n: a["L2_" + n] for n in "win cw wdl wbc wdt wout cbias bdt dpar lnw lnb la".split()}
    state_space(nc, res, "a4", {**w, "sel": a["c_bsel"]})


def l2_ffn(nc, res, a):
    w = {n: a["L2f_" + n] for n in "wr bias wg wu wd".split()}
    routed_experts(nc, res, "f5", {**w, "sel": a["c_sel"], "fresh": a["c_fresh"]})


STAGES = [l0_attn, l0_ffn, l1_attn, l1_ffn, l2_attn, l2_ffn, l3_attn, l3_ffn]


def padded(a, rows, cols):
    out = np.zeros((rows, cols), a.dtype)
    out[:a.shape[0], :a.shape[1]] = a
    return out


def layout(i):
    def dh(w):
        return w.reshape(w.shape[0], H, DH).transpose(0, 2, 1).reshape(w.shape[0], D)

    def rows(v, n=P):
        return np.broadcast_to(v.reshape(1, -1), (n, v.size))

    o = {"x": i["L0_attn_hidden_states"]}
    wa, ba = i["L1_attn_w_attn"], i["L1_attn_b_attn"].reshape(1, -1)
    for n, (wq, wk, wv, bq, bk, bvv) in {
            "L0": (i["L0_attn_Wq"], i["L0_attn_Wk"], i["L0_attn_Wv"], i["L0_attn_bq"].reshape(1, -1),
                   i["L0_attn_bk"].reshape(1, -1), i["L0_attn_bv"]),
            "L1": (wa[:, 0:D], wa[:, D:2 * D], wa[:, 2 * D:], ba[:, 0:D], ba[:, D:2 * D], ba[0, 2 * D:])}.items():
        o[f"{n}_qkv"] = np.stack([dh(wq), dh(wk), wv], 1)
        o[f"{n}_bqk"] = np.concatenate([dh(bq), dh(bk)], 0).T
        o[f"{n}_bv"] = rows(bvv)
    o["L0_attn_rel_bias"] = i["L0_attn_rel_bias"]
    o["L1_attn_w_proj"] = i["L1_attn_w_proj"]
    o["L1_bproj"] = i["L1_attn_b_proj"].reshape(1, -1)
    o["L0_up"] = i["L0_ffn_w_up"].T.reshape(D, 4, P)
    o["L0_down"] = i["L0_ffn_w_down"].T.reshape(4, P, D).transpose(1, 0, 2)
    o["L3_u1"] = padded(i["L3_ffn_U1"], P, P)
    o["L3_v1"] = padded(i["L3_ffn_V1"], P, 4 * P)
    o["L3_u2"] = padded(i["L3_ffn_U2"], 4 * P, P).reshape(4, P, P).transpose(1, 0, 2)
    o["L3_v2"] = padded(i["L3_ffn_V2"], P, P)
    o["L3_b1"] = i["L3_ffn_b1"].reshape(4, P).T
    o["L3_b2"] = i["L3_ffn_b2"].reshape(1, P)
    o["L1_ffn_Wr"] = i["L1_ffn_Wr"]
    o["L1_w1"] = i["L1_ffn_W1"].transpose(1, 0, 2)
    o["L1_b1"] = i["L1_ffn_b1"].reshape(8, 4, P).transpose(2, 0, 1)
    o["L1_w2"] = i["L1_ffn_W2"].reshape(8, 4, P, D).transpose(2, 0, 1, 3)
    o["L1_b2"] = i["L1_ffn_b2"].reshape(1, 8, D)
    for n in ("Wz", "Wh"):
        o["L3_attn_" + n] = i["L3_attn_" + n]
    o["L3_bz"], o["L3_bh"] = i["L3_attn_bz"].reshape(P, 1), i["L3_attn_bh"].reshape(P, 1)
    o["L3_swish"] = np.broadcast_to(i["L3_attn_swish_beta"].reshape(1, 1), (P, 1))
    for n in ("gamma", "beta"):
        o["L3_" + n] = np.broadcast_to(i["L3_attn_ln_" + n].reshape(1, 1, D), (P, G, D))
    def halves(v):
        return v.reshape(2, P).T

    o["L2_win"] = i["L2_attn_W_in"].T.reshape(D, 4, P)
    o["L2_cw"] = np.broadcast_to(i["L2_attn_conv_w"][:, 0, :].T.reshape(1, 4, 2 * P), (P, 4, 2 * P))
    wx = i["L2_attn_W_x"].T.reshape(2, P, 96).transpose(1, 0, 2)
    low, bcs = np.zeros((P, 2, P), wx.dtype), np.zeros((P, 2, P), wx.dtype)
    low[:, :, 0:64] = wx[:, :, 0:64]
    for r in range(3):
        bcs[:, :, 32 * r:32 * r + 32] = wx[:, :, 64:96]
    o["L2_wdl"], o["L2_wbc"] = low, bcs
    o["L2_wdt"] = padded(i["L2_attn_W_dt"].T, P, 2 * P).reshape(P, 2, P)
    o["L2_wout"] = i["L2_attn_W_out"].T.reshape(2, P, D).transpose(1, 0, 2)
    o["L2_cbias"], o["L2_bdt"], o["L2_dpar"] = (halves(i["L2_attn_" + n]) for n in ("conv_b", "b_dt", "D_param"))
    o["L2_lnw"], o["L2_lnb"] = i["L2_attn_ln_w"].reshape(P, 1), i["L2_attn_ln_b"].reshape(P, 1)
    o["L2_la"] = i["L2_attn_log_A"].reshape(2, P, 16).transpose(1, 0, 2)
    gu = i["L2_ffn_gate_up_proj"].reshape(16, 2, 2, 64, D)
    for n, part, shared in (("wg", 0, "gate"), ("wu", 1, "up")):
        pairs = gu[:, :, part].transpose(3, 0, 1, 2).reshape(D, 16, P)
        o["L2f_" + n] = np.concatenate([pairs, i[f"L2_ffn_shared_{shared}_w"].T.reshape(D, 1, P)], 1)
    down = i["L2_ffn_down_proj"].reshape(16, 2, D, 64).transpose(1, 3, 0, 2).reshape(P, 16, D)
    o["L2f_wd"] = np.concatenate([down, i["L2_ffn_shared_down_w"].T.reshape(P, 1, D)], 1)
    o["L2f_wr"] = i["L2_ffn_router_weight"].T
    o["L2f_bias"] = np.broadcast_to(i["L2_ffn_e_score_bias"].reshape(1, 1, 32), (P, G, 32))
    for n, c in {**attention_constants(), **choose_constants(), **routed_constants(), **state_constants()}.items():
        o["c_" + n] = c
    return {k: np.ascontiguousarray(v) for k, v in o.items()}


def kernel(**inputs):
    import concourse.bacc as _bacc
    from concourse.bass_utils import run_bass_kernel_spmd as _run

    nc = _bacc.Bacc("TRN2", target_bir_lowering=False, num_devices=1)
    arrays = layout({name: np.asarray(value) for name, value in inputs.items()})
    args = {name: nc.dram_tensor(name, v.shape, mybir.dt.from_np(v.dtype), kind="ExternalInput").ap()
            for name, v in arrays.items()}
    out = nc.dram_tensor("out", (B, S, D), F32, kind="ExternalOutput").ap()
    program(nc, args, out)
    r = _run(nc, [arrays], core_ids=[0])
    return r.results[0]["out"]
```
